# Optimizing a Trainium2 kernel written in Bass

```python
import numpy as np
import jax
import jax.numpy as jnp

def _softmax(x, axis=-1):
    return jax.nn.softmax(x, axis=axis)

def _gelu(x):
    return jax.nn.gelu(x, approximate=True)

def _silu(x):
    return jax.nn.silu(x)

def _sigmoid(x):
    return jax.nn.sigmoid(x)

def _layernorm(x, axis=-1, eps=1e-05):
    m = jnp.mean(x, axis=axis, keepdims=True)
    v = jnp.var(x, axis=axis, keepdims=True)
    return (x - m) / jnp.sqrt(v + eps)

def _scatter_add(tgt, idx, src, axis=0):
    return tgt.at[idx].add(src)

def _segment_sum(src, seg, n):
    return jax.ops.segment_sum(src, seg, n)
kernel_name = 'mk_sandwich_d2_jaxref_r8_9762a3'

def setup_inputs(seed: int=0):
    np.random.seed(seed)
    _w = jnp.asarray

    def _L0_attn_setup():
        import jax, jax.numpy as jnp
        import numpy as np
        EMBED_DIM = 128
        NUM_HEADS = 16
        HEAD_DIM = EMBED_DIM // NUM_HEADS
        LORA_R = 128
        LORA_SCALING = 1.0 / LORA_R
        key = jax.random.key(seed)
        k1, k2, k3, k4 = jax.random.split(key, 4)
        B, S, E = (2, 256, EMBED_DIM)
        x = jax.random.normal(k1, (B, S, E), dtype=jnp.float32)
        W_in = jax.random.normal(k2, (3 * E, 3 * E), dtype=jnp.float32) * (1.0 / np.sqrt(3 * E))
        A_in = jax.random.normal(k3, (LORA_R, 3 * E), dtype=jnp.float32) * (1.0 / np.sqrt(3 * E))
        B_in = jnp.zeros((3 * E, LORA_R), dtype=jnp.float32)
        W_out = jax.random.normal(k4, (E, E), dtype=jnp.float32) * (1.0 / np.sqrt(E))
        return {'x': x, 'W_in': W_in, 'A_in': A_in, 'B_in': B_in, 'W_out': W_out}
    _L0_attn_in = _L0_attn_setup()

    def _L0_ffn_setup():
        import jax, jax.numpy as jnp
        import numpy as np
        DIM = 128

        def _reference_tuple_inner(x, W_r, W_k, W_v, mu_r, mu_k):
            B, T, C = x.shape
            x_prev = jnp.concatenate([jnp.zeros((B, 1, C), x.dtype), x[:, :-1, :]], axis=1)
            xr = mu_r * x + (1.0 - mu_r) * x_prev
            xk = mu_k * x + (1.0 - mu_k) * x_prev
            r = jax.nn.sigmoid(jnp.einsum('btc,dc->btd', xr, W_r))
            k = jnp.einsum('btc,dc->btd', xk, W_k)
            k_act = jnp.square(jax.nn.relu(k))
            out = r * jnp.einsum('btc,dc->btd', k_act, W_v)
            new_state = x[:, -1, :]
            return (out, new_state)
        key = jax.random.key(seed)
        ks = jax.random.split(key, 6)
        B, T, C = (8, 256, DIM)
        x = jax.random.normal(ks[0], (B, T, C), dtype=jnp.float32)
        s = 1.0 / np.sqrt(C)
        W_r = jax.random.uniform(ks[1], (C, C), jnp.float32, -s, s)
        W_k = jax.random.uniform(ks[2], (C, C), jnp.float32, -s, s)
        W_v = jax.random.uniform(ks[3], (C, C), jnp.float32, -s, s)
        mu_r = jax.random.uniform(ks[4], (C,), jnp.float32)
        mu_k = jax.random.uniform(ks[5], (C,), jnp.float32)
        return {'x': x, 'W_r': W_r, 'W_k': W_k, 'W_v': W_v, 'mu_r': mu_r, 'mu_k': mu_k}
    _L0_ffn_in = _L0_ffn_setup()

    def _L1_attn_setup():
        import jax, jax.numpy as jnp
        import numpy as np
        B, N, D = (2, 256, 128)
        H, DH = (16, 64)
        SOFTCLAMP = 50.0
        SCALE = DH ** (-0.5)
        key = jax.random.key(seed)
        ks = jax.random.split(key, 5)
        std = D ** (-0.5)
        return {'x': jax.random.normal(ks[0], (B, N, D), dtype=jnp.float32), 'Wq': jax.random.normal(ks[1], (H * DH, D), dtype=jnp.float32) * std, 'Wk': jax.random.normal(ks[2], (H * DH, D), dtype=jnp.float32) * std, 'Wv': jax.random.normal(ks[3], (H * DH, D), dtype=jnp.float32) * std, 'Wo': jax.random.normal(ks[4], (D, H * DH), dtype=jnp.float32) * std}
    _L1_attn_in = _L1_attn_setup()

    def _L1_ffn_setup():
        import jax, jax.numpy as jnp
        import numpy as np
        TOP_K = 2

        def _mlp(x, w_fc, w_proj):
            return jnp.square(jax.nn.relu(x @ w_fc.T)) @ w_proj.T
        key = jax.random.key(seed)
        ks = jax.random.split(key, 6)
        B, S, D, E = (4, 256, 128, 8)
        d_ff = 4 * D
        x = jax.random.normal(ks[0], (B, S, D), dtype=jnp.float32)
        router_w = jax.random.normal(ks[1], (E, D), dtype=jnp.float32) * 0.02
        w_fc = jax.random.normal(ks[2], (E, d_ff, D), dtype=jnp.float32) * 0.02
        w_proj = jax.random.normal(ks[3], (E, D, d_ff), dtype=jnp.float32) * 0.02
        shared_fc = jax.random.normal(ks[4], (d_ff, D), dtype=jnp.float32) * 0.02
        shared_proj = jax.random.normal(ks[5], (D, d_ff), dtype=jnp.float32) * 0.02
        return {'x': x, 'router_w': router_w, 'w_fc': w_fc, 'w_proj': w_proj, 'shared_fc': shared_fc, 'shared_proj': shared_proj}
    _L1_ffn_in = _L1_ffn_setup()
    _d = {'L0_attn_x': _L0_attn_in['x'], 'L0_attn_W_in': _L0_attn_in['W_in'], 'L0_attn_A_in': _L0_attn_in['A_in'], 'L0_attn_B_in': _L0_attn_in['B_in'], 'L0_attn_W_out': _L0_attn_in['W_out'], 'L0_ffn_W_r': _L0_ffn_in['W_r'], 'L0_ffn_W_k': _L0_ffn_in['W_k'], 'L0_ffn_W_v': _L0_ffn_in['W_v'], 'L0_ffn_mu_r': _L0_ffn_in['mu_r'], 'L0_ffn_mu_k': _L0_ffn_in['mu_k'], 'L1_attn_Wq': _L1_attn_in['Wq'], 'L1_attn_Wk': _L1_attn_in['Wk'], 'L1_attn_Wv': _L1_attn_in['Wv'], 'L1_attn_Wo': _L1_attn_in['Wo'], 'L1_ffn_router_w': _L1_ffn_in['router_w'], 'L1_ffn_w_fc': _L1_ffn_in['w_fc'], 'L1_ffn_w_proj': _L1_ffn_in['w_proj'], 'L1_ffn_shared_fc': _L1_ffn_in['shared_fc'], 'L1_ffn_shared_proj': _L1_ffn_in['shared_proj']}
    _x0 = _d['L0_attn_x']
    _d['L0_attn_x'] = jax.random.normal(jax.random.fold_in(jax.random.key(seed), 1), (32, 256, 128), dtype=_x0.dtype)
    del _x0
    return _d

def reference(L0_attn_x, L0_attn_W_in, L0_attn_A_in, L0_attn_B_in, L0_attn_W_out, L0_ffn_W_r, L0_ffn_W_k, L0_ffn_W_v, L0_ffn_mu_r, L0_ffn_mu_k, L1_attn_Wq, L1_attn_Wk, L1_attn_Wv, L1_attn_Wo, L1_ffn_router_w, L1_ffn_w_fc, L1_ffn_w_proj, L1_ffn_shared_fc, L1_ffn_shared_proj):

    def _L0_attn_ref(x, W_in, A_in, B_in, W_out):
        import jax, jax.numpy as jnp
        import numpy as np
        EMBED_DIM = 128
        NUM_HEADS = 16
        HEAD_DIM = EMBED_DIM // NUM_HEADS
        LORA_R = 128
        LORA_SCALING = 1.0 / LORA_R
        B, S, E = x.shape
        H, D = (NUM_HEADS, HEAD_DIM)
        x3 = jnp.concatenate([x, x, x], axis=-1)
        qkv = x3 @ W_in.T + x3 @ A_in.T @ B_in.T * LORA_SCALING
        Q, K, V = jnp.split(qkv, 3, axis=-1)
        Q = Q.reshape(B, S, H, D).transpose(0, 2, 1, 3)
        K = K.reshape(B, S, H, D).transpose(0, 2, 1, 3)
        V = V.reshape(B, S, H, D).transpose(0, 2, 1, 3)
        scores = jnp.einsum('bhqd,bhkd->bhqk', Q, K) / jnp.sqrt(jnp.float32(D))
        attn = jax.nn.softmax(scores, axis=-1)
        out = jnp.einsum('bhqk,bhkd->bhqd', attn, V)
        out = out.transpose(0, 2, 1, 3).reshape(B, S, E)
        return out @ W_out.T

    def _L0_ffn_ref(x, W_r, W_k, W_v, mu_r, mu_k):
        import jax, jax.numpy as jnp
        import numpy as np
        DIM = 128

        def _reference_tuple_inner(x, W_r, W_k, W_v, mu_r, mu_k):
            B, T, C = x.shape
            x_prev = jnp.concatenate([jnp.zeros((B, 1, C), x.dtype), x[:, :-1, :]], axis=1)
            xr = mu_r * x + (1.0 - mu_r) * x_prev
            xk = mu_k * x + (1.0 - mu_k) * x_prev
            r = jax.nn.sigmoid(jnp.einsum('btc,dc->btd', xr, W_r))
            k = jnp.einsum('btc,dc->btd', xk, W_k)
            k_act = jnp.square(jax.nn.relu(k))
            out = r * jnp.einsum('btc,dc->btd', k_act, W_v)
            new_state = x[:, -1, :]
            return (out, new_state)
        return _reference_tuple_inner(x, W_r, W_k, W_v, mu_r, mu_k)[0]

    def _L1_attn_ref(x, Wq, Wk, Wv, Wo):
        import jax, jax.numpy as jnp
        import numpy as np
        B, N, D = (2, 256, 128)
        H, DH = (16, 64)
        SOFTCLAMP = 50.0
        SCALE = DH ** (-0.5)
        b, n, _ = x.shape
        q = jnp.einsum('bnd,fd->bnf', x, Wq).reshape(b, n, H, DH).transpose(0, 2, 1, 3)
        k = jnp.einsum('bnd,fd->bnf', x, Wk).reshape(b, n, H, DH).transpose(0, 2, 1, 3)
        v = jnp.einsum('bnd,fd->bnf', x, Wv).reshape(b, n, H, DH).transpose(0, 2, 1, 3)
        sim = jnp.einsum('bhid,bhjd->bhij', q, k) * SCALE
        sim = SOFTCLAMP * jnp.tanh(sim / SOFTCLAMP)
        causal = jnp.tril(jnp.ones((n, n), dtype=bool))
        sim = jnp.where(causal, sim, jnp.finfo(sim.dtype).min)
        attn = jax.nn.softmax(sim, axis=-1)
        out = jnp.einsum('bhij,bhjd->bhid', attn, v)
        out = out.transpose(0, 2, 1, 3).reshape(b, n, H * DH)
        return jnp.einsum('bnf,df->bnd', out, Wo)

    def _L1_ffn_ref(x, router_w, w_fc, w_proj, shared_fc, shared_proj):
        import jax, jax.numpy as jnp
        import numpy as np
        TOP_K = 2

        def _mlp(x, w_fc, w_proj):
            return jnp.square(jax.nn.relu(x @ w_fc.T)) @ w_proj.T
        B, S, D = x.shape
        E = router_w.shape[0]
        T = B * S
        flat = x.reshape(T, D)
        logits = flat @ router_w.T
        probs = jax.nn.softmax(logits.astype(jnp.float32), axis=-1)
        topk_p, topk_i = jax.lax.top_k(probs, TOP_K)
        topk_w = (topk_p / jnp.maximum(topk_p.sum(-1, keepdims=True), 1e-09)).astype(flat.dtype)
        combine = jnp.zeros((T, E), dtype=flat.dtype)
        combine = combine.at[jnp.arange(T)[:, None], topk_i].add(topk_w)
        out = jnp.zeros_like(flat)
        for e in range(E):
            out = out + _mlp(flat, w_fc[e], w_proj[e]) * combine[:, e:e + 1]
        out = out + _mlp(flat, shared_fc, shared_proj)
        return out.reshape(B, S, D)
    x = L0_attn_x
    x = x + _layernorm(_L0_attn_ref(_layernorm(x, axis=-1), L0_attn_W_in, L0_attn_A_in, L0_attn_B_in, L0_attn_W_out), axis=-1)
    x = x + _layernorm(_L0_ffn_ref(_layernorm(x, axis=-1), L0_ffn_W_r, L0_ffn_W_k, L0_ffn_W_v, L0_ffn_mu_r, L0_ffn_mu_k), axis=-1)
    x = x + _layernorm(_L1_attn_ref(_layernorm(x, axis=-1), L1_attn_Wq, L1_attn_Wk, L1_attn_Wv, L1_attn_Wo), axis=-1)
    x = x + _layernorm(_L1_ffn_ref(_layernorm(x, axis=-1), L1_ffn_router_w, L1_ffn_w_fc, L1_ffn_w_proj, L1_ffn_shared_fc, L1_ffn_shared_proj), axis=-1)
    return x

_drawn_inputs = setup_inputs


def setup_inputs(seed=0):
    import zlib

    import numpy as np

    out = dict(_drawn_inputs(seed))
    spreads = {'L0_attn_B_in': (0.0, 0.1)}
    factors = {}
    for name, (base, spread) in spreads.items():
        noise = np.random.default_rng([zlib.crc32(name.encode()), seed]).standard_normal(out[name].shape)
        drawn = base * np.exp(spread * noise) if base else spread * noise
        out[name] = jnp.asarray(drawn.astype(out[name].dtype))
    for name, factor in factors.items():
        out[name] = (out[name] * factor).astype(out[name].dtype)
    return out
```

```python
from contextlib import ExitStack

import concourse.bass as bass
from concourse import mybir

F32 = mybir.dt.float32
F32R = mybir.dt.float32r
U32 = mybir.dt.uint32
ALU = mybir.AluOpType
ACT = mybir.ActivationFunctionType
AX = mybir.AxisListType
P = 128
EPS = 1e-5


class Item:

    def __init__(self, reg, const, unroll):
        self.reg, self.const, self.unroll = reg, const, unroll

    def at(self, mult=1, add=0):
        if self.reg is None:
            return mult * self.const + add
        return self.reg * (mult * self.unroll) + (mult * self.const + add)

    def slot(self, n):
        assert self.unroll % n == 0
        return self.const % n

    def turn(self, n):
        assert self.unroll % n == 0
        if self.reg is None:
            return self.const // n
        return self.reg * (self.unroll // n) + self.const // n


def after(eng, sem, value):
    if isinstance(value, int) and value <= 0:
        return
    eng.wait_ge(sem, value)


class Gates:

    def __init__(self, sem):
        self.dve, self.pool = sem("dve_gate"), sem("pool_gate")

    @staticmethod
    def wait(eng, gate, sem, value):
        eng.wait_ge(sem, value)
        if not isinstance(value, int):
            eng.sem_inc(gate, 1)


def pipeline(eng, items, depth, unroll, step):
    lead = -(-(depth + 3) // unroll) * unroll
    turns = max((items - lead) // unroll, 0)

    def plain(t):
        step(lambda s: Item(None, t - s, unroll) if 0 <= t - s < items else None)

    for t in range(lead):
        plain(t)
    if turns:
        with eng.Fori(0, turns) as g:
            for u in range(unroll):
                step(lambda s, u=u: Item(g, lead + u - s, unroll))
    for t in range(lead + turns * unroll, items + depth - 1):
        plain(t)


def tiles(item, n):
    return bass.ds(item.at(n), n)


def program(nc, x_in, W_in, A_in, B_in, W_out, W_r, W_k, W_v, mu_r, mu_k,
            Wq, Wk, Wv, Wo, router_w, w_fc, w_proj, shared_fc, shared_proj, out):
    B, T, D = x_in.shape
    NT = B * T // P
    KT = T // P
    E = router_w.shape[0]
    assert D == P and T == 2 * P

    x_dram = x_in.rearrange("b (t p) d -> p (b t) d", p=P)
    out_dram = out.rearrange("b (t p) d -> p (b t) d", p=P)

    with ExitStack() as ctx:
        xs = ctx.enter_context(nc.sbuf_tensor("xs", [P, NT, D], F32))
        ident = ctx.enter_context(nc.sbuf_tensor("ident", [P, P], F32))
        neghalf = ctx.enter_context(nc.sbuf_tensor("neghalf", [P, 4], F32))
        gates = Gates(lambda name: ctx.enter_context(nc.semaphore(name)))
        eps = EPS
        layer0(nc, gates, xs, ident, neghalf, x_dram, W_in, A_in, B_in, W_out, W_r, W_k, W_v, mu_r, mu_k,
               B, T, D, NT, KT, eps)
        layer1_attention(nc, gates, xs, ident, neghalf, Wq, Wk, Wv, Wo, B, T, D, NT, KT, eps)
        layer1_experts(nc, gates, xs, ident, neghalf, router_w, w_fc, w_proj, shared_fc, shared_proj,
                       out_dram, B, T, D, NT, E, eps)


class Norm:

    def __init__(self, alloc, name, n, gates):
        sb, sem = alloc
        self.gates = gates
        self.n = n
        self.st = sb(f"{name}_st", [P, 2, n, 6], F32)
        self.mv = sb(f"{name}_mv", [P, 2, n, 2], F32)
        self.ve = sb(f"{name}_ve", [P, 2, n], F32)
        self.rs = sb(f"{name}_rs", [P, 2, n], F32)
        self.s_stats = sem(f"{name}_stats")
        self.s_mean = sem(f"{name}_mean")
        self.s_vareps = sem(f"{name}_vareps")
        self.s_rstd = sem(f"{name}_rstd")

    def stats(self, dve, item, src):
        n, b = self.n, item.slot(2)
        for j in range(n):
            dve.bn_stats(self.st[:, b, j, :], src(j)).then_inc(self.s_stats, 1)
        self.gates.wait(dve, self.gates.dve, self.s_stats, item.at(n, n))
        for j in range(n):
            dve.bn_aggr(self.mv[:, b, j, :], self.st[:, b, j, :]).then_inc(self.s_mean, 1)

    def rstd(self, pool, item, neghalf, eps):
        n, b = self.n, item.slot(2)
        self.gates.wait(pool, self.gates.pool, self.s_mean, item.at(n, n))
        pool.tensor_scalar(self.ve[:, b, :], self.mv[:, b, :, 1], eps, None, ALU.add)\
            .then_inc(self.s_vareps, 1)
        pool.wait_ge(self.s_vareps, item.at(1, 1))
        pool.tensor_tensor(self.rs[:, b, :], self.ve[:, b, :], neghalf[:, 0:n], ALU.pow)\
            .then_inc(self.s_rstd, 1)

    def ready(self, dve, item):
        dve.wait_ge(self.s_rstd, item.at(1, 1))

    def apply(self, dve, item, dst, src, s_done):
        b = item.slot(2)
        for j in range(self.n):
            dve.tensor_scalar(dst(j), src(j), self.mv[:, b, j, 0:1], self.rs[:, b, j:j + 1],
                              ALU.subtract, ALU.mult).then_inc(s_done, 1)


def scope(nc, ctx, phase):
    def sb(name, shape, dt):
        return ctx.enter_context(nc.sbuf_tensor(f"{phase}_{name}", shape, dt))

    def pb(name):
        return ctx.enter_context(nc.psum_tensor(f"{phase}_{name}", [P, 512], F32))

    def sem(name):
        return ctx.enter_context(nc.semaphore(f"{phase}_{name}"))

    return sb, pb, sem


def layer0(nc, gates, xs, ident, neghalf, x_dram, W_in, A_in, B_in, W_out, W_r, W_k, W_v, mu_r, mu_k,
           B, T, D, NT, KT, eps):
    H = 16
    DH = D // H
    SL = 32
    HC = P // SL
    NC = H // HC
    SCALE = float(DH) ** -0.5
    LORA = 1.0 / A_in.shape[0]
    qk_dram = nc.dram_tensor("qk_planes", [B, 2, 4, P, T], F32, kind="Internal").ap()
    max_dram = nc.dram_tensor("max_parts", [4, 2 * H, T], F32, kind="Internal").ap()

    with ExitStack() as ctx:
        sb, pb, sem = scope(nc, ctx, "l0")
        WT = sb("WT", [P, 4, D], F32)
        mu = sb("mu", [P, 2], F32)
        omu = sb("omu", [P, 2], F32)
        vall = sb("vall", [P, NT, D], F32)
        aall = sb("aall", [P, NT, D], F32)

        c3 = ctx.enter_context(ExitStack())
        NBUF = 4
        sb3, _, _ = scope(nc, c3, "l0st")
        QS = [sb3(f"QS{i}", [P, H, T], F32R) for i in range(NBUF)]
        KS = [sb3(f"KS{i}", [P, NC, T], F32R) for i in range(NBUF)]
        c4 = ctx.enter_context(ExitStack())
        WeffT = scope(nc, c4, "l0q")[0]("WeffT", [P, 3 * D], F32)

        s_x0, s_x = sem("s_x_quarter"), sem("s_x_rest")

        with ExitStack() as c2:
            sb2, pb2, sem2 = scope(nc, c2, "l0w")
            w_in = sb2("w_in", [P, 3, 3 * D], F32)
            a_in = sb2("a_in", [P, 3 * D], F32)
            b_in = sb2("b_in", [P, 3, P], F32)
            w4 = sb2("w4", [P, 4, D], F32)
            bT = sb2("bT", [P, 3 * D], F32)
            cz = sb2("cz", [P, 2, T], F32)
            ps_b, ps_e, ps_w = pb2("ps_b"), pb2("ps_e"), pb2("ps_w")
            s_w = sem2("s_weights")
            s_id = sem2("s_ident")
            s_c = sem2("s_rows")
            s_cd = sem2("s_rows_stored")
            s_pe = sem2("s_transposed")
            s_bT = sem2("s_bT")
            s_done = sem2("s_copied")
            with nc.Block() as block:
                @block.sync
                def _(sp):
                    sp.dma_start(w_in[:, :, :], W_in.rearrange("(c p) n -> p c n", p=P)).then_inc(s_w, 16)
                    sp.dma_start(a_in[:, :], A_in).then_inc(s_w, 16)
                    sp.dma_start(b_in[:, :, :], B_in.rearrange("(c p) n -> p c n", p=P)).then_inc(s_w, 16)
                    for n, w in enumerate((W_out, W_r, W_k, W_v)):
                        sp.dma_start(w4[:, n, :], w).then_inc(s_w, 16)
                    for n, m in enumerate((mu_r, mu_k)):
                        sp.dma_start(mu[:, n:n + 1], m.rearrange("(d a) -> d a", a=1)).then_inc(s_w, 16)
                    for q in range(4):
                        sp.dma_start(xs[:, q * NT // 4:(q + 1) * NT // 4, :],
                                     x_dram[:, q * NT // 4:(q + 1) * NT // 4, :]).then_inc(s_x if q else s_x0, 16)

                @block.gpsimd
                def _(pool):
                    pool.memset(ident[:, :], 0.0).then_inc(s_id, 1)
                    pool.memset(neghalf[:, :], -0.5)
                    pool.wait_ge(s_id, 1)
                    pool.affine_select(out=ident[:, :], in_=ident[:, :], compare_op=ALU.not_equal,
                                       fill=1.0, base=0, pattern=[[-1, P]], channel_multiplier=1)\
                        .then_inc(s_id, 1)
                    pool.memset(cz[:, 0, :], 0.0).then_inc(s_c, 1)
                    pool.wait_ge(s_c, 1)
                    pool.affine_select(out=cz[:, 1, :], in_=cz[:, 0, :], compare_op=ALU.is_ge,
                                       fill=1.0, base=-2 * H, pattern=[[0, T]],
                                       channel_multiplier=1).then_inc(s_c, 1)

                @block.tensor
                def _(pe):
                    pe.wait_ge(s_id, 2)
                    pe.wait_ge(s_w, 9 * 16)
                    for c in range(3):
                        mm = pe.transpose(ps_b[:, c * P:(c + 1) * P], b_in[:, c, :], ident[:, :])
                    mm.then_inc(s_pe, 1)
                    for n in range(4):
                        mm = pe.transpose(ps_w[:, n * P:(n + 1) * P], w4[:, n, :], ident[:, :])
                    mm.then_inc(s_pe, 1)
                    pe.wait_ge(s_bT, 1)
                    for c in range(3):
                        o = ps_e[:, c * P:(c + 1) * P]
                        for j in range(3):
                            pe.matmul(o, w_in[:, c, j * D:(j + 1) * D], ident[:, :],
                                      start=(j == 0), stop=False)
                        for j in range(3):
                            mm = pe.matmul(o, a_in[:, j * D:(j + 1) * D], bT[:, c * P:(c + 1) * P],
                                           start=False, stop=(j == 2))
                    mm.then_inc(s_pe, 1)

                @block.scalar
                def _(act):
                    act.wait_ge(s_c, 2)
                    for a in range(2):
                        act.dma_start(qk_dram[:, a, 3, :, :].rearrange("b p t -> p b t"),
                                      cz[:, a, :].unsqueeze(1).broadcast_to([P, B, T])).then_inc(s_cd, 16)
                    act.wait_ge(s_pe, 1)
                    act.activation(bT[:, :], ps_b[:, 0:3 * D], ACT.Copy, scale=LORA).then_inc(s_bT, 1)
                    act.wait_ge(s_pe, 3)
                    for a in range(2):
                        act.activation(WeffT[:, a * D:(a + 1) * D].rearrange("p (r h) -> p r h", h=H),
                                       ps_e[:, a * D:(a + 1) * D].rearrange("p (h r) -> p r h", h=H),
                                       ACT.Copy).then_inc(s_done, 1)
                    act.activation(WeffT[:, 2 * D:3 * D], ps_e[:, 2 * D:3 * D], ACT.Copy).then_inc(s_done, 1)
                    act.wait_ge(s_cd, 32)

                @block.vector
                def _(dve):
                    dve.wait_ge(s_w, 9 * 16)
                    dve.tensor_scalar(omu[:, :], mu[:, :], -1.0, 1.0, ALU.mult, ALU.add).then_inc(s_done, 1)
                    dve.wait_ge(s_pe, 2)
                    dve.tensor_copy(WT[:, :, :], ps_w[:, :].rearrange("p (n d) -> p n d", n=4))\
                        .then_inc(s_done, 1)

        with ExitStack() as c2:
            sb2, pb2, sem2 = scope(nc, c2, "l0in")
            ln = Norm((sb2, sem2), "ln_a", KT, gates)
            xn = sb2("xn", [P, 2, KT, D], F32)
            xT = sb2("xT", [P, 2, T], F32)
            qkh = sb2("qkh", [P, 2, 2, 2, T], F32R)
            qkl = sb2("qkl", [P, 2, 2, 2, T], F32R)
            ps_t = [pb2(f"ps_t{i}") for i in range(2)]
            ps_qk = [pb2(f"ps_qk{i}") for i in range(2)]
            ps_v = [pb2(f"ps_v{i}") for i in range(2)]
            s_xn, s_tp, s_xT = sem2("s_xn"), sem2("s_tp"), sem2("s_xT")
            s_qk, s_v = sem2("s_qk"), sem2("s_v")
            s_hi, s_lo, s_vc = sem2("s_hi"), sem2("s_lo"), sem2("s_vc")
            s_st = [sem2(f"s_stored{i}") for i in range(2)]
            DEPTH = 3
            with nc.Block() as block:
                @block.vector
                def _(dve):
                    def step(at):
                        if i := at(0):
                            if i.reg is None and i.const < NT // 4 // KT:
                                dve.wait_ge(s_x0, 16)
                            else:
                                dve.wait_ge(s_x, 48)
                            ln.stats(dve, i, lambda j: xs[:, i.at(KT, j), :])
                        if i := at(1):
                            b = i.slot(2)
                            ln.ready(dve, i)
                            after(dve, s_tp, i.at(1, -1))
                            ln.apply(dve, i, lambda j: xn[:, b, j, :], lambda j: xs[:, i.at(KT, j), :], s_xn)
                        if i := at(2):
                            b = i.slot(2)
                            pair = i.slot(4) // 2
                            dve.wait_ge(s_hi, i.at(1, 1))
                            after(dve, s_st[pair], i.turn(4) * 96)
                            dve.tensor_tensor(qkl[:, pair, b, :, :], ps_qk[b][:, :].rearrange("p (a t) -> p a t", a=2),
                                              qkh[:, pair, b, :, :], ALU.subtract).then_inc(s_lo, 1)
                    pipeline(dve, B, DEPTH, 4, step)

                @block.gpsimd
                def _(pool):
                    def step(at):
                        if i := at(0):
                            ln.rstd(pool, i, neghalf, eps)
                            if i.reg is None and i.const < NBUF:
                                pool.memset(QS[i.const][:, :, :].bitcast(F32), 0.0)
                    pipeline(pool, B, DEPTH, 4, step)

                @block.tensor
                def _(pe):
                    def step(at):
                        if i := at(2):
                            b = i.slot(2)
                            pe.wait_ge(s_xT, i.at(1, 1))
                            after(pe, s_lo, i.at(1, -1))
                            for a in range(2):
                                mm = pe.matmul(ps_qk[b][:, a * T:(a + 1) * T], WeffT[:, a * D:(a + 1) * D],
                                               xT[:, b, :], start=True, stop=True)
                            mm.then_inc(s_qk, 1)
                            after(pe, s_vc, i.at(1, -1))
                            for j in range(KT):
                                mm = pe.matmul(ps_v[b][:, j * D:(j + 1) * D], xT[:, b, j * P:(j + 1) * P],
                                               WeffT[:, 2 * D:3 * D], start=True, stop=True)
                            mm.then_inc(s_v, 1)
                        if i := at(1):
                            b = i.slot(2)
                            pe.wait_ge(s_xn, i.at(KT, KT))
                            after(pe, s_xT, i.at(1, -1))
                            for j in range(KT):
                                mm = pe.transpose(ps_t[b][:, j * P:(j + 1) * P], xn[:, b, j, :], ident[:, :])
                            mm.then_inc(s_tp, 1)
                    pipeline(pe, B, DEPTH, 4, step)

                @block.scalar
                def _(act):
                    def step(at):
                        if i := at(2):
                            b = i.slot(2)
                            pair = i.slot(4) // 2
                            act.wait_ge(s_qk, i.at(1, 1))
                            after(act, s_st[pair], i.turn(4) * 96)
                            act.activation(qkh[:, pair, b, :, :], ps_qk[b][:, :].rearrange("p (a t) -> p a t", a=2),
                                           ACT.Copy).then_inc(s_hi, 1)
                            act.wait_ge(s_v, i.at(1, 1))
                            act.activation(vall[:, tiles(i, KT), :],
                                           ps_v[b][:, 0:T].rearrange("p (t d) -> p t d", t=KT), ACT.Copy)\
                                .then_inc(s_vc, 1)
                        if i := at(1):
                            b = i.slot(2)
                            act.wait_ge(s_tp, i.at(1, 1))
                            after(act, s_v, i.at(1, -1))
                            act.activation(xT[:, b, :], ps_t[b][:, 0:T], ACT.Copy).then_inc(s_xT, 1)
                    pipeline(act, B, DEPTH, 4, step)

                @block.sync
                def _(sp):
                    def step(at):
                        if (i := at(2)) and i.slot(2) == 1:
                            pair = i.slot(4) // 2
                            for part, s, planes in ((qkh, s_hi, ((0, 0), (0, 2), (1, 1), (1, 2))),
                                                    (qkl, s_lo, ((0, 1), (1, 0)))):
                                sp.wait_ge(s, i.at(1, 1))
                                for a, plane in planes:
                                    sp.dma_start(qk_dram[bass.ds(i.at(1, -1), 2), a, plane, :, :]
                                                 .rearrange("o p t -> p o t"),
                                                 part[:, pair, :, a, :].bitcast(F32)).then_inc(s_st[pair], 16)
                    pipeline(sp, B, DEPTH, 4, step)
                    for b in range(2):
                        sp.wait_ge(s_st[b], B // 4 * 96)

        c4.close()

        with ExitStack() as c2:
            sb2, pb2, sem2 = scope(nc, c2, "l0att")
            V0 = sb2("V0", [P, 2, KT, H, SL], F32)
            NPT = 3
            PT = sb2("PT", [P, NPT, HC, T], F32)
            OT = sb2("OT", [P, NC, T], F32)
            nmax = sb2("nmax", [P, KT, H], F32)
            mparts = sb2("mparts", [P, 2, KT, 2, H], F32R)
            mT = sb2("mT", [2 * H, 2, T], F32)
            rsum = sb2("rsum", [P, 2, H], F32)
            ps_a = [pb2(f"ps_a{i}") for i in range(2)]
            ps_s = [c2.enter_context(nc.psum_tensor(f"l0att_ps_s{i}", [P, HC, T], F32)) for i in range(2)]
            ps_o, ps_x = pb2("ps_o"), pb2("ps_x")
            s_ld = [sem2(f"s_loaded{i}") for i in range(NBUF)]
            s_mr = [sem2(f"s_maxrows{i}") for i in range(NBUF)]
            s_md = sem2("s_maxstored")
            s_a, s_mx, s_mp = sem2("s_passA"), sem2("s_max"), sem2("s_maxparts")
            s_mtp, s_mT = sem2("s_maxT_ps"), sem2("s_maxT")
            s_s, s_e, s_pv, s_oc = sem2("s_scores"), sem2("s_exp"), sem2("s_pv"), sem2("s_ocopied")
            s_v0 = sem2("s_v0")
            s_ot, s_rc, s_n = sem2("s_otT"), sem2("s_recip"), sem2("s_normed")
            STEPS = NC * KT
            LOADS = 2 * HC * 16
            DEPTH = 5
            with nc.Block() as block:
                @block.sync
                def _(sp):
                    def step(at):
                        if i := at(0):
                            b = i.slot(NBUF)
                            after(sp, s_s, i.at(STEPS, -(NBUF - 1) * STEPS))
                            for j in range(HC):
                                for a, dst in enumerate((QS[b][SL * j:SL * (j + 1), j:H:HC, :],
                                                         KS[b][SL * j:SL * (j + 1)])):
                                    src = qk_dram[bass.ds(i.at(), 1), a, :, :, :]\
                                        .rearrange("o g (r c j) t -> j (o g r) c t", r=DH, j=HC)[j]
                                    sp.dma_start(dst.bitcast(F32), src).then_inc(s_ld[b], 16)
                        if i := at(2):
                            b = i.slot(NBUF)
                            sp.wait_ge(s_mT, i.at(1, 1))
                            sp.dma_start(max_dram[b], mT[:, i.slot(2), :]).then_inc(s_md, 16)
                            sp.wait_ge(s_md, i.at(16, 16))
                            for j in range(HC):
                                row = SL * j + 3 * DH
                                sp.dma_start(QS[b][row:row + 2, j:H:HC, :].bitcast(F32),
                                             max_dram[b].rearrange("(l c j) t -> j l c t", l=2, j=HC)[j])\
                                    .then_inc(s_mr[b], 16)
                    pipeline(sp, B, DEPTH, NBUF, step)

                @block.gpsimd
                def _(pool):
                    pool.memset(V0[:, :, :, :, DH + 1:SL], 0.0)
                    pool.memset(V0[:, :, :, :, DH:DH + 1], 1.0)

                    def step(at):
                        if i := at(2):
                            b = i.slot(2)
                            after(pool, s_pv, i.at(STEPS, -STEPS))
                            pool.tensor_copy(V0[:, b, :, :, 0:DH],
                                             vall[:, tiles(i, KT), :].rearrange("p t (h d) -> p t h d", h=H))\
                                .then_inc(s_v0, 1)
                    pipeline(pool, B, DEPTH, NBUF, step)

                @block.tensor
                def _(pe):
                    def pass_a(i, k):
                        t, h = k // 8, 2 * (k % 8)
                        b = i.slot(NBUF)
                        after(pe, s_mx, i.at(16, k - 1))
                        for n in range(2):
                            mm = pe.matmul(ps_a[k % 2][:, n * T:(n + 1) * T], QS[b][:, h + n, t * P:(t + 1) * P],
                                           KS[b][:, (h + n) // HC, :], start=True, stop=True)
                        mm.then_inc(s_a, 1)

                    def scores(i, s):
                        c, kt = s // KT, s % KT
                        b = i.slot(NBUF)
                        after(pe, s_e, i.at(STEPS, s - 1))
                        for n in range(2):
                            mm = pe.matmul(ps_s[s % 2][:, 2 * n:2 * n + 2, :], KS[b][:, c, kt * P:(kt + 1) * P],
                                           QS[b][:, HC * c + 2 * n:HC * c + 2 * n + 2, :], start=True, stop=True)
                        mm.then_inc(s_s, 1)

                    def pv(i, s):
                        c, kt = s // KT, s % KT
                        pe.wait_ge(s_e, i.at(STEPS, s + 1))
                        if s == 0:
                            pe.wait_ge(s_v0, i.at(1, 1))
                        if s % 4 == 0:
                            after(pe, s_oc, i.at(2, s // 4))
                        for j in range(HC):
                            mm = pe.matmul(ps_o[SL * j:SL * (j + 1), (c % 2) * T:(c % 2 + 1) * T],
                                           V0[:, i.slot(2), kt, HC * c + j, :], PT[:, s % NPT, j, :],
                                           start=(kt == 0), stop=(kt == KT - 1))
                        mm.then_inc(s_pv, 1)

                    def max_transposed(i):
                        pe.wait_ge(s_mp, i.at(2, 2))
                        after(pe, s_n, i.at(KT, -2 * KT))
                        for t in range(KT):
                            mm = pe.transpose(ps_x[0:2 * H, t * P:(t + 1) * P],
                                              mparts[:, i.slot(2), t, :, :].bitcast(F32).rearrange("p l h -> p (l h)"),
                                              ident[:, :])
                        mm.then_inc(s_mtp, 1)

                    def out_transposed(i, t, other):
                        if t == 0:
                            pe.wait_ge(s_oc, i.at(2, 2))
                            if other:
                                pe.wait_ge(s_mT, other.at(1, 1))
                        after(pe, s_n, i.at(KT, t))
                        for c in range(NC):
                            mm = pe.transpose(ps_x[:, c * P:(c + 1) * P], OT[:, c, t * P:(t + 1) * P],
                                              ident[:, :])
                        mm.then_inc(s_ot, 1)

                    def step(at):
                        ia, im, ib, io = at(1), at(2), at(3), at(4)
                        if ia:
                            b = ia.slot(NBUF)
                            pe.wait_ge(s_ld[b], ia.turn(NBUF) * LOADS + LOADS)
                        if ib:
                            b = ib.slot(NBUF)
                            pe.wait_ge(s_mr[b], ib.turn(NBUF) * 64 + 64)
                        for s in range(STEPS):
                            if ia:
                                pass_a(ia, 2 * s)
                            if ib:
                                scores(ib, s)
                            if ia:
                                pass_a(ia, 2 * s + 1)
                            if ib and s >= 2:
                                pv(ib, s - 2)
                            elif io and s < 2:
                                pv(io, STEPS - 2 + s)
                            if im and s == 0:
                                max_transposed(im)
                            if io and s in (3, 5):
                                out_transposed(io, (s - 3) // 2, im if s == 3 else None)
                    pipeline(pe, B, DEPTH, NBUF, step)

                @block.scalar
                def _(act):
                    def o_copied(i, n):
                        act.wait_ge(s_pv, i.at(STEPS, 4 * n + 4))
                        if n == 0:
                            after(act, s_ot, i.at(KT))
                        act.activation(OT[:, 2 * n:2 * n + 2, :],
                                       ps_o[:, :].rearrange("p (c t) -> p c t", c=2), ACT.Copy)\
                            .then_inc(s_oc, 1)

                    def step(at):
                        im, ib, io = at(2), at(3), at(4)
                        if im:
                            act.wait_ge(s_mtp, im.at(1, 1))
                            after(act, s_md, im.at(16, -16))
                            act.activation(mT[:, im.slot(2), :], ps_x[0:2 * H, 0:T], ACT.Copy).then_inc(s_mT, 1)
                        for s in range(STEPS):
                            if ib:
                                act.wait_ge(s_s, ib.at(STEPS, s + 1))
                                after(act, s_pv, ib.at(STEPS, s - 1 if s < 2 else s - NPT + 1))
                                act.activation(PT[:, s % NPT, :, :], ps_s[s % 2][:, :, :], ACT.Exp, scale=SCALE)\
                                    .then_inc(s_e, 1)
                            if ib and s == 5:
                                o_copied(ib, 0)
                            if io and s == 1:
                                o_copied(io, 1)
                    pipeline(act, B, DEPTH, NBUF, step)

                @block.vector
                def _(dve):
                    def normalise(i, t):
                        dve.wait_ge(s_ot, i.at(KT, t + 1))
                        o = ps_x[:, :].rearrange("p (h s) -> p h s", h=H)
                        dve.reciprocal(rsum[:, t, :], o[:, :, DH]).then_inc(s_rc, 1)
                        dve.wait_ge(s_rc, i.at(KT, t + 1))
                        dst = aall[:, bass.ds(i.at(KT, t), 1), :].rearrange("p o (h d) -> p (o h) d", h=H)
                        dve.tensor_tensor(dst, o[:, :, 0:DH],
                                          rsum[:, t, :].unsqueeze(2).broadcast_to([P, H, DH]),
                                          ALU.mult).then_inc(s_n, 1)

                    def step(at):
                        ia, io = at(1), at(4)
                        for k in range(2 * STEPS):
                            if ia:
                                t, h = k // 8, 2 * (k % 8)
                                dve.wait_ge(s_a, ia.at(16, k + 1))
                                if k == 0:
                                    after(dve, s_mp, ia.at(2))
                                dve.tensor_reduce(nmax[:, t, h:h + 2], ps_a[k % 2][:, :].rearrange("p (n t) -> p n t", n=2),
                                                  AX.X, ALU.max, negate=True).then_inc(s_mx, 1)
                            if io and k in (7, 11):
                                normalise(io, (k - 7) // 4)
                        if ia:
                            b = ia.slot(2)
                            dve.wait_ge(s_mx, ia.at(16, 16))
                            after(dve, s_mtp, ia.at(1, -1))
                            dve.tensor_copy(mparts[:, b, :, 0, :], nmax[:, :, :]).then_inc(s_mp, 1)
                            dve.wait_ge(s_mp, ia.at(2, 1))
                            dve.tensor_tensor(mparts[:, b, :, 1, :], nmax[:, :, :], mparts[:, b, :, 0, :],
                                              ALU.subtract).then_inc(s_mp, 1)
                    pipeline(dve, B, DEPTH, NBUF, step)

        c3.close()

        with ExitStack() as c2:
            sb2, pb2, sem2 = scope(nc, c2, "l0mix")
            G = 2 * KT
            N = G * P
            ln1, ln2, ln3 = (Norm((sb2, sem2), f"ln_c{k}", G, gates) for k in (1, 2, 3))
            an = sb2("an", [P, 2, G, D], F32)
            aT = sb2("aT", [P, 2, N], F32)
            y = sb2("y", [P, 2, G, D], F32)
            xn = sb2("xn", [P, 2, G, D], F32)
            xT = sb2("xT", [P, 2, 2, T + 1], F32)
            prev = sb2("prev", [P, 2, 2, N], F32)
            mix = sb2("mix", [P, 2, 2, N], F32)
            kr = sb2("kr", [P, 2, N], F32)
            k2 = sb2("k2", [P, 2, N], F32)
            sg = sb2("sg", [P, 2, G, D], F32)
            f = sb2("f", [P, 2, G, D], F32)
            ps_at = pb2("ps_at")
            ps_y = [pb2(f"ps_y{i}") for i in range(2)]
            ps_xt, ps_k, ps_r = pb2("ps_xt"), pb2("ps_k"), pb2("ps_r")
            ps_kv = [pb2(f"ps_kv{i}") for i in range(2)]
            names = "an at aT y yn x1 xn tp xT pv mix k r kr k2 sg kv f fn x2".split()
            s = {n: sem2(f"s_{n}") for n in names}
            s_z = sem2("s_z")
            DEPTH = 8

            def g3(ap):
                return ap.rearrange("p (g d) -> p g d", g=G)

            with nc.Block() as block:
                @block.tensor
                def _(pe):
                    def step(at):
                        if i := at(4):
                            b = i.slot(2)
                            pe.wait_ge(s["mix"], i.at(2, 2))
                            after(pe, s["kr"], i.at(1))
                            pe.matmul(ps_k[:, :], WT[:, 2, :], mix[:, b, 1, :], start=True, stop=True)\
                                .then_inc(s["k"], 1)
                            after(pe, s["sg"], i.at(1))
                            for j in range(G):
                                mm = pe.matmul(ps_r[:, j * P:(j + 1) * P], mix[:, b, 0, j * P:(j + 1) * P],
                                               WT[:, 1, :], start=True, stop=True)
                            mm.then_inc(s["r"], 1)
                        if i := at(5):
                            b = i.slot(2)
                            pe.wait_ge(s["k2"], i.at(1, 1))
                            after(pe, s["f"], i.at(1, -1))
                            for j in range(G):
                                mm = pe.matmul(ps_kv[b][:, j * P:(j + 1) * P], k2[:, b, j * P:(j + 1) * P],
                                               WT[:, 3, :], start=True, stop=True)
                            mm.then_inc(s["kv"], 1)
                        if i := at(3):
                            b = i.slot(2)
                            pe.wait_ge(s["xn"], i.at(G, G))
                            after(pe, s["xT"], i.at(1))
                            for j in range(G):
                                mm = pe.transpose(ps_xt[:, j * P:(j + 1) * P], xn[:, b, j, :], ident[:, :])
                            mm.then_inc(s["tp"], 1)
                        if i := at(1):
                            b = i.slot(2)
                            pe.wait_ge(s["aT"], i.at(1, 1))
                            after(pe, s["yn"], i.at(G, -G))
                            for j in range(G):
                                mm = pe.matmul(ps_y[b][:, j * P:(j + 1) * P], aT[:, b, j * P:(j + 1) * P],
                                               WT[:, 0, :], start=True, stop=True)
                            mm.then_inc(s["y"], 1)
                        if i := at(0):
                            pe.wait_ge(s["an"], i.at(1, 1))
                            after(pe, s["aT"], i.at(1))
                            for j in range(G):
                                mm = pe.transpose(ps_at[:, j * P:(j + 1) * P],
                                                  an[:, i.slot(2), j, :], ident[:, :])
                            mm.then_inc(s["at"], 1)
                    pipeline(pe, NT // G, DEPTH, 2, step)

                @block.scalar
                def _(act):
                    def step(at):
                        if i := at(4):
                            b = i.slot(2)
                            act.wait_ge(s["k"], i.at(1, 1))
                            after(act, s["k2"], i.at(1, -1))
                            act.activation(kr[:, b, :], ps_k[:, :], ACT.Relu).then_inc(s["kr"], 1)
                            act.wait_ge(s["r"], i.at(1, 1))
                            after(act, s["f"], i.at(1, -1))
                            act.activation(sg[:, b, :, :], g3(ps_r[:, :]), ACT.Sigmoid).then_inc(s["sg"], 1)
                        if i := at(3):
                            b = i.slot(2)
                            act.wait_ge(s["tp"], i.at(1, 1))
                            after(act, s["mix"], i.at(2, -2))
                            act.activation(xT[:, b, :, 1:T + 1], ps_xt[:, :].rearrange("p (c t) -> p c t", c=2),
                                           ACT.Copy).then_inc(s["xT"], 1)
                        if i := at(0):
                            b = i.slot(2)
                            act.wait_ge(s["at"], i.at(1, 1))
                            after(act, s["y"], i.at(1, -1))
                            act.activation(aT[:, b, :], ps_at[:, :], ACT.Copy).then_inc(s["aT"], 1)
                    pipeline(act, NT // G, DEPTH, 2, step)

                @block.gpsimd
                def _(pool):
                    def step(at):
                        if i := at(0):
                            after(pool, s["at"], i.at(1, -1))
                            pool.tensor_copy(an[:, i.slot(2), :, :], aall[:, tiles(i, G), :]).then_inc(s["an"], 1)
                        if i := at(6):
                            ln3.rstd(pool, i, neghalf, eps)
                        if i := at(3):
                            b = i.slot(2)
                            after(pool, s["mix"], i.at(2, -2))
                            gates.wait(pool, gates.pool, s["xT"], i.at(1, 1))
                            for n in range(2):
                                pool.tensor_scalar(prev[:, b, n, :].rearrange("p (c t) -> p c t", c=2),
                                                   xT[:, b, :, 0:T], omu[:, n:n + 1], None, ALU.mult)\
                                    .then_inc(s["pv"], 1)
                        if i := at(2):
                            ln2.rstd(pool, i, neghalf, eps)
                        if i := at(1):
                            ln1.rstd(pool, i, neghalf, eps)
                    pool.memset(xT[:, :, :, 0:1], 0.0)
                    pipeline(pool, NT // G, DEPTH, 2, step)

                @block.vector
                def _(dve):
                    def step(at):
                        if i := at(6):
                            b = i.slot(2)
                            dve.wait_ge(s["kv"], i.at(1, 1))
                            dve.wait_ge(s["sg"], i.at(1, 1))
                            dve.tensor_tensor(f[:, b, :, :], g3(ps_kv[b][:, :]), sg[:, b, :, :], ALU.mult)\
                                .then_inc(s["f"], 1)
                        if i := at(4):
                            b = i.slot(2)
                            dve.wait_ge(s["pv"], i.at(2, 2))
                            after(dve, s["r"], i.at(1, -1))
                            for n in range(2):
                                dve.scalar_tensor_tensor(mix[:, b, n, :].rearrange("p (c t) -> p c t", c=2),
                                                         xT[:, b, :, 1:T + 1], mu[:, n:n + 1],
                                                         prev[:, b, n, :].rearrange("p (c t) -> p c t", c=2),
                                                         ALU.mult, ALU.add).then_inc(s["mix"], 1)
                        if i := at(5):
                            b = i.slot(2)
                            dve.wait_ge(s["kr"], i.at(1, 1))
                            after(dve, s["kv"], i.at(1, -1))
                            dve.tensor_tensor(k2[:, b, :], kr[:, b, :], kr[:, b, :], ALU.mult)\
                                .then_inc(s["k2"], 1)
                        if i := at(6):
                            gates.wait(dve, gates.dve, s["f"], i.at(1, 1))
                            ln3.stats(dve, i, lambda j: f[:, i.slot(2), j, :])
                        if i := at(3):
                            b = i.slot(2)
                            ln2.ready(dve, i)
                            after(dve, s["tp"], i.at(1, -1))
                            ln2.apply(dve, i, lambda j: xn[:, b, j, :], lambda j: xs[:, i.at(G, j), :], s["xn"])
                        if i := at(7):
                            b = i.slot(2)
                            ln3.ready(dve, i)
                            ln3.apply(dve, i, lambda j: y[:, b, j, :], lambda j: f[:, b, j, :], s["fn"])
                            dve.wait_ge(s["fn"], i.at(G, G))
                            dve.tensor_tensor(xs[:, tiles(i, G), :], xs[:, tiles(i, G), :], y[:, b, :, :],
                                              ALU.add).then_inc(s["x2"], 1)
                        if i := at(2):
                            b = i.slot(2)
                            ln1.ready(dve, i)
                            ln1.apply(dve, i, lambda j: y[:, b, j, :], lambda j: ps_y[b][:, j * P:(j + 1) * P],
                                      s["yn"])
                            dve.wait_ge(s["yn"], i.at(G, G))
                            dve.tensor_tensor(xs[:, tiles(i, G), :], xs[:, tiles(i, G), :], y[:, b, :, :],
                                              ALU.add).then_inc(s["x1"], 1)
                            gates.wait(dve, gates.dve, s["x1"], i.at(1, 1))
                            ln2.stats(dve, i, lambda j: xs[:, i.at(G, j), :])
                        if i := at(1):
                            b = i.slot(2)
                            gates.wait(dve, gates.dve, s["y"], i.at(1, 1))
                            ln1.stats(dve, i, lambda j: ps_y[b][:, j * P:(j + 1) * P])
                    pipeline(dve, NT // G, DEPTH, 2, step)


def split_matmul(pe, out, w, x, start=True, stop=True):
    pe.matmul(out, w[0], x[0], start=start, stop=False)
    pe.matmul(out, w[0], x[1], start=False, stop=False)
    return pe.matmul(out, w[1], x[0], start=False, stop=stop)


def layer1_attention(nc, gates, xs, ident, neghalf, Wq, Wk, Wv, Wo, B, T, D, NT, KT, eps):
    H = 16
    F = Wq.shape[0]
    DH = F // H
    NP = H // 2
    CLAMP = 50.0
    SCALE = float(DH) ** -0.5
    W = T + P
    with ExitStack() as ctx:
        sb, pb, sem = scope(nc, ctx, "l1")
        wh = sb("wh", [P, 3, F], F32R)
        wl = sb("wl", [P, 3, F], F32R)
        woT = sb("woT", [P, NP, D], F32)
        cols = sb("cols", [P, 4, 32], F32)
        sel = sb("sel", [P, NP, P], F32R)

        with ExitStack() as c2:
            sb2, pb2, sem2 = scope(nc, c2, "l1w")
            nat = sb2("nat", [P, 3, NP, D], F32)
            wo = sb2("wo", [P, F], F32)
            self32 = sb2("self32", [P, NP, P], F32)
            ps = [pb2(f"ps{i}") for i in range(4)]
            s_w, s_pe, s_hi, s_lo = sem2("s_w"), sem2("s_pe"), sem2("s_hi"), sem2("s_lo")
            s_c, s_sel = sem2("s_c"), sem2("s_sel")
            G = 3 * NP // 4
            with nc.Block() as block:
                @block.sync
                def _(sp):
                    for n, w in enumerate((Wq, Wk, Wv)):
                        sp.dma_start(nat[:, n, :, :], w.rearrange("(c p) d -> p c d", p=P)).then_inc(s_w, 16)
                    sp.dma_start(wo[:, :], Wo).then_inc(s_w, 16)
                    sp.wait_ge(s_w, 64)

                @block.gpsimd
                def _(pool):
                    pool.memset(cols[:, :, 0:4], 0.0).then_inc(s_c, 1)
                    pool.memset(cols[:, :, 4:32], 1.0)
                    pool.memset(self32[:, :, :], 0.0).then_inc(s_c, 1)
                    pool.wait_ge(s_c, 2)
                    for c in range(4):
                        pool.memset(cols[:, c, c:c + 1], 1.0)
                    for h in range(H):
                        o = self32[:, h // 2, (h % 2) * DH:(h % 2 + 1) * DH]
                        last = pool.affine_select(out=o, in_=o, compare_op=ALU.not_equal, fill=1.0,
                                                  base=-(32 * (h % 4) + h // 4), pattern=[[0, DH]],
                                                  channel_multiplier=1)
                    last.then_inc(s_sel, 1)

                @block.tensor
                def _(pe):
                    pe.wait_ge(s_w, 64)
                    for g in range(G + 2):
                        if g >= 4:
                            pe.wait_ge(s_lo, g - 3)
                        for n in range(4):
                            c = 4 * g + n
                            src = nat[:, c // NP, c % NP, :] if g < G else wo[:, (c - 4 * G) * P:(c - 4 * G + 1) * P]
                            mm = pe.transpose(ps[g % 4][:, n * P:(n + 1) * P], src, ident[:, :])
                        mm.then_inc(s_pe, 1)

                @block.scalar
                def _(act):
                    for g in range(G):
                        act.wait_ge(s_pe, g + 1)
                        a, c = g // 2, g % 2 * 512
                        act.activation(wh[:, a, c:c + 512], ps[g % 4][:, :], ACT.Copy).then_inc(s_hi, 1)

                @block.vector
                def _(dve):
                    for g in range(G):
                        dve.wait_ge(s_hi, g + 1)
                        a, c = g // 2, g % 2 * 512
                        dve.tensor_tensor(wl[:, a, c:c + 512], ps[g % 4][:, :], wh[:, a, c:c + 512],
                                          ALU.subtract).then_inc(s_lo, 1)
                    for g in range(2):
                        dve.wait_ge(s_pe, G + g + 1)
                        dve.tensor_copy(woT[:, 4 * g:4 * g + 4, :], ps[(G + g) % 4][:, :].rearrange("p (n d) -> p n d", n=4))
                    dve.wait_ge(s_sel, 1)
                    dve.tensor_copy(sel[:, :, :], self32[:, :, :])

        with ExitStack() as c2:
            sb2, pb2, sem2 = scope(nc, c2, "l1att")
            ln = Norm((sb2, sem2), "l1_ln", KT, gates)
            ln2 = Norm((sb2, sem2), "l1_ln2", KT, gates)
            xn = sb2("xn", [P, 2, KT, D], F32)
            xh = sb2("xh", [P, 2, T], F32R)
            xl = sb2("xl", [P, 2, T], F32R)
            kT = sb2("kT", [P, 2, NP, T], F32)
            qm = sb2("qm", [P, 2, NP, 2, T], F32)
            V = sb2("V", [P, 2, KT, F], F32)
            th = sb2("th", [P, 2, 2, W], F32)
            pt = sb2("pt", [P, 4, 2, 3, P], F32)
            oraw = sb2("oraw", [P, 2, NP, T], F32)
            on = sb2("on", [P, 2, 2, T], F32)
            rec = sb2("rec", [P, T], F32)
            rh = sb2("rh", [P, T], F32R)
            rl = sb2("rl", [P, T], F32R)
            y = sb2("y", [P, 2, KT, D], F32)
            ps_s = c2.enter_context(nc.psum_tensor("l1att_ps_s", [P, 2, 512], F32))
            ps_qk, ps_j = pb2("ps_qk"), pb2("ps_j")
            ps_o = [pb2(f"ps_o{i}") for i in range(2)]
            ps_sum, ps_y = pb2("ps_sum"), pb2("ps_y")
            names = "z xn tp xh xl qk qkc v vc sc th ex mk pv oc rec rh rl r on y yn x".split()
            s = {n: sem2(f"s_{n}") for n in names}
            DEPTH = 6

            def copy_qk(eng, i, p):
                b = i.slot(2)
                after(eng, s["sc"], i.at(NP, -NP))
                for hh in range(2):
                    r = slice(hh * DH, (hh + 1) * DH)
                    if p % 2:
                        eng.activation(qm[r, b, p, hh, :], ps_qk[r, 0:T], ACT.Copy)
                    else:
                        eng.tensor_copy(qm[r, b, p, hh, :], ps_qk[r, 0:T])
                if p % 2:
                    eng.activation(kT[:, b, p, :], ps_qk[:, T:2 * T], ACT.Copy).then_inc(s["qkc"], 1)
                else:
                    eng.tensor_copy(kT[:, b, p, :], ps_qk[:, T:2 * T]).then_inc(s["qkc"], 1)

            with nc.Block() as block:
                @block.tensor
                def _(pe):
                    def scores(i, p):
                        b = i.slot(2)
                        after(pe, s["th"], i.at(NP, p))
                        if p == 0:
                            pe.wait_ge(s["qkc"], i.at(NP, NP))
                        for hh in range(2):
                            pe.matmul(ps_s[:, hh, 0:T], kT[:, b, p, 0:P], qm[:, b, p, hh, :], start=True, stop=True)
                            mm = pe.matmul(ps_s[:, hh, T:W], kT[:, b, p, P:T], qm[:, b, p, hh, P:T],
                                           start=True, stop=True)
                        mm.then_inc(s["sc"], 1)

                    def project(i, p):
                        b = i.slot(2)
                        if p == 0:
                            pe.wait_ge(s["xl"], i.at(1, 1))
                        after(pe, s["qkc"], i.at(NP, p))
                        c = slice(p * P, (p + 1) * P)
                        for a in range(2):
                            mm = split_matmul(pe, ps_qk[:, a * T:(a + 1) * T], (wh[:, a, c], wl[:, a, c]),
                                              (xh[:, b, :], xl[:, b, :]))
                        mm.then_inc(s["qk"], 1)

                    def values(i, u, io):
                        b, kt, half = i.slot(2), u // 2, u % 2
                        if io:
                            pe.wait_ge(s["on"], io.at(4, u + 1))
                        elif u:
                            pe.wait_ge(s["vc"], i.at(4, u))
                        else:
                            pe.wait_ge(s["xl"], i.at(1, 2))
                        c = slice(kt * P, (kt + 1) * P)
                        f = slice(half * 512, (half + 1) * 512)
                        pe.matmul(ps_j[:, :], xh[:, b, c], wh[:, 2, f], start=True, stop=False)
                        pe.matmul(ps_j[:, :], xh[:, b, c], wl[:, 2, f], start=False, stop=False)
                        pe.matmul(ps_j[:, :], xl[:, b, c], wh[:, 2, f], start=False, stop=True)\
                            .then_inc(s["v"], 1)

                    def spread(i, u, ip, ix):
                        if u == 0:
                            pe.wait_ge(s["rl"], i.at(1, 1))
                            if ix:
                                pe.wait_ge(s["xl"], ix.at(1, 1))
                        if ip and u:
                            pe.wait_ge(s["vc"], ip.at(4, u))
                        elif not ip and u == 0:
                            pe.wait_ge(s["vc"], 4 * B)
                        elif not ip:
                            pe.wait_ge(s["on"], i.at(4, u))
                        elif u == 0:
                            after(pe, s["vc"], ip.at(4))
                        for n in range(2):
                            o = ps_j[:, n * T:(n + 1) * T]
                            pe.matmul(o, sel[:, 2 * u + n, :], rh[:, :], start=True, stop=False)
                            mm = pe.matmul(o, sel[:, 2 * u + n, :], rl[:, :], start=False, stop=True)
                        mm.then_inc(s["r"], 1)

                    def project_out(i, u):
                        pe.wait_ge(s["on"], i.at(4, u + 1))
                        if u == 0:
                            after(pe, s["yn"], i.at(KT))
                        for n in range(2):
                            for t in range(KT):
                                mm = pe.matmul(ps_y[:, t * P:(t + 1) * P], on[:, u % 2, n, t * P:(t + 1) * P],
                                               woT[:, 2 * u + n, :], start=(u == 0 and n == 0 and t == 0),
                                               stop=(u == 3 and n == 1), skip_group_check=True)
                        mm.then_inc(s["y"], 1)

                    def pv(i, p):
                        b = i.slot(2)
                        pe.wait_ge(s["mk"], i.at(NP, p + 1))
                        if p % 2 == 0:
                            after(pe, s["oc"], i.at(4, p // 2 - 1))
                        if p == 0:
                            pe.wait_ge(s["vc"], i.at(4, 4))
                            after(pe, s["rec"], i.at(1))
                        o, c = ps_o[p // 2 % 2], p % 2 * T
                        for kt in range(KT):
                            for hh in range(2):
                                h = 2 * p + hh
                                pr = pt[:, p % 4, hh, 0:2, :] if kt == 0 else pt[:, p % 4, hh, 2:3, :]
                                pe.matmul(o[hh * DH:(hh + 1) * DH, c + kt * P:c + T], V[:, b, kt, h * DH:(h + 1) * DH],
                                          pr, start=(kt == 0), stop=(kt == 1), skip_group_check=True)
                        for kt in range(KT):
                            for hh in range(2):
                                h = 2 * p + hh
                                pr = pt[:, p % 4, hh, 0:2, :] if kt == 0 else pt[:, p % 4, hh, 2:3, :]
                                j = 32 * (h % 4)
                                mm = pe.matmul(ps_sum[j:j + 32, kt * P:T], cols[:, h // 4, :], pr,
                                               start=(h < 4 and kt == 0), stop=(h >= 12 and kt == 1),
                                               skip_group_check=True)
                        mm.then_inc(s["pv"], 1)

                    def turned(i):
                        pe.wait_ge(s["xn"], i.at(KT, KT))
                        after(pe, s["vc"], i.at(4, -4))
                        for j in range(KT):
                            mm = pe.transpose(ps_j[:, j * P:(j + 1) * P], xn[:, i.slot(2), j, :], ident[:, :])
                        mm.then_inc(s["tp"], 1)

                    def step(at):
                        ix, ip, ic, io = at(1), at(2), at(3), at(4)
                        if ix:
                            turned(ix)
                        for p in range(NP):
                            if ic:
                                scores(ic, p)
                            if ic and p >= 2:
                                pv(ic, p - 2)
                            if ip:
                                project(ip, p)
                            if p % 2 == 0:
                                if io:
                                    spread(io, p // 2, ip, ix)
                            else:
                                if ip:
                                    values(ip, p // 2, io)
                                if io:
                                    project_out(io, p // 2)
                        if ic:
                            pv(ic, NP - 2)
                            pv(ic, NP - 1)
                    pipeline(pe, B, DEPTH, 2, step)

                @block.scalar
                def _(act):
                    def probabilities(i, p):
                        if p < NP:
                            act.wait_ge(s["sc"], i.at(NP, p + 1))
                            after(act, s["ex"], i.at(NP, p - 1))
                            act.activation(th[:, p % 2, :, :], ps_s[:, :, 0:W], ACT.Tanh, scale=SCALE / CLAMP)\
                                .then_inc(s["th"], 1)
                        if p:
                            act.wait_ge(s["th"], i.at(NP, p))
                            after(act, s["pv"], i.at(NP, p - 4))
                            act.activation(pt[:, (p - 1) % 4, :, :, :].rearrange("p h a b -> p h (a b)"),
                                           th[:, (p - 1) % 2, :, :], ACT.Exp, scale=CLAMP).then_inc(s["ex"], 1)

                    def step(at):
                        ix, ip, ic = at(1), at(2), at(3)
                        if ix:
                            b = ix.slot(2)
                            act.wait_ge(s["tp"], ix.at(1, 1))
                            after(act, s["v"], ix.at(4, -4))
                            act.activation(xh[:, b, :], ps_j[:, 0:T], ACT.Copy).then_inc(s["xh"], 1)
                        for p in range(NP + 1):
                            if ic:
                                probabilities(ic, p)
                            if ip and p < NP and p % 2:
                                act.wait_ge(s["qk"], ip.at(NP, p + 1))
                                copy_qk(act, ip, p)
                            if ip and p < NP and p % 2:
                                u = p // 2
                                b, kt, half = ip.slot(2), u // 2, u % 2
                                act.wait_ge(s["v"], ip.at(4, u + 1))
                                if u == 0:
                                    after(act, s["pv"], ip.at(NP, -NP))
                                act.activation(V[:, b, kt, half * 512:(half + 1) * 512], ps_j[:, :], ACT.Copy)\
                                    .then_inc(s["vc"], 1)
                    pipeline(act, B, DEPTH, 2, step)

                @block.gpsimd
                def _(pool):
                    def step(at):
                        if not at(3) and at(0):
                            ln.rstd(pool, at(0), neghalf, eps)
                        if i := at(3):
                            for p in range(NP):
                                if p == 4 and at(0):
                                    ln.rstd(pool, at(0), neghalf, eps)
                                gates.wait(pool, gates.pool, s["ex"], i.at(NP, p + 1))
                                for hh in range(2):
                                    d = pt[:, p % 4, hh, 0:3:2, :]
                                    last = pool.affine_select(out=d, in_=d, compare_op=ALU.is_ge, fill=0.0, base=0,
                                                              pattern=[[0, 2], [1, P]], channel_multiplier=-1)
                                last.then_inc(s["mk"], 1)
                        if i := at(4):
                            ln2.rstd(pool, i, neghalf, eps)
                    pipeline(pool, B, DEPTH, 2, step)

                @block.vector
                def _(dve):
                    for b in range(2):
                        dve.memset(qm[:, b, :, :, :], 0.0).then_inc(s["z"], 1)
                    dve.wait_ge(s["z"], 2)

                    def step(at):
                        i0, ix, ip, ic, io, iy = (at(k) for k in range(6))
                        if iy:
                            b = iy.slot(2)
                            ln2.ready(dve, iy)
                            ln2.apply(dve, iy, lambda j: y[:, b, j, :], lambda j: ps_y[:, j * P:(j + 1) * P], s["yn"])
                            dve.wait_ge(s["yn"], iy.at(KT, KT))
                            dve.tensor_tensor(xs[:, tiles(iy, KT), :], xs[:, tiles(iy, KT), :], y[:, b, :, :],
                                              ALU.add).then_inc(s["x"], 1)
                        if ix:
                            b = ix.slot(2)
                            dve.wait_ge(s["xh"], ix.at(1, 1))
                            dve.tensor_tensor(xl[:, b, :], ps_j[:, 0:T], xh[:, b, :], ALU.subtract)\
                                .then_inc(s["xl"], 1)
                        if io:
                            dve.wait_ge(s["pv"], io.at(NP, NP))
                            after(dve, s["rl"], io.at(1))
                            dve.reciprocal(rec[:, :], ps_sum[:, 0:T]).then_inc(s["rec"], 1)
                            dve.wait_ge(s["rec"], io.at(1, 1))
                            after(dve, s["r"], io.at(4))
                            dve.tensor_copy(rh[:, :], rec[:, :]).then_inc(s["rh"], 1)
                            dve.wait_ge(s["rh"], io.at(1, 1))
                            dve.tensor_tensor(rl[:, :], rec[:, :], rh[:, :], ALU.subtract).then_inc(s["rl"], 1)
                        for p in range(NP + 1):
                            if ip and p < NP and p % 2 == 0:
                                dve.wait_ge(s["qk"], ip.at(NP, p + 1))
                                copy_qk(dve, ip, p)
                            if io and p < NP and p % 2 == 0:
                                u = p // 2
                                dve.wait_ge(s["r"], io.at(4, u + 1))
                                after(dve, s["y"], io.at(4, u - 1))
                                dve.tensor_tensor(on[:, u % 2, :, :], ps_j[:, :].rearrange("p (n t) -> p n t", n=2),
                                                  oraw[:, io.slot(2), 2 * u:2 * u + 2, :], ALU.mult)\
                                    .then_inc(s["on"], 1)
                            if ic and p >= 4 and p % 2 == 0 or ic and p == NP:
                                for u in ([p // 2 - 2] if p < NP else [2, 3]):
                                    dve.wait_ge(s["pv"], ic.at(NP, 2 * u + 2))
                                    dve.tensor_copy(oraw[:, ic.slot(2), 2 * u:2 * u + 2, :],
                                                    ps_o[u % 2][:, :].rearrange("p (n t) -> p n t", n=2))\
                                        .then_inc(s["oc"], 1)
                            if p == 3:
                                if i0:
                                    ln.stats(dve, i0, lambda j: xs[:, i0.at(KT, j), :])
                            if p == 5 and i0:
                                b = i0.slot(2)
                                ln.ready(dve, i0)
                                after(dve, s["tp"], i0.at(1, -1))
                                ln.apply(dve, i0, lambda j: xn[:, b, j, :], lambda j: xs[:, i0.at(KT, j), :], s["xn"])
                        if io:
                            gates.wait(dve, gates.dve, s["y"], io.at(4, 4))
                            ln2.stats(dve, io, lambda j: ps_y[:, j * P:(j + 1) * P])
                    pipeline(dve, B, DEPTH, 2, step)


def layer1_experts(nc, gates, xs, ident, neghalf, router_w, w_fc, w_proj, shared_fc, shared_proj, out_dram,
                   B, T, D, NT, E, eps):
    F = w_fc.shape[1]
    NF = F // P
    NE = E + 1
    G = 4
    N = G * P
    with ExitStack() as ctx:
        sb, pb, sem = scope(nc, ctx, "moe")
        fh = sb("fh", [P, NE, F], F32R)
        fl = sb("fl", [P, NE, F], F32R)
        pT = sb("pT", [P, NE, NF, D], F32)
        rT = sb("rT", [P, E], F32)
        iota = sb("iota", [P, G, E], F32)

        with ExitStack() as c2:
            sb2, pb2, sem2 = scope(nc, c2, "moew")
            nat = sb2("nat", [P, 2, 2, NF, D], F32)
            rw = sb2("rw", [E, D], F32)
            ii = sb2("ii", [P, G, E], mybir.dt.int32)
            ps_f = [pb2(f"ps_f{i}") for i in range(2)]
            ps_p = [pb2(f"ps_p{i}") for i in range(2)]
            ps_r = pb2("ps_r")
            s_w = [sem2(f"s_w{i}") for i in range(2)]
            s_r, s_rp, s_io = sem2("s_r"), sem2("s_rp"), sem2("s_io")
            s_f, s_p, s_hi, s_lo, s_pc = (sem2(n) for n in "s_f s_p s_hi s_lo s_pc".split())
            with nc.Block() as block:
                @block.sync
                def _(sp):
                    sp.dma_start(rw[:, :], router_w).then_inc(s_r, 16)
                    for e in range(NE):
                        if e >= 2:
                            sp.wait_ge(s_p, e - 1)
                        fc, pr = (w_fc[e], w_proj[e]) if e < E else (shared_fc, shared_proj)
                        sp.dma_start(nat[:, e % 2, 0, :, :], fc.rearrange("(c p) d -> p c d", p=P))\
                            .then_inc(s_w[e % 2], 16)
                        sp.dma_start(nat[:, e % 2, 1, :, :], pr.rearrange("d (c p) -> d c p", p=P))\
                            .then_inc(s_w[e % 2], 16)

                @block.gpsimd
                def _(pool):
                    pool.iota(ii[:, :, :], [[0, G], [1, E]], base=0, channel_multiplier=0).then_inc(s_io, 1)

                @block.tensor
                def _(pe):
                    pe.wait_ge(s_r, 16)
                    pe.transpose(ps_r[:, 0:E], rw[:, :], ident[0:E, 0:E]).then_inc(s_rp, 1)
                    for e in range(NE):
                        pe.wait_ge(s_w[e % 2], 32 * (e // 2 + 1))
                        if e >= 2:
                            pe.wait_ge(s_lo, e - 1)
                            pe.wait_ge(s_pc, e - 1)
                        for ps, k, s in ((ps_f, 0, s_f), (ps_p, 1, s_p)):
                            for c in range(NF):
                                mm = pe.transpose(ps[e % 2][:, c * P:(c + 1) * P], nat[:, e % 2, k, c, :], ident[:, :])
                            mm.then_inc(s, 1)

                @block.scalar
                def _(act):
                    for e in range(NE):
                        act.wait_ge(s_f, e + 1)
                        act.activation(fh[:, e, :], ps_f[e % 2][:, :], ACT.Copy).then_inc(s_hi, 1)
                        act.wait_ge(s_p, e + 1)
                        act.activation(pT[:, e, :, :], ps_p[e % 2][:, :].rearrange("p (c d) -> p c d", c=NF),
                                       ACT.Copy).then_inc(s_pc, 1)

                @block.vector
                def _(dve):
                    dve.wait_ge(s_rp, 1)
                    dve.tensor_copy(rT[:, :], ps_r[:, 0:E])
                    dve.wait_ge(s_io, 1)
                    dve.tensor_copy(iota[:, :, :], ii[:, :, :])
                    for e in range(NE):
                        dve.wait_ge(s_hi, e + 1)
                        dve.tensor_tensor(fl[:, e, :], ps_f[e % 2][:, :], fh[:, e, :], ALU.subtract)\
                            .then_inc(s_lo, 1)

        with ExitStack() as c2:
            sb2, pb2, sem2 = scope(nc, c2, "exp")
            ln, ln2 = (Norm((sb2, sem2), f"moe_ln{k}", G, gates) for k in (1, 2))
            xn = sb2("xn", [P, 2, G, D], F32)
            x32 = sb2("x32", [P, 2, N], F32)
            xh = sb2("xh", [P, 2, N], F32R)
            xl = sb2("xl", [P, 2, N], F32R)
            r = sb2("r", [P, 2, N], F32)
            h = sb2("h", [P, 3, N], F32)
            acc = sb2("acc", [P, 2, G, D], F32)
            z = sb2("z", [P, 2, G, D], F32)
            lmax = sb2("lmax", [P, G], F32)
            lg = sb2("lg", [P, G, E], F32)
            ex = sb2("ex", [P, G, E], F32)
            esum = sb2("esum", [P, G], F32)
            erec = sb2("erec", [P, G], F32)
            pr = sb2("pr", [P, G, E], F32)
            top = sb2("top", [P, G, 8], F32)
            idx = sb2("idx", [P, G, 8], U32)
            idf = sb2("idf", [P, G, 8], F32)
            den = sb2("den", [P, G], F32)
            denm = sb2("denm", [P, G], F32)
            drec = sb2("drec", [P, G], F32)
            m0 = sb2("m0", [P, G, E], F32)
            m1 = sb2("m1", [P, G, E], F32)
            mk = sb2("mk", [P, G, E], F32)
            pw = sb2("pw", [P, G, E], F32)
            cw = sb2("cw", [P, 2, G, E], F32)
            ps_t, ps_r = pb2("ps_t"), pb2("ps_r")
            ps_h = [pb2(f"ps_h{i}") for i in range(3)]
            ps_y = [pb2(f"ps_y{i}") for i in range(2)]
            names = "xn tp x32 xh xl rt lsub lexp a r h b acc z x".split()
            s = {n: sem2(f"s_{n}") for n in names}
            s_r = sem2("s_router")
            s_out = [sem2(f"s_out{i}") for i in range(2)]
            DEPTH = 5
            CH = NE * NF

            def per_expert(ap):
                return ap.unsqueeze(2).broadcast_to([P, G, E])

            with nc.Block() as block:
                @block.tensor
                def _(pe):
                    def hidden(i, k):
                        b, e, f = i.slot(2), k // NF, k % NF
                        if k == 0:
                            pe.wait_ge(s["xl"], i.at(1, 1))
                        after(pe, s["r"], i.at(CH, k - 2))
                        c = slice(f * P, (f + 1) * P)
                        split_matmul(pe, ps_h[k % 3][:, :], (fh[:, e, c], fl[:, e, c]), (xh[:, b, :], xl[:, b, :]))\
                            .then_inc(s["a"], 1)

                    def projected(i, k):
                        e, f = k // NF, k % NF
                        pe.wait_ge(s["h"], i.at(CH, k + 1))
                        if f == 0:
                            after(pe, s["acc"], i.at(NE, e - 1))
                        bank = ps_y[(i.slot(2) * NE + e) % 2]
                        for t in range(G):
                            mm = pe.matmul(bank[:, t * P:(t + 1) * P], h[:, k % 3, t * P:(t + 1) * P], pT[:, e, f, :],
                                           start=(f == 0 and t == 0), stop=(f == NF - 1), skip_group_check=True)
                        mm.then_inc(s["b"], 1)

                    def step(at):
                        if i := at(1):
                            b = i.slot(2)
                            pe.wait_ge(s["xn"], i.at(G, G))
                            after(pe, s["x32"], i.at(1))
                            for j in range(G):
                                mm = pe.transpose(ps_t[:, j * P:(j + 1) * P], xn[:, b, j, :], ident[:, :])
                            mm.then_inc(s["tp"], 1)
                        i = at(2)
                        for k in range(CH + 2):
                            if i and k < CH:
                                hidden(i, k)
                            if k == 4 and at(1):
                                b = at(1).slot(2)
                                pe.wait_ge(s["x32"], at(1).at(1, 1))
                                after(pe, s["lsub"], at(1).at(1))
                                for j in range(G):
                                    mm = pe.matmul(ps_r[:, j * E:(j + 1) * E], x32[:, b, j * P:(j + 1) * P],
                                                   rT[:, :], start=True, stop=True)
                                mm.then_inc(s["rt"], 1)
                            if i and k >= 2:
                                projected(i, k - 2)
                    pipeline(pe, NT // G, DEPTH, 2, step)

                @block.scalar
                def _(act):
                    def step(at):
                        if i := at(1):
                            b = i.slot(2)
                            act.wait_ge(s["tp"], i.at(1, 1))
                            after(act, s["rt"], i.at(1, -1))
                            after(act, s["xl"], i.at(1, -1))
                            act.activation(x32[:, b, :], ps_t[:, :], ACT.Copy).then_inc(s["x32"], 1)
                        i = at(2)
                        for k in range(CH):
                            if i:
                                act.wait_ge(s["a"], i.at(CH, k + 1))
                                after(act, s["h"], i.at(CH, k - 1))
                                act.activation(r[:, k % 2, :], ps_h[k % 3][:, :], ACT.Relu).then_inc(s["r"], 1)
                            if k == 12 and at(1):
                                act.wait_ge(s["lsub"], at(1).at(1, 1))
                                act.activation(ex[:, :, :], lg[:, :, :], ACT.Exp).then_inc(s["lexp"], 1)
                    pipeline(act, NT // G, DEPTH, 2, step)

                @block.gpsimd
                def _(pool):
                    def step(at):
                        if i := at(0):
                            ln.rstd(pool, i, neghalf, eps)
                        if i := at(3):
                            ln2.rstd(pool, i, neghalf, eps)
                    pipeline(pool, NT // G, DEPTH, 2, step)

                @block.vector
                def _(dve):
                    def route(i):
                        n = [0]

                        def link(ins):
                            n[0] += 1
                            ins.then_inc(s_r, 1)
                            gates.wait(dve, gates.dve, s_r, i.at(ROUTE, n[0]))

                        dve.wait_ge(s["rt"], i.at(1, 1))
                        lo = ps_r[:, 0:G * E].rearrange("p (g e) -> p g e", g=G)
                        link(dve.tensor_reduce(lmax[:, :], lo, AX.X, ALU.max))
                        dve.tensor_tensor(lg[:, :, :], lo, per_expert(lmax[:, :]), ALU.subtract)\
                            .then_inc(s["lsub"], 1)
                        dve.wait_ge(s["lexp"], i.at(1, 1))
                        link(dve.tensor_reduce(esum[:, :], ex[:, :, :], AX.X, ALU.add))
                        link(dve.reciprocal(erec[:, :], esum[:, :]))
                        link(dve.tensor_tensor(pr[:, :, :], ex[:, :, :], per_expert(erec[:, :]), ALU.mult))
                        for j in range(G):
                            link(dve.max(top[:, j, :], pr[:, j, :]))
                        for j in range(G):
                            link(dve.max_index(idx[:, j, :], top[:, j, :], pr[:, j, :]))
                        link(dve.tensor_copy(idf[:, :, :], idx[:, :, :]))
                        link(dve.tensor_tensor(den[:, :], top[:, :, 0], top[:, :, 1], ALU.add))
                        link(dve.tensor_scalar(denm[:, :], den[:, :], 1e-9, None, ALU.max))
                        link(dve.reciprocal(drec[:, :], denm[:, :]))
                        link(dve.tensor_tensor(m0[:, :, :], iota[:, :, :], per_expert(idf[:, :, 0]), ALU.is_equal))
                        link(dve.tensor_tensor(m1[:, :, :], iota[:, :, :], per_expert(idf[:, :, 1]), ALU.is_equal))
                        link(dve.tensor_tensor(mk[:, :, :], m0[:, :, :], m1[:, :, :], ALU.add))
                        link(dve.tensor_tensor(pw[:, :, :], pr[:, :, :], per_expert(drec[:, :]), ALU.mult))
                        link(dve.tensor_tensor(cw[:, i.slot(2), :, :], pw[:, :, :], mk[:, :, :], ALU.mult))
                        assert n[0] == ROUTE

                    ROUTE = 13 + 2 * G

                    def weighed(i, e):
                        b = i.slot(2)
                        bank = ps_y[(i.slot(2) * NE + e) % 2]
                        dve.wait_ge(s["b"], i.at(CH, NF * (e + 1)))
                        if e:
                            dve.wait_ge(s["acc"], i.at(NE, e))
                        for t in range(G):
                            y = bank[:, t * P:(t + 1) * P]
                            a = acc[:, b, t, :]
                            if e == 0:
                                o = dve.tensor_scalar(a, y, cw[:, b, t, 0:1], None, ALU.mult)
                            elif e < E:
                                o = dve.scalar_tensor_tensor(a, y, cw[:, b, t, e:e + 1], a, ALU.mult, ALU.add)
                            else:
                                o = dve.tensor_tensor(a, y, a, ALU.add)
                        o.then_inc(s["acc"], 1)

                    def step(at):
                        if i := at(4):
                            b = i.slot(2)
                            ln2.ready(dve, i)
                            ln2.apply(dve, i, lambda j: z[:, b, j, :], lambda j: acc[:, b, j, :], s["z"])
                            dve.wait_ge(s["z"], i.at(G, G))
                            dve.tensor_tensor(xs[:, tiles(i, G), :], xs[:, tiles(i, G), :], z[:, b, :, :],
                                              ALU.add).then_inc(s["x"], 1)
                        i = at(2)
                        for k in range(CH + 2):
                            if i and k < CH:
                                dve.wait_ge(s["r"], i.at(CH, k + 1))
                                after(dve, s["b"], i.at(CH, k - 2))
                                dve.tensor_tensor(h[:, k % 3, :], r[:, k % 2, :], r[:, k % 2, :], ALU.mult)\
                                    .then_inc(s["h"], 1)
                            if k == 2 and at(1):
                                b = at(1).slot(2)
                                dve.wait_ge(s["x32"], at(1).at(1, 1))
                                after(dve, s["a"], at(1).at(CH, -CH))
                                dve.tensor_copy(xh[:, b, :], x32[:, b, :]).then_inc(s["xh"], 1)
                                dve.wait_ge(s["xh"], at(1).at(1, 1))
                                dve.tensor_tensor(xl[:, b, :], x32[:, b, :], xh[:, b, :], ALU.subtract)\
                                    .then_inc(s["xl"], 1)
                            if k == 12 and at(1):
                                route(at(1))
                            if k == 22 and at(0):
                                i0 = at(0)
                                ln.stats(dve, i0, lambda j: xs[:, i0.at(G, j), :])
                            if k == 30 and at(0):
                                b = i0.slot(2)
                                ln.ready(dve, i0)
                                after(dve, s["tp"], i0.at(1, -1))
                                ln.apply(dve, i0, lambda j: xn[:, b, j, :], lambda j: xs[:, i0.at(G, j), :], s["xn"])
                            if i and k >= NF + 1 and (k - 1) % NF == 0:
                                weighed(i, (k - 1) // NF - 1)
                        if i:
                            b = i.slot(2)
                            gates.wait(dve, gates.dve, s["acc"], i.at(NE, NE))
                        if i := at(3):
                            pass
                    def step_with_stats(at):
                        step(at)
                        if i := at(2):
                            ln2.stats(dve, i, lambda j: acc[:, i.slot(2), j, :])
                    pipeline(dve, NT // G, DEPTH, 2, step_with_stats)

                @block.sync
                def _(sp):
                    def step(at):
                        if i := at(4):
                            sp.wait_ge(s["x"], i.at(1, 1))
                            sp.dma_start(out_dram[:, tiles(i, G), :], xs[:, tiles(i, G), :])\
                                .then_inc(s_out[i.slot(2)], 16)
                    pipeline(sp, NT // G, DEPTH, 2, step)
                    for b in range(2):
                        sp.wait_ge(s_out[b], NT // G // 2 * 16)


INPUTS = ("L0_attn_x", "L0_attn_W_in", "L0_attn_A_in", "L0_attn_B_in", "L0_attn_W_out", "L0_ffn_W_r",
          "L0_ffn_W_k", "L0_ffn_W_v", "L0_ffn_mu_r", "L0_ffn_mu_k", "L1_attn_Wq", "L1_attn_Wk",
          "L1_attn_Wv", "L1_attn_Wo", "L1_ffn_router_w", "L1_ffn_w_fc", "L1_ffn_w_proj",
          "L1_ffn_shared_fc", "L1_ffn_shared_proj")


def kernel(**inputs):
    import numpy as np
    from concourse import bacc
    from concourse.bass_utils import run_bass_kernel_spmd

    nc = bacc.Bacc("TRN2", target_bir_lowering=False, num_devices=1)
    arrays, args = {}, []
    for name in INPUTS:
        a = np.ascontiguousarray(inputs[name])
        arrays[f"in_{name}"] = a
        args.append(nc.dram_tensor(f"in_{name}", a.shape, mybir.dt.from_np(a.dtype), kind="ExternalInput").ap())
    out = nc.dram_tensor("out_x", inputs["L0_attn_x"].shape, F32, kind="ExternalOutput").ap()
    program(nc, *args, out)
    r = run_bass_kernel_spmd(nc, [arrays], core_ids=[0])
    return r.results[0]["out_x"]
```

```python
from contextlib import ExitStack

import concourse.bass as bass
from concourse import mybir

F32 = mybir.dt.float32
F32R = mybir.dt.float32r
U32 = mybir.dt.uint32
ALU = mybir.AluOpType
ACT = mybir.ActivationFunctionType
AX = mybir.AxisListType
P = 128
EPS = 1e-5


class Item:

    def __init__(self, reg, const, unroll):
        self.reg, self.const, self.unroll = reg, const, unroll

    def at(self, mult=1, add=0):
        if self.reg is None:
            return mult * self.const + add
        return self.reg * (mult * self.unroll) + (mult * self.const + add)

    def slot(self, n):
        assert self.unroll % n == 0
        return self.const % n

    def turn(self, n):
        assert self.unroll % n == 0
        if self.reg is None:
            return self.const // n
        return self.reg * (self.unroll // n) + self.const // n


def after(eng, sem, value):
    if isinstance(value, int) and value <= 0:
        return
    eng.wait_ge(sem, value)


class Gates:

    def __init__(self, sem):
        self.dve, self.pool = sem("dve_gate"), sem("pool_gate")

    @staticmethod
    def wait(eng, gate, sem, value):
        eng.wait_ge(sem, value)
        if not isinstance(value, int):
            eng.sem_inc(gate, 1)


def pipeline(eng, items, depth, unroll, step):
    lead = -(-(depth + 3) // unroll) * unroll
    turns = max((items - lead) // unroll, 0)

    def plain(t):
        step(lambda s: Item(None, t - s, unroll) if 0 <= t - s < items else None)

    for t in range(lead):
        plain(t)
    if turns:
        with eng.Fori(0, turns) as g:
            for u in range(unroll):
                step(lambda s, u=u: Item(g, lead + u - s, unroll))
    for t in range(lead + turns * unroll, items + depth - 1):
        plain(t)


def tiles(item, n):
    return bass.ds(item.at(n), n)


def program(nc, x_in, W_in, A_in, B_in, W_out, W_r, W_k, W_v, mu_r, mu_k,
            Wq, Wk, Wv, Wo, router_w, w_fc, w_proj, shared_fc, shared_proj, out):
    B, T, D = x_in.shape
    NT = B * T // P
    KT = T // P
    E = router_w.shape[0]
    assert D == P and T == 2 * P

    x_dram = x_in.rearrange("b (t p) d -> p (b t) d", p=P)
    out_dram = out.rearrange("b (t p) d -> p (b t) d", p=P)

    with ExitStack() as ctx:
        xs = ctx.enter_context(nc.sbuf_tensor("xs", [P, NT, D], F32))
        ident = ctx.enter_context(nc.sbuf_tensor("ident", [P, P], F32))
        neghalf = ctx.enter_context(nc.sbuf_tensor("neghalf", [P, 4], F32))
        gates = Gates(lambda name: ctx.enter_context(nc.semaphore(name)))
        eps = EPS
        layer0(nc, gates, xs, ident, neghalf, x_dram, W_in, A_in, B_in, W_out, W_r, W_k, W_v, mu_r, mu_k,
               B, T, D, NT, KT, eps)
        layer1_attention(nc, gates, xs, ident, neghalf, Wq, Wk, Wv, Wo, B, T, D, NT, KT, eps)
        layer1_experts(nc, gates, xs, ident, neghalf, router_w, w_fc, w_proj, shared_fc, shared_proj,
                       out_dram, B, T, D, NT, E, eps)


class Norm:

    def __init__(self, alloc, name, n, gates):
        sb, sem = alloc
        self.gates = gates
        self.n = n
        self.st = sb(f"{name}_st", [P, 2, n, 6], F32)
        self.mv = sb(f"{name}_mv", [P, 2, n, 2], F32)
        self.ve = sb(f"{name}_ve", [P, 2, n], F32)
        self.rs = sb(f"{name}_rs", [P, 2, n], F32)
        self.s_stats = sem(f"{name}_stats")
        self.s_mean = sem(f"{name}_mean")
        self.s_vareps = sem(f"{name}_vareps")
        self.s_rstd = sem(f"{name}_rstd")

    def stats(self, dve, item, src):
        n, b = self.n, item.slot(2)
        for j in range(n):
            dve.bn_stats(self.st[:, b, j, :], src(j)).then_inc(self.s_stats, 1)
        self.gates.wait(dve, self.gates.dve, self.s_stats, item.at(n, n))
        for j in range(n):
            dve.bn_aggr(self.mv[:, b, j, :], self.st[:, b, j, :]).then_inc(self.s_mean, 1)

    def rstd(self, pool, item, neghalf, eps):
        n, b = self.n, item.slot(2)
        self.gates.wait(pool, self.gates.pool, self.s_mean, item.at(n, n))
        pool.tensor_scalar(self.ve[:, b, :], self.mv[:, b, :, 1], eps, None, ALU.add)\
            .then_inc(self.s_vareps, 1)
        pool.wait_ge(self.s_vareps, item.at(1, 1))
        pool.tensor_tensor(self.rs[:, b, :], self.ve[:, b, :], neghalf[:, 0:n], ALU.pow)\
            .then_inc(self.s_rstd, 1)

    def ready(self, dve, item):
        dve.wait_ge(self.s_rstd, item.at(1, 1))

    def apply(self, dve, item, dst, src, s_done):
        b = item.slot(2)
        for j in range(self.n):
            dve.tensor_scalar(dst(j), src(j), self.mv[:, b, j, 0:1], self.rs[:, b, j:j + 1],
                              ALU.subtract, ALU.mult).then_inc(s_done, 1)


def scope(nc, ctx, phase):
    def sb(name, shape, dt):
        return ctx.enter_context(nc.sbuf_tensor(f"{phase}_{name}", shape, dt))

    def pb(name):
        return ctx.enter_context(nc.psum_tensor(f"{phase}_{name}", [P, 512], F32))

    def sem(name):
        return ctx.enter_context(nc.semaphore(f"{phase}_{name}"))

    return sb, pb, sem


def layer0(nc, gates, xs, ident, neghalf, x_dram, W_in, A_in, B_in, W_out, W_r, W_k, W_v, mu_r, mu_k,
           B, T, D, NT, KT, eps):
    H = 16
    DH = D // H
    SL = 32
    HC = P // SL
    NC = H // HC
    SCALE = float(DH) ** -0.5
    LORA = 1.0 / A_in.shape[0]
    qk_dram = nc.dram_tensor("qk_planes", [B, 2, 4, P, T], F32, kind="Internal").ap()
    max_dram = nc.dram_tensor("max_parts", [4, 2 * H, T], F32, kind="Internal").ap()

    with ExitStack() as ctx:
        sb, pb, sem = scope(nc, ctx, "l0")
        WT = sb("WT", [P, 4, D], F32)
        mu = sb("mu", [P, 2], F32)
        omu = sb("omu", [P, 2], F32)
        vall = sb("vall", [P, NT, D], F32)
        aall = sb("aall", [P, NT, D], F32)

        c3 = ctx.enter_context(ExitStack())
        NBUF = 4
        sb3, _, _ = scope(nc, c3, "l0st")
        QS = [sb3(f"QS{i}", [P, H, T], F32R) for i in range(NBUF)]
        KS = [sb3(f"KS{i}", [P, NC, T], F32R) for i in range(NBUF)]
        c4 = ctx.enter_context(ExitStack())
        WeffT = scope(nc, c4, "l0q")[0]("WeffT", [P, 3 * D], F32)

        s_x0, s_x = sem("s_x_quarter"), sem("s_x_rest")

        with ExitStack() as c2:
            sb2, pb2, sem2 = scope(nc, c2, "l0w")
            w_in = sb2("w_in", [P, 3, 3 * D], F32)
            a_in = sb2("a_in", [P, 3 * D], F32)
            b_in = sb2("b_in", [P, 3, P], F32)
            w4 = sb2("w4", [P, 4, D], F32)
            bT = sb2("bT", [P, 3 * D], F32)
            cz = sb2("cz", [P, 2, T], F32)
            ps_b, ps_e, ps_w = pb2("ps_b"), pb2("ps_e"), pb2("ps_w")
            s_w = sem2("s_weights")
            s_id = sem2("s_ident")
            s_c = sem2("s_rows")
            s_cd = sem2("s_rows_stored")
            s_pe = sem2("s_transposed")
            s_bT = sem2("s_bT")
            s_done = sem2("s_copied")
            with nc.Block() as block:
                @block.sync
                def _(sp):
                    sp.dma_start(w_in[:, :, :], W_in.rearrange("(c p) n -> p c n", p=P)).then_inc(s_w, 16)
                    sp.dma_start(a_in[:, :], A_in).then_inc(s_w, 16)
                    sp.dma_start(b_in[:, :, :], B_in.rearrange("(c p) n -> p c n", p=P)).then_inc(s_w, 16)
                    for n, w in enumerate((W_out, W_r, W_k, W_v)):
                        sp.dma_start(w4[:, n, :], w).then_inc(s_w, 16)
                    for n, m in enumerate((mu_r, mu_k)):
                        sp.dma_start(mu[:, n:n + 1], m.rearrange("(d a) -> d a", a=1)).then_inc(s_w, 16)
                    for q in range(4):
                        sp.dma_start(xs[:, q * NT // 4:(q + 1) * NT // 4, :],
                                     x_dram[:, q * NT // 4:(q + 1) * NT // 4, :]).then_inc(s_x if q else s_x0, 16)

                @block.gpsimd
                def _(pool):
                    pool.memset(ident[:, :], 0.0).then_inc(s_id, 1)
                    pool.memset(neghalf[:, :], -0.5)
                    pool.wait_ge(s_id, 1)
                    pool.affine_select(out=ident[:, :], in_=ident[:, :], compare_op=ALU.not_equal,
                                       fill=1.0, base=0, pattern=[[-1, P]], channel_multiplier=1)\
                        .then_inc(s_id, 1)
                    pool.memset(cz[:, 0, :], 0.0).then_inc(s_c, 1)
                    pool.wait_ge(s_c, 1)
                    pool.affine_select(out=cz[:, 1, :], in_=cz[:, 0, :], compare_op=ALU.is_ge,
                                       fill=1.0, base=-2 * H, pattern=[[0, T]],
                                       channel_multiplier=1).then_inc(s_c, 1)

                @block.tensor
                def _(pe):
                    pe.wait_ge(s_id, 2)
                    pe.wait_ge(s_w, 9 * 16)
                    for c in range(3):
                        mm = pe.transpose(ps_b[:, c * P:(c + 1) * P], b_in[:, c, :], ident[:, :])
                    mm.then_inc(s_pe, 1)
                    for n in range(4):
                        mm = pe.transpose(ps_w[:, n * P:(n + 1) * P], w4[:, n, :], ident[:, :])
                    mm.then_inc(s_pe, 1)
                    pe.wait_ge(s_bT, 1)
                    for c in range(3):
                        o = ps_e[:, c * P:(c + 1) * P]
                        for j in range(3):
                            pe.matmul(o, w_in[:, c, j * D:(j + 1) * D], ident[:, :],
                                      start=(j == 0), stop=False)
                        for j in range(3):
                            mm = pe.matmul(o, a_in[:, j * D:(j + 1) * D], bT[:, c * P:(c + 1) * P],
                                           start=False, stop=(j == 2))
                    mm.then_inc(s_pe, 1)

                @block.scalar
                def _(act):
                    act.wait_ge(s_c, 2)
                    for a in range(2):
                        act.dma_start(qk_dram[:, a, 3, :, :].rearrange("b p t -> p b t"),
                                      cz[:, a, :].unsqueeze(1).broadcast_to([P, B, T])).then_inc(s_cd, 16)
                    act.wait_ge(s_pe, 1)
                    act.activation(bT[:, :], ps_b[:, 0:3 * D], ACT.Copy, scale=LORA).then_inc(s_bT, 1)
                    act.wait_ge(s_pe, 3)
                    for a in range(2):
                        act.activation(WeffT[:, a * D:(a + 1) * D].rearrange("p (r h) -> p r h", h=H),
                                       ps_e[:, a * D:(a + 1) * D].rearrange("p (h r) -> p r h", h=H),
                                       ACT.Copy).then_inc(s_done, 1)
                    act.activation(WeffT[:, 2 * D:3 * D], ps_e[:, 2 * D:3 * D], ACT.Copy).then_inc(s_done, 1)
                    act.wait_ge(s_cd, 32)

                @block.vector
                def _(dve):
                    dve.wait_ge(s_w, 9 * 16)
                    dve.tensor_scalar(omu[:, :], mu[:, :], -1.0, 1.0, ALU.mult, ALU.add).then_inc(s_done, 1)
                    dve.wait_ge(s_pe, 2)
                    dve.tensor_copy(WT[:, :, :], ps_w[:, :].rearrange("p (n d) -> p n d", n=4))\
                        .then_inc(s_done, 1)

        with ExitStack() as c2:
            sb2, pb2, sem2 = scope(nc, c2, "l0in")
            ln = Norm((sb2, sem2), "ln_a", KT, gates)
            xn = sb2("xn", [P, 2, KT, D], F32)
            xT = sb2("xT", [P, 2, T], F32)
            qkh = sb2("qkh", [P, 2, 2, 2, T], F32R)
            qkl = sb2("qkl", [P, 2, 2, 2, T], F32R)
            ps_t = [pb2(f"ps_t{i}") for i in range(2)]
            ps_qk = [pb2(f"ps_qk{i}") for i in range(2)]
            ps_v = [pb2(f"ps_v{i}") for i in range(2)]
            s_xn, s_tp, s_xT = sem2("s_xn"), sem2("s_tp"), sem2("s_xT")
            s_qk, s_v = sem2("s_qk"), sem2("s_v")
            s_hi, s_lo, s_vc = sem2("s_hi"), sem2("s_lo"), sem2("s_vc")
            s_st = [sem2(f"s_stored{i}") for i in range(2)]
            DEPTH = 3
            with nc.Block() as block:
                @block.vector
                def _(dve):
                    def step(at):
                        if i := at(0):
                            if i.reg is None and i.const < NT // 4 // KT:
                                dve.wait_ge(s_x0, 16)
                            else:
                                dve.wait_ge(s_x, 48)
                            ln.stats(dve, i, lambda j: xs[:, i.at(KT, j), :])
                        if i := at(1):
                            b = i.slot(2)
                            ln.ready(dve, i)
                            after(dve, s_tp, i.at(1, -1))
                            ln.apply(dve, i, lambda j: xn[:, b, j, :], lambda j: xs[:, i.at(KT, j), :], s_xn)
                        if i := at(2):
                            b = i.slot(2)
                            pair = i.slot(4) // 2
                            dve.wait_ge(s_hi, i.at(1, 1))
                            after(dve, s_st[pair], i.turn(4) * 96)
                            dve.tensor_tensor(qkl[:, pair, b, :, :], ps_qk[b][:, :].rearrange("p (a t) -> p a t", a=2),
                                              qkh[:, pair, b, :, :], ALU.subtract).then_inc(s_lo, 1)
                    pipeline(dve, B, DEPTH, 4, step)

                @block.gpsimd
                def _(pool):
                    def step(at):
                        if i := at(0):
                            ln.rstd(pool, i, neghalf, eps)
                            if i.reg is None and i.const < NBUF:
                                pool.memset(QS[i.const][:, :, :].bitcast(F32), 0.0)
                    pipeline(pool, B, DEPTH, 4, step)

                @block.tensor
                def _(pe):
                    def step(at):
                        if i := at(2):
                            b = i.slot(2)
                            pe.wait_ge(s_xT, i.at(1, 1))
                            after(pe, s_lo, i.at(1, -1))
                            for a in range(2):
                                mm = pe.matmul(ps_qk[b][:, a * T:(a + 1) * T], WeffT[:, a * D:(a + 1) * D],
                                               xT[:, b, :], start=True, stop=True)
                            mm.then_inc(s_qk, 1)
                            after(pe, s_vc, i.at(1, -1))
                            for j in range(KT):
                                mm = pe.matmul(ps_v[b][:, j * D:(j + 1) * D], xT[:, b, j * P:(j + 1) * P],
                                               WeffT[:, 2 * D:3 * D], start=True, stop=True)
                            mm.then_inc(s_v, 1)
                        if i := at(1):
                            b = i.slot(2)
                            pe.wait_ge(s_xn, i.at(KT, KT))
                            after(pe, s_xT, i.at(1, -1))
                            for j in range(KT):
                                mm = pe.transpose(ps_t[b][:, j * P:(j + 1) * P], xn[:, b, j, :], ident[:, :])
                            mm.then_inc(s_tp, 1)
                    pipeline(pe, B, DEPTH, 4, step)

                @block.scalar
                def _(act):
                    def step(at):
                        if i := at(2):
                            b = i.slot(2)
                            pair = i.slot(4) // 2
                            act.wait_ge(s_qk, i.at(1, 1))
                            after(act, s_st[pair], i.turn(4) * 96)
                            act.activation(qkh[:, pair, b, :, :], ps_qk[b][:, :].rearrange("p (a t) -> p a t", a=2),
                                           ACT.Copy).then_inc(s_hi, 1)
                            act.wait_ge(s_v, i.at(1, 1))
                            act.activation(vall[:, tiles(i, KT), :],
                                           ps_v[b][:, 0:T].rearrange("p (t d) -> p t d", t=KT), ACT.Copy)\
                                .then_inc(s_vc, 1)
                        if i := at(1):
                            b = i.slot(2)
                            act.wait_ge(s_tp, i.at(1, 1))
                            after(act, s_v, i.at(1, -1))
                            act.activation(xT[:, b, :], ps_t[b][:, 0:T], ACT.Copy).then_inc(s_xT, 1)
                    pipeline(act, B, DEPTH, 4, step)

                @block.sync
                def _(sp):
                    def step(at):
                        if (i := at(2)) and i.slot(2) == 1:
                            pair = i.slot(4) // 2
                            for part, s, planes in ((qkh, s_hi, ((0, 0), (0, 2), (1, 1), (1, 2))),
                                                    (qkl, s_lo, ((0, 1), (1, 0)))):
                                sp.wait_ge(s, i.at(1, 1))
                                for a, plane in planes:
                                    sp.dma_start(qk_dram[bass.ds(i.at(1, -1), 2), a, plane, :, :]
                                                 .rearrange("o p t -> p o t"),
                                                 part[:, pair, :, a, :].bitcast(F32)).then_inc(s_st[pair], 16)
                    pipeline(sp, B, DEPTH, 4, step)
                    for b in range(2):
                        sp.wait_ge(s_st[b], B // 4 * 96)

        c4.close()

        with ExitStack() as c2:
            sb2, pb2, sem2 = scope(nc, c2, "l0att")
            V0 = sb2("V0", [P, 2, KT, H, SL], F32)
            NPT = 3
            PT = sb2("PT", [P, NPT, HC, T], F32)
            OT = sb2("OT", [P, NC, T], F32)
            nmax = sb2("nmax", [P, KT, H], F32)
            mparts = sb2("mparts", [P, 2, KT, 2, H], F32R)
            mT = sb2("mT", [2 * H, 2, T], F32)
            rsum = sb2("rsum", [P, 2, H], F32)
            ps_a = [pb2(f"ps_a{i}") for i in range(2)]
            ps_s = [c2.enter_context(nc.psum_tensor(f"l0att_ps_s{i}", [P, HC, T], F32)) for i in range(2)]
            ps_o, ps_x = pb2("ps_o"), pb2("ps_x")
            s_ld = [sem2(f"s_loaded{i}") for i in range(NBUF)]
            s_mr = [sem2(f"s_maxrows{i}") for i in range(NBUF)]
            s_md = sem2("s_maxstored")
            s_a, s_mx, s_mp = sem2("s_passA"), sem2("s_max"), sem2("s_maxparts")
            s_mtp, s_mT = sem2("s_maxT_ps"), sem2("s_maxT")
            s_s, s_e, s_pv, s_oc = sem2("s_scores"), sem2("s_exp"), sem2("s_pv"), sem2("s_ocopied")
            s_v0 = sem2("s_v0")
            s_ot, s_rc, s_n = sem2("s_otT"), sem2("s_recip"), sem2("s_normed")
            STEPS = NC * KT
            LOADS = 2 * HC * 16
            DEPTH = 5
            with nc.Block() as block:
                @block.sync
                def _(sp):
                    def step(at):
                        if i := at(0):
                            b = i.slot(NBUF)
                            after(sp, s_s, i.at(STEPS, -(NBUF - 1) * STEPS))
                            for j in range(HC):
                                for a, dst in enumerate((QS[b][SL * j:SL * (j + 1), j:H:HC, :],
                                                         KS[b][SL * j:SL * (j + 1)])):
                                    src = qk_dram[bass.ds(i.at(), 1), a, :, :, :]\
                                        .rearrange("o g (r c j) t -> j (o g r) c t", r=DH, j=HC)[j]
                                    sp.dma_start(dst.bitcast(F32), src).then_inc(s_ld[b], 16)
                        if i := at(2):
                            b = i.slot(NBUF)
                            sp.wait_ge(s_mT, i.at(1, 1))
                            sp.dma_start(max_dram[b], mT[:, i.slot(2), :]).then_inc(s_md, 16)
                            sp.wait_ge(s_md, i.at(16, 16))
                            for j in range(HC):
                                row = SL * j + 3 * DH
                                sp.dma_start(QS[b][row:row + 2, j:H:HC, :].bitcast(F32),
                                             max_dram[b].rearrange("(l c j) t -> j l c t", l=2, j=HC)[j])\
                                    .then_inc(s_mr[b], 16)
                    pipeline(sp, B, DEPTH, NBUF, step)

                @block.gpsimd
                def _(pool):
                    pool.memset(V0[:, :, :, :, DH + 1:SL], 0.0)
                    pool.memset(V0[:, :, :, :, DH:DH + 1], 1.0)

                    def step(at):
                        if i := at(2):
                            b = i.slot(2)
                            after(pool, s_pv, i.at(STEPS, -STEPS))
                            pool.tensor_copy(V0[:, b, :, :, 0:DH],
                                             vall[:, tiles(i, KT), :].rearrange("p t (h d) -> p t h d", h=H))\
                                .then_inc(s_v0, 1)
                    pipeline(pool, B, DEPTH, NBUF, step)

                @block.tensor
                def _(pe):
                    def pass_a(i, k):
                        t, h = k // 8, 2 * (k % 8)
                        b = i.slot(NBUF)
                        after(pe, s_mx, i.at(16, k - 1))
                        for n in range(2):
                            mm = pe.matmul(ps_a[k % 2][:, n * T:(n + 1) * T], QS[b][:, h + n, t * P:(t + 1) * P],
                                           KS[b][:, (h + n) // HC, :], start=True, stop=True)
                        mm.then_inc(s_a, 1)

                    def scores(i, s):
                        c, kt = s // KT, s % KT
                        b = i.slot(NBUF)
                        after(pe, s_e, i.at(STEPS, s - 1))
                        for n in range(2):
                            mm = pe.matmul(ps_s[s % 2][:, 2 * n:2 * n + 2, :], KS[b][:, c, kt * P:(kt + 1) * P],
                                           QS[b][:, HC * c + 2 * n:HC * c + 2 * n + 2, :], start=True, stop=True)
                        mm.then_inc(s_s, 1)

                    def pv(i, s):
                        c, kt = s // KT, s % KT
                        pe.wait_ge(s_e, i.at(STEPS, s + 1))
                        if s == 0:
                            pe.wait_ge(s_v0, i.at(1, 1))
                        if s % 4 == 0:
                            after(pe, s_oc, i.at(2, s // 4))
                        for j in range(HC):
                            mm = pe.matmul(ps_o[SL * j:SL * (j + 1), (c % 2) * T:(c % 2 + 1) * T],
                                           V0[:, i.slot(2), kt, HC * c + j, :], PT[:, s % NPT, j, :],
                                           start=(kt == 0), stop=(kt == KT - 1))
                        mm.then_inc(s_pv, 1)

                    def max_transposed(i):
                        pe.wait_ge(s_mp, i.at(2, 2))
                        after(pe, s_n, i.at(KT, -2 * KT))
                        for t in range(KT):
                            mm = pe.transpose(ps_x[0:2 * H, t * P:(t + 1) * P],
                                              mparts[:, i.slot(2), t, :, :].bitcast(F32).rearrange("p l h -> p (l h)"),
                                              ident[:, :])
                        mm.then_inc(s_mtp, 1)

                    def out_transposed(i, t, other):
                        if t == 0:
                            pe.wait_ge(s_oc, i.at(2, 2))
                            if other:
                                pe.wait_ge(s_mT, other.at(1, 1))
                        after(pe, s_n, i.at(KT, t))
                        for c in range(NC):
                            mm = pe.transpose(ps_x[:, c * P:(c + 1) * P], OT[:, c, t * P:(t + 1) * P],
                                              ident[:, :])
                        mm.then_inc(s_ot, 1)

                    def step(at):
                        ia, im, ib, io = at(1), at(2), at(3), at(4)
                        if ia:
                            b = ia.slot(NBUF)
                            pe.wait_ge(s_ld[b], ia.turn(NBUF) * LOADS + LOADS)
                        if ib:
                            b = ib.slot(NBUF)
                            pe.wait_ge(s_mr[b], ib.turn(NBUF) * 64 + 64)
                        for s in range(STEPS):
                            if ia:
                                pass_a(ia, 2 * s)
                            if ib:
                                scores(ib, s)
                            if ia:
                                pass_a(ia, 2 * s + 1)
                            if ib and s >= 2:
                                pv(ib, s - 2)
                            elif io and s < 2:
                                pv(io, STEPS - 2 + s)
                            if im and s == 0:
                                max_transposed(im)
                            if io and s in (3, 5):
                                out_transposed(io, (s - 3) // 2, im if s == 3 else None)
                    pipeline(pe, B, DEPTH, NBUF, step)

                @block.scalar
                def _(act):
                    def o_copied(i, n):
                        act.wait_ge(s_pv, i.at(STEPS, 4 * n + 4))
                        if n == 0:
                            after(act, s_ot, i.at(KT))
                        act.activation(OT[:, 2 * n:2 * n + 2, :],
                                       ps_o[:, :].rearrange("p (c t) -> p c t", c=2), ACT.Copy)\
                            .then_inc(s_oc, 1)

                    def step(at):
                        im, ib, io = at(2), at(3), at(4)
                        if im:
                            act.wait_ge(s_mtp, im.at(1, 1))
                            after(act, s_md, im.at(16, -16))
                            act.activation(mT[:, im.slot(2), :], ps_x[0:2 * H, 0:T], ACT.Copy).then_inc(s_mT, 1)
                        for s in range(STEPS):
                            if ib:
                                act.wait_ge(s_s, ib.at(STEPS, s + 1))
                                after(act, s_pv, ib.at(STEPS, s - 1 if s < 2 else s - NPT + 1))
                                act.activation(PT[:, s % NPT, :, :], ps_s[s % 2][:, :, :], ACT.Exp, scale=SCALE)\
                                    .then_inc(s_e, 1)
                            if ib and s == 5:
                                o_copied(ib, 0)
                            if io and s == 1:
                                o_copied(io, 1)
                    pipeline(act, B, DEPTH, NBUF, step)

                @block.vector
                def _(dve):
                    def normalise(i, t):
                        dve.wait_ge(s_ot, i.at(KT, t + 1))
                        o = ps_x[:, :].rearrange("p (h s) -> p h s", h=H)
                        dve.reciprocal(rsum[:, t, :], o[:, :, DH]).then_inc(s_rc, 1)
                        dve.wait_ge(s_rc, i.at(KT, t + 1))
                        dst = aall[:, bass.ds(i.at(KT, t), 1), :].rearrange("p o (h d) -> p (o h) d", h=H)
                        dve.tensor_tensor(dst, o[:, :, 0:DH],
                                          rsum[:, t, :].unsqueeze(2).broadcast_to([P, H, DH]),
                                          ALU.mult).then_inc(s_n, 1)

                    def step(at):
                        ia, io = at(1), at(4)
                        for k in range(2 * STEPS):
                            if ia:
                                t, h = k // 8, 2 * (k % 8)
                                dve.wait_ge(s_a, ia.at(16, k + 1))
                                if k == 0:
                                    after(dve, s_mp, ia.at(2))
                                dve.tensor_reduce(nmax[:, t, h:h + 2], ps_a[k % 2][:, :].rearrange("p (n t) -> p n t", n=2),
                                                  AX.X, ALU.max, negate=True).then_inc(s_mx, 1)
                            if io and k in (7, 11):
                                normalise(io, (k - 7) // 4)
                        if ia:
                            b = ia.slot(2)
                            dve.wait_ge(s_mx, ia.at(16, 16))
                            after(dve, s_mtp, ia.at(1, -1))
                            dve.tensor_copy(mparts[:, b, :, 0, :], nmax[:, :, :]).then_inc(s_mp, 1)
                            dve.wait_ge(s_mp, ia.at(2, 1))
                            dve.tensor_tensor(mparts[:, b, :, 1, :], nmax[:, :, :], mparts[:, b, :, 0, :],
                                              ALU.subtract).then_inc(s_mp, 1)
                    pipeline(dve, B, DEPTH, NBUF, step)

        c3.close()

        with ExitStack() as c2:
            sb2, pb2, sem2 = scope(nc, c2, "l0mix")
            G = 2 * KT
            N = G * P
            ln1, ln2, ln3 = (Norm((sb2, sem2), f"ln_c{k}", G, gates) for k in (1, 2, 3))
            an = sb2("an", [P, 2, G, D], F32)
            aT = sb2("aT", [P, 2, N], F32)
            y = sb2("y", [P, 2, G, D], F32)
            xn = sb2("xn", [P, 2, G, D], F32)
            xT = sb2("xT", [P, 2, 2, T + 1], F32)
            prev = sb2("prev", [P, 2, 2, N], F32)
            mix = sb2("mix", [P, 2, 2, N], F32)
            kr = sb2("kr", [P, 2, N], F32)
            k2 = sb2("k2", [P, 2, N], F32)
            sg = sb2("sg", [P, 2, G, D], F32)
            f = sb2("f", [P, 2, G, D], F32)
            ps_at = pb2("ps_at")
            ps_y = [pb2(f"ps_y{i}") for i in range(2)]
            ps_xt, ps_k, ps_r = pb2("ps_xt"), pb2("ps_k"), pb2("ps_r")
            ps_kv = [pb2(f"ps_kv{i}") for i in range(2)]
            names = "an at aT y yn x1 xn tp xT pv mix k r kr k2 sg kv f fn x2".split()
            s = {n: sem2(f"s_{n}") for n in names}
            s_z = sem2("s_z")
            DEPTH = 8

            def g3(ap):
                return ap.rearrange("p (g d) -> p g d", g=G)

            with nc.Block() as block:
                @block.tensor
                def _(pe):
                    def step(at):
                        if i := at(4):
                            b = i.slot(2)
                            pe.wait_ge(s["mix"], i.at(2, 2))
                            after(pe, s["kr"], i.at(1))
                            pe.matmul(ps_k[:, :], WT[:, 2, :], mix[:, b, 1, :], start=True, stop=True)\
                                .then_inc(s["k"], 1)
                            after(pe, s["sg"], i.at(1))
                            for j in range(G):
                                mm = pe.matmul(ps_r[:, j * P:(j + 1) * P], mix[:, b, 0, j * P:(j + 1) * P],
                                               WT[:, 1, :], start=True, stop=True)
                            mm.then_inc(s["r"], 1)
                        if i := at(5):
                            b = i.slot(2)
                            pe.wait_ge(s["k2"], i.at(1, 1))
                            after(pe, s["f"], i.at(1, -1))
                            for j in range(G):
                                mm = pe.matmul(ps_kv[b][:, j * P:(j + 1) * P], k2[:, b, j * P:(j + 1) * P],
                                               WT[:, 3, :], start=True, stop=True)
                            mm.then_inc(s["kv"], 1)
                        if i := at(3):
                            b = i.slot(2)
                            pe.wait_ge(s["xn"], i.at(G, G))
                            after(pe, s["xT"], i.at(1))
                            for j in range(G):
                                mm = pe.transpose(ps_xt[:, j * P:(j + 1) * P], xn[:, b, j, :], ident[:, :])
                            mm.then_inc(s["tp"], 1)
                        if i := at(1):
                            b = i.slot(2)
                            pe.wait_ge(s["aT"], i.at(1, 1))
                            after(pe, s["yn"], i.at(G, -G))
                            for j in range(G):
                                mm = pe.matmul(ps_y[b][:, j * P:(j + 1) * P], aT[:, b, j * P:(j + 1) * P],
                                               WT[:, 0, :], start=True, stop=True)
                            mm.then_inc(s["y"], 1)
                        if i := at(0):
                            pe.wait_ge(s["an"], i.at(1, 1))
                            after(pe, s["aT"], i.at(1))
                            for j in range(G):
                                mm = pe.transpose(ps_at[:, j * P:(j + 1) * P],
                                                  an[:, i.slot(2), j, :], ident[:, :])
                            mm.then_inc(s["at"], 1)
                    pipeline(pe, NT // G, DEPTH, 2, step)

                @block.scalar
                def _(act):
                    def step(at):
                        if i := at(4):
                            b = i.slot(2)
                            act.wait_ge(s["k"], i.at(1, 1))
                            after(act, s["k2"], i.at(1, -1))
                            act.activation(kr[:, b, :], ps_k[:, :], ACT.Relu).then_inc(s["kr"], 1)
                            act.wait_ge(s["r"], i.at(1, 1))
                            after(act, s["f"], i.at(1, -1))
                            act.activation(sg[:, b, :, :], g3(ps_r[:, :]), ACT.Sigmoid).then_inc(s["sg"], 1)
                        if i := at(3):
                            b = i.slot(2)
                            act.wait_ge(s["tp"], i.at(1, 1))
                            after(act, s["mix"], i.at(2, -2))
                            act.activation(xT[:, b, :, 1:T + 1], ps_xt[:, :].rearrange("p (c t) -> p c t", c=2),
                                           ACT.Copy).then_inc(s["xT"], 1)
                        if i := at(0):
                            b = i.slot(2)
                            act.wait_ge(s["at"], i.at(1, 1))
                            after(act, s["y"], i.at(1, -1))
                            act.activation(aT[:, b, :], ps_at[:, :], ACT.Copy).then_inc(s["aT"], 1)
                    pipeline(act, NT // G, DEPTH, 2, step)

                @block.gpsimd
                def _(pool):
                    def step(at):
                        if i := at(0):
                            after(pool, s["at"], i.at(1, -1))
                            pool.tensor_copy(an[:, i.slot(2), :, :], aall[:, tiles(i, G), :]).then_inc(s["an"], 1)
                        if i := at(6):
                            ln3.rstd(pool, i, neghalf, eps)
                        if i := at(3):
                            b = i.slot(2)
                            after(pool, s["mix"], i.at(2, -2))
                            gates.wait(pool, gates.pool, s["xT"], i.at(1, 1))
                            for n in range(2):
                                pool.tensor_scalar(prev[:, b, n, :].rearrange("p (c t) -> p c t", c=2),
                                                   xT[:, b, :, 0:T], omu[:, n:n + 1], None, ALU.mult)\
                                    .then_inc(s["pv"], 1)
                        if i := at(2):
                            ln2.rstd(pool, i, neghalf, eps)
                        if i := at(1):
                            ln1.rstd(pool, i, neghalf, eps)
                    pool.memset(xT[:, :, :, 0:1], 0.0)
                    pipeline(pool, NT // G, DEPTH, 2, step)

                @block.vector
                def _(dve):
                    def step(at):
                        if i := at(6):
                            b = i.slot(2)
                            dve.wait_ge(s["kv"], i.at(1, 1))
                            dve.wait_ge(s["sg"], i.at(1, 1))
                            dve.tensor_tensor(f[:, b, :, :], g3(ps_kv[b][:, :]), sg[:, b, :, :], ALU.mult)\
                                .then_inc(s["f"], 1)
                        if i := at(4):
                            b = i.slot(2)
                            dve.wait_ge(s["pv"], i.at(2, 2))
                            after(dve, s["r"], i.at(1, -1))
                            for n in range(2):
                                dve.scalar_tensor_tensor(mix[:, b, n, :].rearrange("p (c t) -> p c t", c=2),
                                                         xT[:, b, :, 1:T + 1], mu[:, n:n + 1],
                                                         prev[:, b, n, :].rearrange("p (c t) -> p c t", c=2),
                                                         ALU.mult, ALU.add).then_inc(s["mix"], 1)
                        if i := at(5):
                            b = i.slot(2)
                            dve.wait_ge(s["kr"], i.at(1, 1))
                            after(dve, s["kv"], i.at(1, -1))
                            dve.tensor_tensor(k2[:, b, :], kr[:, b, :], kr[:, b, :], ALU.mult)\
                                .then_inc(s["k2"], 1)
                        if i := at(6):
                            gates.wait(dve, gates.dve, s["f"], i.at(1, 1))
                            ln3.stats(dve, i, lambda j: f[:, i.slot(2), j, :])
                        if i := at(3):
                            b = i.slot(2)
                            ln2.ready(dve, i)
                            after(dve, s["tp"], i.at(1, -1))
                            ln2.apply(dve, i, lambda j: xn[:, b, j, :], lambda j: xs[:, i.at(G, j), :], s["xn"])
                        if i := at(7):
                            b = i.slot(2)
                            ln3.ready(dve, i)
                            ln3.apply(dve, i, lambda j: y[:, b, j, :], lambda j: f[:, b, j, :], s["fn"])
                            dve.wait_ge(s["fn"], i.at(G, G))
                            dve.tensor_tensor(xs[:, tiles(i, G), :], xs[:, tiles(i, G), :], y[:, b, :, :],
                                              ALU.add).then_inc(s["x2"], 1)
                        if i := at(2):
                            b = i.slot(2)
                            ln1.ready(dve, i)
                            ln1.apply(dve, i, lambda j: y[:, b, j, :], lambda j: ps_y[b][:, j * P:(j + 1) * P],
                                      s["yn"])
                            dve.wait_ge(s["yn"], i.at(G, G))
                            dve.tensor_tensor(xs[:, tiles(i, G), :], xs[:, tiles(i, G), :], y[:, b, :, :],
                                              ALU.add).then_inc(s["x1"], 1)
                            gates.wait(dve, gates.dve, s["x1"], i.at(1, 1))
                            ln2.stats(dve, i, lambda j: xs[:, i.at(G, j), :])
                        if i := at(1):
                            b = i.slot(2)
                            gates.wait(dve, gates.dve, s["y"], i.at(1, 1))
                            ln1.stats(dve, i, lambda j: ps_y[b][:, j * P:(j + 1) * P])
                    pipeline(dve, NT // G, DEPTH, 2, step)


def split_matmul(pe, out, w, x, start=True, stop=True):
    pe.matmul(out, w[0], x[0], start=start, stop=False)
    pe.matmul(out, w[0], x[1], start=False, stop=False)
    return pe.matmul(out, w[1], x[0], start=False, stop=stop)


def layer1_attention(nc, gates, xs, ident, neghalf, Wq, Wk, Wv, Wo, B, T, D, NT, KT, eps):
    H = 16
    F = Wq.shape[0]
    DH = F // H
    NP = H // 2
    CLAMP = 50.0
    SCALE = float(DH) ** -0.5
    W0, W = 2 * T, 2 * T + 2 * P
    with ExitStack() as ctx:
        sb, pb, sem = scope(nc, ctx, "l1")
        mh = sb("mh", [P, H, D], F32R)
        ml = sb("ml", [P, H, D], F32R)
        vh = sb("vh", [P, F], F32R)
        vl = sb("vl", [P, F], F32R)
        woT = sb("woT", [P, NP, D], F32)
        cols = sb("cols", [P, 4, 32], F32)
        sel = sb("sel", [P, NP, P], F32R)

        with ExitStack() as c2:
            sb2, pb2, sem2 = scope(nc, c2, "l1w")
            natq = sb2("natq", [DH, H, D], F32)
            natk = sb2("natk", [DH, H, D], F32)
            natv = sb2("natv", [P, NP, D], F32)
            wo = sb2("wo", [P, F], F32)
            self32 = sb2("self32", [P, NP, P], F32)
            ps = [pb2(f"ps{i}") for i in range(4)]
            s_w, s_pe, s_hi, s_lo = sem2("s_w"), sem2("s_pe"), sem2("s_hi"), sem2("s_lo")
            s_c, s_sel = sem2("s_c"), sem2("s_sel")
            GM = H // 4
            GV = NP // 4

            def parts(g):
                if g < GM:
                    return tuple(w[:, 4 * g:4 * g + 4, :].rearrange("p n d -> p (n d)") for w in (mh, ml))
                c = 512 * (g - GM)
                return vh[:, c:c + 512], vl[:, c:c + 512]

            with nc.Block() as block:
                @block.sync
                def _(sp):
                    for w, nat in ((Wq, natq), (Wk, natk)):
                        sp.dma_start(nat[:, :, :], w.rearrange("(h r) d -> r h d", r=DH)).then_inc(s_w, 16)
                    sp.dma_start(natv[:, :, :], Wv.rearrange("(c p) d -> p c d", p=P)).then_inc(s_w, 16)
                    sp.dma_start(wo[:, :], Wo).then_inc(s_w, 16)
                    sp.wait_ge(s_w, 64)

                @block.gpsimd
                def _(pool):
                    pool.memset(cols[:, :, 0:4], 0.0).then_inc(s_c, 1)
                    pool.memset(cols[:, :, 4:32], 1.0)
                    pool.memset(self32[:, :, :], 0.0).then_inc(s_c, 1)
                    pool.wait_ge(s_c, 2)
                    for c in range(4):
                        pool.memset(cols[:, c, c:c + 1], 1.0)
                    for h in range(H):
                        o = self32[:, h // 2, (h % 2) * DH:(h % 2 + 1) * DH]
                        last = pool.affine_select(out=o, in_=o, compare_op=ALU.not_equal, fill=1.0,
                                                  base=-(32 * (h % 4) + h // 4), pattern=[[0, DH]],
                                                  channel_multiplier=1)
                    last.then_inc(s_sel, 1)

                @block.tensor
                def _(pe):
                    pe.wait_ge(s_w, 64)
                    for g in range(GM + 2 * GV):
                        if g >= 4:
                            pe.wait_ge(s_lo, g - 3)
                        for n in range(4):
                            o = ps[g % 4][:, n * P:(n + 1) * P]
                            c = 4 * (g - GM) + n
                            if g < GM:
                                mm = pe.matmul(o, natq[:, 4 * g + n, :], natk[:, 4 * g + n, :], start=True, stop=True)
                            elif g < GM + GV:
                                mm = pe.transpose(o, natv[:, c, :], ident[:, :])
                            else:
                                mm = pe.transpose(o, wo[:, (c - NP) * P:(c - NP + 1) * P], ident[:, :])
                        mm.then_inc(s_pe, 1)

                @block.scalar
                def _(act):
                    for g in range(GM + GV):
                        act.wait_ge(s_pe, g + 1)
                        act.activation(parts(g)[0], ps[g % 4][:, :], ACT.Copy).then_inc(s_hi, 1)

                @block.vector
                def _(dve):
                    for g in range(GM + GV):
                        dve.wait_ge(s_hi, g + 1)
                        dve.tensor_tensor(parts(g)[1], ps[g % 4][:, :], parts(g)[0],
                                          ALU.subtract).then_inc(s_lo, 1)
                    for g in range(GV):
                        dve.wait_ge(s_pe, GM + GV + g + 1)
                        dve.tensor_copy(woT[:, 4 * g:4 * g + 4, :],
                                        ps[(GM + GV + g) % 4][:, :].rearrange("p (n d) -> p n d", n=4))
                    dve.wait_ge(s_sel, 1)
                    dve.tensor_copy(sel[:, :, :], self32[:, :, :])

        with ExitStack() as c2:
            sb2, pb2, sem2 = scope(nc, c2, "l1att")
            ln = Norm((sb2, sem2), "l1_ln", KT, gates)
            ln2 = Norm((sb2, sem2), "l1_ln2", KT, gates)
            xn = sb2("xn", [P, 2, KT, D], F32)
            xh = sb2("xh", [P, 3, T], F32R)
            xl = sb2("xl", [P, 3, T], F32R)
            tH = sb2("tH", [P, NP, 2, T], F32R)
            tL = sb2("tL", [P, NP, 2, T], F32R)
            V = sb2("V", [P, 2, KT, F], F32)
            th = sb2("th", [P, 2, W], F32)
            pt = sb2("pt", [P, 4, W], F32)
            both = sb2("both", [P, 2, 2, P], F32)
            oraw = sb2("oraw", [P, 2, NP, T], F32)
            on = sb2("on", [P, 2, 2, T], F32)
            sums = sb2("sums", [P, T], F32)
            rec = sb2("rec", [P, 2, T], F32)
            rh = sb2("rh", [P, 2, T], F32R)
            rl = sb2("rl", [P, 2, T], F32R)
            y = sb2("y", [P, 2, KT, D], F32)
            z = sb2("z", [P, 2, KT, D], F32)
            ps_s = c2.enter_context(nc.psum_tensor("l1att_ps_s", [P, 1024], F32))
            ps_t, ps_j = pb2("ps_t"), pb2("ps_j")
            ps_o = [pb2(f"ps_o{i}") for i in range(2)]
            ps_sum, ps_y = pb2("ps_sum"), pb2("ps_y")
            names = "xn tp xh xl t tH tL v vc sc th ex mk ad pv oc sum rec rh rl r on y yc yn x".split()
            s = {n: sem2(f"s_{n}") for n in names}
            DEPTH = 7
            UNROLL = 6

            with nc.Block() as block:
                @block.tensor
                def _(pe):
                    def scores(i, p):
                        b = i.slot(3)
                        after(pe, s["th"], i.at(NP, p))
                        if p == 0:
                            pe.wait_ge(s["tL"], i.at(NP, NP))
                        split_matmul(pe, ps_s[:, 0:W0], (xh[:, b, 0:P], xl[:, b, 0:P]),
                                     (tH[:, p, :, :], tL[:, p, :, :]))
                        split_matmul(pe, ps_s[:, W0:W], (xh[:, b, P:T], xl[:, b, P:T]),
                                     (tH[:, p, :, P:T], tL[:, p, :, P:T])).then_inc(s["sc"], 1)

                    def project(i, p):
                        b = i.slot(3)
                        if p == 0:
                            pe.wait_ge(s["xl"], i.at(1, 1))
                        after(pe, s["tL"], i.at(NP, p))
                        for hh in range(2):
                            mm = split_matmul(pe, ps_t[:, hh * T:(hh + 1) * T],
                                              (mh[:, 2 * p + hh, :], ml[:, 2 * p + hh, :]),
                                              (xh[:, b, :], xl[:, b, :]))
                        mm.then_inc(s["t"], 1)

                    def values(i, u, io):
                        b, kt, half = i.slot(3), u // 2, u % 2
                        if io:
                            pe.wait_ge(s["on"], io.at(4, u + 1))
                        elif u:
                            pe.wait_ge(s["vc"], i.at(4, u))
                        else:
                            pe.wait_ge(s["xl"], i.at(1, 2))
                        c = slice(kt * P, (kt + 1) * P)
                        f = slice(half * 512, (half + 1) * 512)
                        split_matmul(pe, ps_j[:, :], (xh[:, b, c], xl[:, b, c]), (vh[:, f], vl[:, f]))\
                            .then_inc(s["v"], 1)

                    def spread(i, u, ip, ix):
                        if u == 0:
                            pe.wait_ge(s["rl"], i.at(1, 1))
                            if ix:
                                pe.wait_ge(s["xl"], ix.at(1, 1))
                            else:
                                pe.wait_ge(s["vc"], min(i.at(4, 12), 4 * B))
                        if not ix or not ip:
                            after(pe, s["on"], i.at(4, u))
                        if ip and u:
                            pe.wait_ge(s["vc"], ip.at(4, u))
                        for n in range(2):
                            o = ps_j[:, n * T:(n + 1) * T]
                            pe.matmul(o, sel[:, 2 * u + n, :], rh[:, i.slot(2), :], start=True, stop=False)
                            mm = pe.matmul(o, sel[:, 2 * u + n, :], rl[:, i.slot(2), :], start=False, stop=True)
                        mm.then_inc(s["r"], 1)

                    def project_out(i, u):
                        pe.wait_ge(s["on"], i.at(4, u + 1))
                        if u == 0:
                            after(pe, s["yc"], i.at(1))
                        for n in range(2):
                            for t in range(KT):
                                mm = pe.matmul(ps_y[:, t * P:(t + 1) * P], on[:, u % 2, n, t * P:(t + 1) * P],
                                               woT[:, 2 * u + n, :], start=(u == 0 and n == 0 and t == 0),
                                               stop=(u == 3 and n == 1), skip_group_check=True)
                        mm.then_inc(s["y"], 1)

                    def pv(i, p):
                        b = i.slot(2)
                        pe.wait_ge(s["mk"], i.at(NP, p + 1))
                        if p % 2 == 0:
                            after(pe, s["oc"], i.at(4, p // 2 - 1))
                        if p == 0:
                            pe.wait_ge(s["vc"], i.at(4, 4))
                        o, c = ps_o[p // 2 % 2], p % 2 * T

                        def probs(kt, hh):
                            at, n = (hh * T, T) if kt == 0 else (W0 + hh * P, P)
                            return pt[:, p % 4, at:at + n]

                        for kt in range(KT):
                            for hh in range(2):
                                h = 2 * p + hh
                                pe.matmul(o[hh * DH:(hh + 1) * DH, c + kt * P:c + T], V[:, b, kt, h * DH:(h + 1) * DH],
                                          probs(kt, hh), start=(kt == 0), stop=(kt == 1), skip_group_check=True)

                    def probability_sums(i, p):
                        pe.wait_ge(s["ad"], i.at(NP, p + 1))
                        if p == 0:
                            after(pe, s["sum"], i.at(1))
                        for hh in range(2):
                            h = 2 * p + hh
                            j = 32 * (h % 4)
                            for half, m in enumerate((pt[:, p % 4, hh * T:hh * T + P], both[:, p % 2, hh, :])):
                                mm = pe.matmul(ps_sum[j:j + 32, half * P:(half + 1) * P], cols[:, h // 4, :], m,
                                               start=(h < 4 and half == 0), stop=(h >= 12),
                                               skip_group_check=True)
                        mm.then_inc(s["pv"], 1)

                    def turned(i):
                        pe.wait_ge(s["xn"], i.at(KT, KT))
                        after(pe, s["vc"], i.at(4, -4))
                        for j in range(KT):
                            mm = pe.transpose(ps_j[:, j * P:(j + 1) * P], xn[:, i.slot(2), j, :], ident[:, :])
                        mm.then_inc(s["tp"], 1)

                    def step(at):
                        ix, ip, ic, il, io = at(1), at(2), at(3), at(4), at(5)
                        if ix:
                            turned(ix)
                        for p in range(NP):
                            if ic:
                                scores(ic, p)
                            if ic and p >= 2:
                                pv(ic, p - 2)
                            if il and p < 2:
                                pv(il, NP - 2 + p)
                            if ip:
                                project(ip, p)
                            if ic and p >= 2:
                                probability_sums(ic, p - 2)
                            if il and p < 2:
                                probability_sums(il, NP - 2 + p)
                            if p % 2 == 0:
                                if io:
                                    spread(io, p // 2, ip, ix)
                            else:
                                if ip:
                                    values(ip, p // 2, io)
                                if io:
                                    project_out(io, p // 2)
                    pipeline(pe, B, DEPTH, UNROLL, step)

                @block.scalar
                def _(act):
                    def probabilities(i, p):
                        if p < NP:
                            act.wait_ge(s["sc"], i.at(NP, p + 1))
                            after(act, s["ex"], i.at(NP, p - 1))
                            act.activation(th[:, p % 2, :], ps_s[:, 0:W], ACT.Tanh, scale=SCALE / CLAMP)\
                                .then_inc(s["th"], 1)
                        if p:
                            act.wait_ge(s["th"], i.at(NP, p))
                            after(act, s["pv"], i.at(NP, p - 4))
                            act.activation(pt[:, (p - 1) % 4, :], th[:, (p - 1) % 2, :], ACT.Exp, scale=CLAMP)\
                                .then_inc(s["ex"], 1)

                    def step(at):
                        ix, ip, ic, il, iy = at(1), at(2), at(3), at(4), at(6)
                        if iy:
                            act.wait_ge(s["y"], iy.at(4, 4))
                            after(act, s["yn"], iy.at(KT, -KT))
                            act.activation(y[:, iy.slot(2), :, :], ps_y[:, 0:T].rearrange("p (t d) -> p t d", t=KT),
                                           ACT.Copy).then_inc(s["yc"], 1)
                        if ix:
                            act.wait_ge(s["tp"], ix.at(1, 1))
                            after(act, s["sc"], ix.at(NP, -2 * NP))
                            act.activation(xh[:, ix.slot(3), :], ps_j[:, 0:T], ACT.Copy).then_inc(s["xh"], 1)
                        for p in range(NP + 1):
                            if ic:
                                probabilities(ic, p)
                            if ip and p < NP:
                                act.wait_ge(s["t"], ip.at(NP, p + 1))
                                after(act, s["sc"], ip.at(NP, p + 1 - NP))
                                act.activation(tH[:, p, :, :], ps_t[:, :].rearrange("p (n t) -> p n t", n=2),
                                               ACT.Copy).then_inc(s["tH"], 1)
                            if ip and p < NP and p % 2:
                                u = p // 2
                                b, kt, half = ip.slot(2), u // 2, u % 2
                                act.wait_ge(s["v"], ip.at(4, u + 1))
                                if u == 0:
                                    after(act, s["pv"], ip.at(NP, -NP))
                                act.activation(V[:, b, kt, half * 512:(half + 1) * 512], ps_j[:, :], ACT.Copy)\
                                    .then_inc(s["vc"], 1)
                            if il and p == 1:
                                act.wait_ge(s["pv"], il.at(NP, NP))
                                after(act, s["rec"], il.at(1))
                                act.activation(sums[:, :], ps_sum[:, 0:T], ACT.Copy).then_inc(s["sum"], 1)
                    pipeline(act, B, DEPTH, UNROLL, step)

                @block.gpsimd
                def _(pool):
                    def masked(i, p):
                        gates.wait(pool, gates.pool, s["ex"], i.at(NP, p + 1))
                        for d in (pt[:, p % 4, 0:W0].rearrange("p (h t) -> p h t", h=2)[:, :, 0:P],
                                  pt[:, p % 4, W0:W].rearrange("p (h t) -> p h t", h=2)):
                            last = pool.affine_select(out=d, in_=d, compare_op=ALU.is_ge, fill=0.0, base=0,
                                                      pattern=[[0, 2], [1, P]], channel_multiplier=-1)
                        last.then_inc(s["mk"], 1)

                    def step(at):
                        i0, ic, iy = at(0), at(3), at(6)
                        for p in range(NP):
                            if p == 6 and iy:
                                ln2.rstd(pool, iy, neghalf, eps)
                            if p == 4 and i0:
                                ln.rstd(pool, i0, neghalf, eps)
                            if ic:
                                masked(ic, p)
                    pipeline(pool, B, DEPTH, UNROLL, step)

                @block.vector
                def _(dve):
                    def copied(i, u):
                        dve.wait_ge(s["pv"], i.at(NP, 2 * u + 2))
                        dve.tensor_copy(oraw[:, i.slot(2), 2 * u:2 * u + 2, :],
                                        ps_o[u % 2][:, :].rearrange("p (n t) -> p n t", n=2)).then_inc(s["oc"], 1)

                    def added(i, p):
                        dve.wait_ge(s["mk"], i.at(NP, p + 1))
                        after(dve, s["pv"], i.at(NP, p - 1))
                        dve.tensor_tensor(both[:, p % 2, :, :],
                                          pt[:, p % 4, 0:W0].rearrange("p (h t) -> p h t", h=2)[:, :, P:T],
                                          pt[:, p % 4, W0:W].rearrange("p (h t) -> p h t", h=2), ALU.add)\
                            .then_inc(s["ad"], 1)

                    def step(at):
                        i0, ix, ip, ic, il, io, iy = (at(k) for k in range(7))
                        if ix:
                            b = ix.slot(3)
                            dve.wait_ge(s["xh"], ix.at(1, 1))
                            dve.tensor_tensor(xl[:, b, :], ps_j[:, 0:T], xh[:, b, :], ALU.subtract)\
                                .then_inc(s["xl"], 1)
                        for p in range(NP):
                            if ip:
                                dve.wait_ge(s["tH"], ip.at(NP, p + 1))
                                dve.tensor_tensor(tL[:, p, :, :], ps_t[:, :].rearrange("p (n t) -> p n t", n=2),
                                                  tH[:, p, :, :], ALU.subtract).then_inc(s["tL"], 1)
                            if io and p % 2 == 0:
                                u = p // 2
                                dve.wait_ge(s["r"], io.at(4, u + 1))
                                after(dve, s["y"], io.at(4, u - 1))
                                dve.tensor_tensor(on[:, u % 2, :, :], ps_j[:, :].rearrange("p (n t) -> p n t", n=2),
                                                  oraw[:, io.slot(2), 2 * u:2 * u + 2, :], ALU.mult)\
                                    .then_inc(s["on"], 1)
                            if ic and p:
                                added(ic, p - 1)
                            if il and p == 0:
                                added(il, NP - 1)
                            if il and p == 1:
                                dve.wait_ge(s["sum"], il.at(1, 1))
                                dve.reciprocal(rec[:, il.slot(2), :], sums[:, :]).then_inc(s["rec"], 1)
                            if il and p == 2:
                                copied(il, 3)
                                dve.wait_ge(s["rec"], il.at(1, 1))
                                after(dve, s["r"], il.at(4, -4))
                                dve.tensor_copy(rh[:, il.slot(2), :], rec[:, il.slot(2), :]).then_inc(s["rh"], 1)
                            if ic and p >= 3 and p % 2:
                                copied(ic, (p - 3) // 2)
                            if il and p == 3:
                                b = il.slot(2)
                                dve.wait_ge(s["rh"], il.at(1, 1))
                                dve.tensor_tensor(rl[:, b, :], rec[:, b, :], rh[:, b, :], ALU.subtract)\
                                    .then_inc(s["rl"], 1)
                            if iy and p == 5:
                                gates.wait(dve, gates.dve, s["yc"], iy.at(1, 1))
                                ln2.stats(dve, iy, lambda j: y[:, iy.slot(2), j, :])
                            if iy and p == 7:
                                b = iy.slot(2)
                                ln2.ready(dve, iy)
                                ln2.apply(dve, iy, lambda j: z[:, b, j, :], lambda j: y[:, b, j, :], s["yn"])
                            if iy and p == 7:
                                dve.wait_ge(s["yn"], iy.at(KT, KT))
                                dve.tensor_tensor(xs[:, tiles(iy, KT), :], xs[:, tiles(iy, KT), :],
                                                  z[:, iy.slot(2), :, :], ALU.add).then_inc(s["x"], 1)
                            if i0 and p == 3:
                                ln.stats(dve, i0, lambda j: xs[:, i0.at(KT, j), :])
                            if i0 and p == 5:
                                ln.ready(dve, i0)
                                after(dve, s["tp"], i0.at(1, -1))
                                ln.apply(dve, i0, lambda j: xn[:, i0.slot(2), j, :],
                                         lambda j: xs[:, i0.at(KT, j), :], s["xn"])
                    pipeline(dve, B, DEPTH, UNROLL, step)


def layer1_experts(nc, gates, xs, ident, neghalf, router_w, w_fc, w_proj, shared_fc, shared_proj, out_dram,
                   B, T, D, NT, E, eps):
    F = w_fc.shape[1]
    NF = F // P
    NE = E + 1
    G = 4
    N = G * P
    with ExitStack() as ctx:
        sb, pb, sem = scope(nc, ctx, "moe")
        fh = sb("fh", [P, NE, F], F32R)
        fl = sb("fl", [P, NE, F], F32R)
        pT = sb("pT", [P, NE, NF, D], F32)
        rT = sb("rT", [P, E], F32)
        iota = sb("iota", [P, G, E], F32)

        with ExitStack() as c2:
            sb2, pb2, sem2 = scope(nc, c2, "moew")
            nat = sb2("nat", [P, 2, 2, NF, D], F32)
            rw = sb2("rw", [E, D], F32)
            ii = sb2("ii", [P, G, E], mybir.dt.int32)
            ps_f = [pb2(f"ps_f{i}") for i in range(2)]
            ps_p = [pb2(f"ps_p{i}") for i in range(2)]
            ps_r = pb2("ps_r")
            s_w = [sem2(f"s_w{i}") for i in range(2)]
            s_r, s_rp, s_io = sem2("s_r"), sem2("s_rp"), sem2("s_io")
            s_f, s_p, s_hi, s_lo, s_pc = (sem2(n) for n in "s_f s_p s_hi s_lo s_pc".split())
            with nc.Block() as block:
                @block.sync
                def _(sp):
                    sp.dma_start(rw[:, :], router_w).then_inc(s_r, 16)
                    for e in range(NE):
                        if e >= 2:
                            sp.wait_ge(s_p, e - 1)
                        fc, pr = (w_fc[e], w_proj[e]) if e < E else (shared_fc, shared_proj)
                        sp.dma_start(nat[:, e % 2, 0, :, :], fc.rearrange("(c p) d -> p c d", p=P))\
                            .then_inc(s_w[e % 2], 16)
                        sp.dma_start(nat[:, e % 2, 1, :, :], pr.rearrange("d (c p) -> d c p", p=P))\
                            .then_inc(s_w[e % 2], 16)

                @block.gpsimd
                def _(pool):
                    pool.iota(ii[:, :, :], [[0, G], [1, E]], base=0, channel_multiplier=0).then_inc(s_io, 1)

                @block.tensor
                def _(pe):
                    pe.wait_ge(s_r, 16)
                    pe.transpose(ps_r[:, 0:E], rw[:, :], ident[0:E, 0:E]).then_inc(s_rp, 1)
                    for e in range(NE):
                        pe.wait_ge(s_w[e % 2], 32 * (e // 2 + 1))
                        if e >= 2:
                            pe.wait_ge(s_lo, e - 1)
                            pe.wait_ge(s_pc, e - 1)
                        for ps, k, s in ((ps_f, 0, s_f), (ps_p, 1, s_p)):
                            for c in range(NF):
                                mm = pe.transpose(ps[e % 2][:, c * P:(c + 1) * P], nat[:, e % 2, k, c, :], ident[:, :])
                            mm.then_inc(s, 1)

                @block.scalar
                def _(act):
                    for e in range(NE):
                        act.wait_ge(s_f, e + 1)
                        act.activation(fh[:, e, :], ps_f[e % 2][:, :], ACT.Copy).then_inc(s_hi, 1)
                        act.wait_ge(s_p, e + 1)
                        act.activation(pT[:, e, :, :], ps_p[e % 2][:, :].rearrange("p (c d) -> p c d", c=NF),
                                       ACT.Copy).then_inc(s_pc, 1)

                @block.vector
                def _(dve):
                    dve.wait_ge(s_rp, 1)
                    dve.tensor_copy(rT[:, :], ps_r[:, 0:E])
                    dve.wait_ge(s_io, 1)
                    dve.tensor_copy(iota[:, :, :], ii[:, :, :])
                    for e in range(NE):
                        dve.wait_ge(s_hi, e + 1)
                        dve.tensor_tensor(fl[:, e, :], ps_f[e % 2][:, :], fh[:, e, :], ALU.subtract)\
                            .then_inc(s_lo, 1)

        with ExitStack() as c2:
            sb2, pb2, sem2 = scope(nc, c2, "exp")
            ln, ln2 = (Norm((sb2, sem2), f"moe_ln{k}", G, gates) for k in (1, 2))
            xn = sb2("xn", [P, 2, G, D], F32)
            x32 = sb2("x32", [P, 2, N], F32)
            xh = sb2("xh", [P, 2, N], F32R)
            xl = sb2("xl", [P, 2, N], F32R)
            r = sb2("r", [P, 2, N], F32)
            h = sb2("h", [P, 3, N], F32)
            acc = sb2("acc", [P, 2, G, D], F32)
            z = sb2("z", [P, 2, G, D], F32)
            lmax = sb2("lmax", [P, G], F32)
            lg = sb2("lg", [P, G, E], F32)
            ex = sb2("ex", [P, G, E], F32)
            esum = sb2("esum", [P, G], F32)
            erec = sb2("erec", [P, G], F32)
            pr = sb2("pr", [P, G, E], F32)
            top = sb2("top", [P, G, 8], F32)
            idx = sb2("idx", [P, G, 8], U32)
            idf = sb2("idf", [P, G, 8], F32)
            den = sb2("den", [P, G], F32)
            denm = sb2("denm", [P, G], F32)
            drec = sb2("drec", [P, G], F32)
            m0 = sb2("m0", [P, G, E], F32)
            m1 = sb2("m1", [P, G, E], F32)
            mk = sb2("mk", [P, G, E], F32)
            pw = sb2("pw", [P, G, E], F32)
            cw = sb2("cw", [P, 2, G, E], F32)
            ps_t, ps_r = pb2("ps_t"), pb2("ps_r")
            ps_h = [pb2(f"ps_h{i}") for i in range(3)]
            ps_y = [pb2(f"ps_y{i}") for i in range(2)]
            names = "xn tp x32 xh xl rt lsub lexp a r h b acc z x".split()
            s = {n: sem2(f"s_{n}") for n in names}
            s_r = sem2("s_router")
            s_out = [sem2(f"s_out{i}") for i in range(2)]
            DEPTH = 5
            CH = NE * NF

            def per_expert(ap):
                return ap.unsqueeze(2).broadcast_to([P, G, E])

            with nc.Block() as block:
                @block.tensor
                def _(pe):
                    def hidden(i, k):
                        b, e, f = i.slot(2), k // NF, k % NF
                        if k == 0:
                            pe.wait_ge(s["xl"], i.at(1, 1))
                        after(pe, s["r"], i.at(CH, k - 2))
                        c = slice(f * P, (f + 1) * P)
                        split_matmul(pe, ps_h[k % 3][:, :], (fh[:, e, c], fl[:, e, c]), (xh[:, b, :], xl[:, b, :]))\
                            .then_inc(s["a"], 1)

                    def projected(i, k):
                        e, f = k // NF, k % NF
                        pe.wait_ge(s["h"], i.at(CH, k + 1))
                        if f == 0:
                            after(pe, s["acc"], i.at(NE, e - 1))
                        bank = ps_y[(i.slot(2) * NE + e) % 2]
                        for t in range(G):
                            mm = pe.matmul(bank[:, t * P:(t + 1) * P], h[:, k % 3, t * P:(t + 1) * P], pT[:, e, f, :],
                                           start=(f == 0 and t == 0), stop=(f == NF - 1), skip_group_check=True)
                        mm.then_inc(s["b"], 1)

                    def step(at):
                        if i := at(1):
                            b = i.slot(2)
                            pe.wait_ge(s["xn"], i.at(G, G))
                            after(pe, s["x32"], i.at(1))
                            for j in range(G):
                                mm = pe.transpose(ps_t[:, j * P:(j + 1) * P], xn[:, b, j, :], ident[:, :])
                            mm.then_inc(s["tp"], 1)
                        i = at(2)
                        for k in range(CH + 2):
                            if i and k < CH:
                                hidden(i, k)
                            if k == 4 and at(1):
                                b = at(1).slot(2)
                                pe.wait_ge(s["x32"], at(1).at(1, 1))
                                after(pe, s["lsub"], at(1).at(1))
                                for j in range(G):
                                    mm = pe.matmul(ps_r[:, j * E:(j + 1) * E], x32[:, b, j * P:(j + 1) * P],
                                                   rT[:, :], start=True, stop=True)
                                mm.then_inc(s["rt"], 1)
                            if i and k >= 2:
                                projected(i, k - 2)
                    pipeline(pe, NT // G, DEPTH, 2, step)

                @block.scalar
                def _(act):
                    def step(at):
                        if i := at(1):
                            b = i.slot(2)
                            act.wait_ge(s["tp"], i.at(1, 1))
                            after(act, s["rt"], i.at(1, -1))
                            after(act, s["xl"], i.at(1, -1))
                            act.activation(x32[:, b, :], ps_t[:, :], ACT.Copy).then_inc(s["x32"], 1)
                        i = at(2)
                        for k in range(CH):
                            if i:
                                act.wait_ge(s["a"], i.at(CH, k + 1))
                                after(act, s["h"], i.at(CH, k - 1))
                                act.activation(r[:, k % 2, :], ps_h[k % 3][:, :], ACT.Relu).then_inc(s["r"], 1)
                            if k == 12 and at(1):
                                act.wait_ge(s["lsub"], at(1).at(1, 1))
                                act.activation(ex[:, :, :], lg[:, :, :], ACT.Exp).then_inc(s["lexp"], 1)
                    pipeline(act, NT // G, DEPTH, 2, step)

                @block.gpsimd
                def _(pool):
                    def step(at):
                        if i := at(0):
                            ln.rstd(pool, i, neghalf, eps)
                        if i := at(3):
                            ln2.rstd(pool, i, neghalf, eps)
                    pipeline(pool, NT // G, DEPTH, 2, step)

                @block.vector
                def _(dve):
                    def route(i):
                        n = [0]

                        def link(ins):
                            n[0] += 1
                            ins.then_inc(s_r, 1)
                            gates.wait(dve, gates.dve, s_r, i.at(ROUTE, n[0]))

                        dve.wait_ge(s["rt"], i.at(1, 1))
                        lo = ps_r[:, 0:G * E].rearrange("p (g e) -> p g e", g=G)
                        link(dve.tensor_reduce(lmax[:, :], lo, AX.X, ALU.max))
                        dve.tensor_tensor(lg[:, :, :], lo, per_expert(lmax[:, :]), ALU.subtract)\
                            .then_inc(s["lsub"], 1)
                        dve.wait_ge(s["lexp"], i.at(1, 1))
                        link(dve.tensor_reduce(esum[:, :], ex[:, :, :], AX.X, ALU.add))
                        link(dve.reciprocal(erec[:, :], esum[:, :]))
                        link(dve.tensor_tensor(pr[:, :, :], ex[:, :, :], per_expert(erec[:, :]), ALU.mult))
                        for j in range(G):
                            link(dve.max(top[:, j, :], pr[:, j, :]))
                        for j in range(G):
                            link(dve.max_index(idx[:, j, :], top[:, j, :], pr[:, j, :]))
                        link(dve.tensor_copy(idf[:, :, :], idx[:, :, :]))
                        link(dve.tensor_tensor(den[:, :], top[:, :, 0], top[:, :, 1], ALU.add))
                        link(dve.tensor_scalar(denm[:, :], den[:, :], 1e-9, None, ALU.max))
                        link(dve.reciprocal(drec[:, :], denm[:, :]))
                        link(dve.tensor_tensor(m0[:, :, :], iota[:, :, :], per_expert(idf[:, :, 0]), ALU.is_equal))
                        link(dve.tensor_tensor(m1[:, :, :], iota[:, :, :], per_expert(idf[:, :, 1]), ALU.is_equal))
                        link(dve.tensor_tensor(mk[:, :, :], m0[:, :, :], m1[:, :, :], ALU.add))
                        link(dve.tensor_tensor(pw[:, :, :], pr[:, :, :], per_expert(drec[:, :]), ALU.mult))
                        link(dve.tensor_tensor(cw[:, i.slot(2), :, :], pw[:, :, :], mk[:, :, :], ALU.mult))
                        assert n[0] == ROUTE

                    ROUTE = 13 + 2 * G

                    def weighed(i, e):
                        b = i.slot(2)
                        bank = ps_y[(i.slot(2) * NE + e) % 2]
                        dve.wait_ge(s["b"], i.at(CH, NF * (e + 1)))
                        if e:
                            dve.wait_ge(s["acc"], i.at(NE, e))
                        for t in range(G):
                            y = bank[:, t * P:(t + 1) * P]
                            a = acc[:, b, t, :]
                            if e == 0:
                                o = dve.tensor_scalar(a, y, cw[:, b, t, 0:1], None, ALU.mult)
                            elif e < E:
                                o = dve.scalar_tensor_tensor(a, y, cw[:, b, t, e:e + 1], a, ALU.mult, ALU.add)
                            else:
                                o = dve.tensor_tensor(a, y, a, ALU.add)
                        o.then_inc(s["acc"], 1)

                    def step(at):
                        if i := at(4):
                            b = i.slot(2)
                            ln2.ready(dve, i)
                            ln2.apply(dve, i, lambda j: z[:, b, j, :], lambda j: acc[:, b, j, :], s["z"])
                            dve.wait_ge(s["z"], i.at(G, G))
                            dve.tensor_tensor(xs[:, tiles(i, G), :], xs[:, tiles(i, G), :], z[:, b, :, :],
                                              ALU.add).then_inc(s["x"], 1)
                        i = at(2)
                        for k in range(CH + 2):
                            if i and k < CH:
                                dve.wait_ge(s["r"], i.at(CH, k + 1))
                                after(dve, s["b"], i.at(CH, k - 2))
                                dve.tensor_tensor(h[:, k % 3, :], r[:, k % 2, :], r[:, k % 2, :], ALU.mult)\
                                    .then_inc(s["h"], 1)
                            if k == 2 and at(1):
                                b = at(1).slot(2)
                                dve.wait_ge(s["x32"], at(1).at(1, 1))
                                after(dve, s["a"], at(1).at(CH, -CH))
                                dve.tensor_copy(xh[:, b, :], x32[:, b, :]).then_inc(s["xh"], 1)
                                dve.wait_ge(s["xh"], at(1).at(1, 1))
                                dve.tensor_tensor(xl[:, b, :], x32[:, b, :], xh[:, b, :], ALU.subtract)\
                                    .then_inc(s["xl"], 1)
                            if k == 12 and at(1):
                                route(at(1))
                            if k == 22 and at(0):
                                i0 = at(0)
                                ln.stats(dve, i0, lambda j: xs[:, i0.at(G, j), :])
                            if k == 30 and at(0):
                                b = i0.slot(2)
                                ln.ready(dve, i0)
                                after(dve, s["tp"], i0.at(1, -1))
                                ln.apply(dve, i0, lambda j: xn[:, b, j, :], lambda j: xs[:, i0.at(G, j), :], s["xn"])
                            if i and k >= NF + 1 and (k - 1) % NF == 0:
                                weighed(i, (k - 1) // NF - 1)
                        if i:
                            b = i.slot(2)
                            gates.wait(dve, gates.dve, s["acc"], i.at(NE, NE))
                        if i := at(3):
                            pass
                    def step_with_stats(at):
                        step(at)
                        if i := at(2):
                            ln2.stats(dve, i, lambda j: acc[:, i.slot(2), j, :])
                    pipeline(dve, NT // G, DEPTH, 2, step_with_stats)

                @block.sync
                def _(sp):
                    def step(at):
                        if i := at(4):
                            sp.wait_ge(s["x"], i.at(1, 1))
                            sp.dma_start(out_dram[:, tiles(i, G), :], xs[:, tiles(i, G), :])\
                                .then_inc(s_out[i.slot(2)], 16)
                    pipeline(sp, NT // G, DEPTH, 2, step)
                    for b in range(2):
                        sp.wait_ge(s_out[b], NT // G // 2 * 16)


INPUTS = ("L0_attn_x", "L0_attn_W_in", "L0_attn_A_in", "L0_attn_B_in", "L0_attn_W_out", "L0_ffn_W_r",
          "L0_ffn_W_k", "L0_ffn_W_v", "L0_ffn_mu_r", "L0_ffn_mu_k", "L1_attn_Wq", "L1_attn_Wk",
          "L1_attn_Wv", "L1_attn_Wo", "L1_ffn_router_w", "L1_ffn_w_fc", "L1_ffn_w_proj",
          "L1_ffn_shared_fc", "L1_ffn_shared_proj")


def kernel(**inputs):
    import numpy as np
    from concourse import bacc
    from concourse.bass_utils import run_bass_kernel_spmd

    nc = bacc.Bacc("TRN2", target_bir_lowering=False, num_devices=1)
    arrays, args = {}, []
    for name in INPUTS:
        a = np.ascontiguousarray(inputs[name])
        arrays[f"in_{name}"] = a
        args.append(nc.dram_tensor(f"in_{name}", a.shape, mybir.dt.from_np(a.dtype), kind="ExternalInput").ap())
    out = nc.dram_tensor("out_x", inputs["L0_attn_x"].shape, F32, kind="ExternalOutput").ap()
    program(nc, *args, out)
    r = run_bass_kernel_spmd(nc, [arrays], core_ids=[0])
    return r.results[0]["out_x"]
```

```python
from contextlib import ExitStack

import concourse.bass as bass
from concourse import mybir

F32 = mybir.dt.float32
F32R = mybir.dt.float32r
U32 = mybir.dt.uint32
ALU = mybir.AluOpType
ACT = mybir.ActivationFunctionType
AX = mybir.AxisListType
P = 128
EPS = 1e-5


class Item:

    def __init__(self, reg, const, unroll):
        self.reg, self.const, self.unroll = reg, const, unroll

    def at(self, mult=1, add=0):
        if self.reg is None:
            return mult * self.const + add
        return self.reg * (mult * self.unroll) + (mult * self.const + add)

    def slot(self, n):
        assert self.unroll % n == 0
        return self.const % n

    def turn(self, n):
        assert self.unroll % n == 0
        if self.reg is None:
            return self.const // n
        return self.reg * (self.unroll // n) + self.const // n


def after(eng, sem, value):
    if isinstance(value, int) and value <= 0:
        return
    eng.wait_ge(sem, value)


class Gates:

    def __init__(self, sem):
        self.dve, self.pool = sem("dve_gate"), sem("pool_gate")

    @staticmethod
    def wait(eng, gate, sem, value):
        eng.wait_ge(sem, value)
        if not isinstance(value, int):
            eng.sem_inc(gate, 1)


def pipeline(eng, items, depth, unroll, step):
    lead = -(-(depth + 3) // unroll) * unroll
    turns = max((items - lead) // unroll, 0)

    def plain(t):
        step(lambda s: Item(None, t - s, unroll) if 0 <= t - s < items else None)

    for t in range(lead):
        plain(t)
    if turns:
        with eng.Fori(0, turns) as g:
            for u in range(unroll):
                step(lambda s, u=u: Item(g, lead + u - s, unroll))
    for t in range(lead + turns * unroll, items + depth - 1):
        plain(t)


def tiles(item, n):
    return bass.ds(item.at(n), n)


def program(nc, x_in, W_in, A_in, B_in, W_out, W_r, W_k, W_v, mu_r, mu_k,
            Wq, Wk, Wv, Wo, router_w, w_fc, w_proj, shared_fc, shared_proj, out):
    B, T, D = x_in.shape
    NT = B * T // P
    KT = T // P
    E = router_w.shape[0]
    assert D == P and T == 2 * P

    x_dram = x_in.rearrange("b (t p) d -> p (b t) d", p=P)
    out_dram = out.rearrange("b (t p) d -> p (b t) d", p=P)

    with ExitStack() as ctx:
        xs = ctx.enter_context(nc.sbuf_tensor("xs", [P, NT, D], F32))
        ident = ctx.enter_context(nc.sbuf_tensor("ident", [P, P], F32))
        neghalf = ctx.enter_context(nc.sbuf_tensor("neghalf", [P, 4], F32))
        spare = ctx.enter_context(nc.sbuf_tensor("spare", [P, NT, D], F32))
        s_next = ctx.enter_context(nc.semaphore("next_weights"))
        gates = Gates(lambda name: ctx.enter_context(nc.semaphore(name)))
        eps = EPS
        layer0(nc, gates, xs, ident, neghalf, spare, s_next, (Wq, Wk, Wv, Wo), x_dram, W_in, A_in, B_in,
               W_out, W_r, W_k, W_v, mu_r, mu_k, B, T, D, NT, KT, eps)
        layer1_attention(nc, gates, xs, ident, neghalf, spare, s_next, Wq, Wk, Wv, Wo, w_fc, w_proj,
                         B, T, D, NT, KT, eps)
        layer1_experts(nc, gates, xs, ident, neghalf, spare, s_next, router_w, w_fc, w_proj, shared_fc, shared_proj,
                       out_dram, B, T, D, NT, E, eps)


class Norm:

    def __init__(self, alloc, name, n, gates, shifted=False):
        sb, sem = alloc
        self.gates = gates
        self.n = n
        self.st = sb(f"{name}_st", [P, 2, n, 6], F32)
        self.mv = sb(f"{name}_mv", [P, 2, n, 2], F32)
        self.ve = sb(f"{name}_ve", [P, 2, n], F32)
        self.rs = sb(f"{name}_rs", [P, 2, n], F32)
        self.s_stats = sem(f"{name}_stats")
        self.s_mean = sem(f"{name}_mean")
        self.s_vareps = sem(f"{name}_vareps")
        self.s_rstd = sem(f"{name}_rstd")
        self.shifted = shifted
        if shifted:
            self.neg = sb(f"{name}_neg", [P, 2, n], F32)
            self.sh = sb(f"{name}_sh", [P, 2, n], F32)
            self.s_neg = sem(f"{name}_neg_mean")
            self.s_shift = sem(f"{name}_shift")

    def stats(self, dve, item, src):
        n, b = self.n, item.slot(2)
        for j in range(n):
            dve.bn_stats(self.st[:, b, j, :], src(j)).then_inc(self.s_stats, 1)
        self.gates.wait(dve, self.gates.dve, self.s_stats, item.at(n, n))
        for j in range(n):
            dve.bn_aggr(self.mv[:, b, j, :], self.st[:, b, j, :]).then_inc(self.s_mean, 1)

    def rstd(self, pool, item, neghalf, eps):
        n, b = self.n, item.slot(2)
        self.gates.wait(pool, self.gates.pool, self.s_mean, item.at(n, n))
        pool.tensor_scalar(self.ve[:, b, :], self.mv[:, b, :, 1], eps, None, ALU.add)\
            .then_inc(self.s_vareps, 1)
        if self.shifted:
            pool.tensor_scalar(self.neg[:, b, :], self.mv[:, b, :, 0], -1.0, None, ALU.mult)\
                .then_inc(self.s_neg, 1)
        pool.wait_ge(self.s_vareps, item.at(1, 1))
        pool.tensor_tensor(self.rs[:, b, :], self.ve[:, b, :], neghalf[:, 0:n], ALU.pow)\
            .then_inc(self.s_rstd, 1)

    def shift(self, pool, item):
        b = item.slot(2)
        pool.wait_ge(self.s_neg, item.at(1, 1))
        pool.wait_ge(self.s_rstd, item.at(1, 1))
        pool.tensor_tensor(self.sh[:, b, :], self.neg[:, b, :], self.rs[:, b, :], ALU.mult)\
            .then_inc(self.s_shift, 1)

    def apply_scaled(self, act, item, dst, src, s_done):
        b = item.slot(2)
        act.wait_ge(self.s_shift, item.at(1, 1))
        for j in range(self.n):
            act.activation(dst(j), src(j), ACT.Identity, bias=self.sh[:, b, j:j + 1],
                           scale=self.rs[:, b, j:j + 1]).then_inc(s_done, 1)

    def ready(self, dve, item):
        dve.wait_ge(self.s_rstd, item.at(1, 1))

    def apply(self, dve, item, dst, src, s_done):
        b = item.slot(2)
        for j in range(self.n):
            dve.tensor_scalar(dst(j), src(j), self.mv[:, b, j, 0:1], self.rs[:, b, j:j + 1],
                              ALU.subtract, ALU.mult).then_inc(s_done, 1)


def scope(nc, ctx, phase):
    def sb(name, shape, dt):
        return ctx.enter_context(nc.sbuf_tensor(f"{phase}_{name}", shape, dt))

    def pb(name):
        return ctx.enter_context(nc.psum_tensor(f"{phase}_{name}", [P, 512], F32))

    def sem(name):
        return ctx.enter_context(nc.semaphore(f"{phase}_{name}"))

    return sb, pb, sem


def layer1_natural(spare, H, F, D):
    DH, n = F // H, F // P
    return (spare[0:DH, 0:H, :], spare[0:DH, H:2 * H, :], spare[:, 2 * H:2 * H + n, :],
            spare[:, 2 * H + n:2 * H + 2 * n, :].rearrange("p c d -> p (c d)"))


def expert_natural(spare, e, NF):
    return spare[:, 2 * NF * e:2 * NF * e + NF, :], spare[:, 2 * NF * e + NF:2 * NF * (e + 1), :]


def layer0(nc, gates, xs, ident, neghalf, vall, s_next, next_weights, x_dram, W_in, A_in, B_in, W_out,
           W_r, W_k, W_v, mu_r, mu_k, B, T, D, NT, KT, eps):
    H = 16
    DH = D // H
    SL = 32
    HC = P // SL
    NC = H // HC
    SCALE = float(DH) ** -0.5
    LORA = 1.0 / A_in.shape[0]
    qk_dram = nc.dram_tensor("qk_planes", [B // 2, 2, 3, P, 2 * T], F32, kind="Internal").ap()
    max_dram = nc.dram_tensor("max_parts", [4, 2 * H, T], F32, kind="Internal").ap()

    with ExitStack() as ctx:
        sb, pb, sem = scope(nc, ctx, "l0")
        WT = sb("WT", [P, 4, D], F32)
        mu = sb("mu", [P, 2], F32)
        omu = sb("omu", [P, 2], F32)
        aall = sb("aall", [P, NT, D], F32)

        c3 = ctx.enter_context(ExitStack())
        NBUF = 4
        sb3, _, _ = scope(nc, c3, "l0st")
        QS = [sb3(f"QS{i}", [P, H, T], F32R) for i in range(NBUF)]
        KS = [sb3(f"KS{i}", [P, NC, T], F32R) for i in range(NBUF)]
        c4 = ctx.enter_context(ExitStack())
        sb4, _, _ = scope(nc, c4, "l0q")
        WeffT = sb4("WeffT", [P, 3 * D], F32)
        ones = sb4("ones", [2, NC, T], F32)

        s_x0, s_x = sem("s_x_quarter"), sem("s_x_rest")
        s_ones = sem("s_ones_placed")

        with ExitStack() as c2:
            sb2, pb2, sem2 = scope(nc, c2, "l0w")
            w_in = sb2("w_in", [P, 3, 3 * D], F32)
            a_in = sb2("a_in", [P, 3 * D], F32)
            b_in = sb2("b_in", [P, 3, P], F32)
            w4 = sb2("w4", [P, 4, D], F32)
            bT = sb2("bT", [P, 3 * D], F32)
            ps_b, ps_e, ps_w = pb2("ps_b"), pb2("ps_e"), pb2("ps_w")
            s_w = sem2("s_weights")
            s_id = sem2("s_ident")
            s_set = sem2("s_set")
            s_pe = sem2("s_transposed")
            s_bT = sem2("s_bT")
            with nc.Block() as block:
                @block.sync
                def _(sp):
                    sp.dma_start(w_in[:, :, :], W_in.rearrange("(c p) n -> p c n", p=P)).then_inc(s_w, 16)
                    sp.dma_start(a_in[:, :], A_in).then_inc(s_w, 16)
                    sp.dma_start(b_in[:, :, :], B_in.rearrange("(c p) n -> p c n", p=P)).then_inc(s_w, 16)
                    for n, w in enumerate((W_out, W_r, W_k, W_v)):
                        sp.dma_start(w4[:, n, :], w).then_inc(s_w, 16)
                    for n, m in enumerate((mu_r, mu_k)):
                        sp.dma_start(mu[:, n:n + 1], m.rearrange("(d a) -> d a", a=1)).then_inc(s_w, 16)
                    for q in range(4):
                        sp.dma_start(xs[:, q * NT // 4:(q + 1) * NT // 4, :],
                                     x_dram[:, q * NT // 4:(q + 1) * NT // 4, :]).then_inc(s_x if q else s_x0, 16)
                    sp.wait_ge(s_set, 1 + NBUF)
                    for b in range(NBUF):
                        for j in range(HC):
                            row = SL * j + 3 * DH
                            sp.dma_start(KS[b][row:row + 2, :, :].bitcast(F32), ones[:, :, :]).then_inc(s_ones, 16)

                @block.gpsimd
                def _(pool):
                    pool.memset(ident[:, :], 0.0).then_inc(s_id, 1)
                    pool.memset(neghalf[:, :], -0.5)
                    pool.wait_ge(s_id, 1)
                    pool.affine_select(out=ident[:, :], in_=ident[:, :], compare_op=ALU.not_equal,
                                       fill=1.0, base=0, pattern=[[-1, P]], channel_multiplier=1)\
                        .then_inc(s_id, 1)
                    pool.memset(ones[:, :, :], 1.0).then_inc(s_set, 1)
                    for b in range(NBUF):
                        pool.memset(KS[b][:, :, :].bitcast(F32), 0.0).then_inc(s_set, 1)
                    for b in range(NBUF):
                        pool.memset(QS[b][:, :, :].bitcast(F32), 0.0)

                @block.tensor
                def _(pe):
                    pe.wait_ge(s_id, 2)
                    pe.wait_ge(s_w, 9 * 16)
                    for c in range(3):
                        mm = pe.transpose(ps_b[:, c * P:(c + 1) * P], b_in[:, c, :], ident[:, :])
                    mm.then_inc(s_pe, 1)
                    for n in range(4):
                        mm = pe.transpose(ps_w[:, n * P:(n + 1) * P], w4[:, n, :], ident[:, :])
                    mm.then_inc(s_pe, 1)
                    pe.wait_ge(s_bT, 1)
                    for c in range(3):
                        o = ps_e[:, c * P:(c + 1) * P]
                        for j in range(3):
                            pe.matmul(o, w_in[:, c, j * D:(j + 1) * D], ident[:, :],
                                      start=(j == 0), stop=False)
                        for j in range(3):
                            mm = pe.matmul(o, a_in[:, j * D:(j + 1) * D], bT[:, c * P:(c + 1) * P],
                                           start=False, stop=(j == 2))
                    mm.then_inc(s_pe, 1)

                @block.scalar
                def _(act):
                    act.wait_ge(s_pe, 1)
                    act.activation(bT[:, :], ps_b[:, 0:3 * D], ACT.Copy, scale=LORA).then_inc(s_bT, 1)
                    act.wait_ge(s_pe, 3)
                    for a in range(2):
                        act.activation(WeffT[:, a * D:(a + 1) * D].rearrange("p (r h) -> p r h", h=H),
                                       ps_e[:, a * D:(a + 1) * D].rearrange("p (h r) -> p r h", h=H),
                                       ACT.Copy)
                    act.activation(WeffT[:, 2 * D:3 * D], ps_e[:, 2 * D:3 * D], ACT.Copy)

                @block.vector
                def _(dve):
                    dve.wait_ge(s_w, 9 * 16)
                    dve.tensor_scalar(omu[:, :], mu[:, :], -1.0, 1.0, ALU.mult, ALU.add)
                    dve.wait_ge(s_pe, 2)
                    dve.tensor_copy(WT[:, :, :], ps_w[:, :].rearrange("p (n d) -> p n d", n=4))

        with ExitStack() as c2:
            sb2, pb2, sem2 = scope(nc, c2, "l0in")
            ln = Norm((sb2, sem2), "ln_a", KT, gates)
            xn = sb2("xn", [P, 2, KT, D], F32)
            xT = sb2("xT", [P, 4, T], F32)
            qkh = sb2("qkh", [P, 2, 2, 2, T], F32R)
            qkl = sb2("qkl", [P, 2, 2, 2, T], F32R)
            ps_t = [pb2(f"ps_t{i}") for i in range(2)]
            ps_qk = [pb2(f"ps_qk{i}") for i in range(2)]
            ps_v = [pb2(f"ps_v{i}") for i in range(2)]
            s_xn, s_tp, s_xT = sem2("s_xn"), sem2("s_tp"), sem2("s_xT")
            s_qk, s_v = sem2("s_qk"), sem2("s_v")
            s_hi, s_lo, s_vc = sem2("s_hi"), sem2("s_lo"), sem2("s_vc")
            s_st = [sem2(f"s_stored{i}") for i in range(2)]
            DEPTH = 5
            with nc.Block() as block:
                @block.vector
                def _(dve):
                    def step(at):
                        if i := at(0):
                            if i.reg is None and i.const < NT // 4 // KT:
                                dve.wait_ge(s_x0, 16)
                            else:
                                dve.wait_ge(s_x, 48)
                            ln.stats(dve, i, lambda j: xs[:, i.at(KT, j), :])
                        if i := at(1):
                            b = i.slot(2)
                            ln.ready(dve, i)
                            after(dve, s_tp, i.at(1, -1))
                            ln.apply(dve, i, lambda j: xn[:, b, j, :], lambda j: xs[:, i.at(KT, j), :], s_xn)
                        if i := at(4):
                            b = i.slot(2)
                            pair = i.slot(4) // 2
                            dve.wait_ge(s_hi, i.at(1, 1))
                            after(dve, s_st[pair], i.turn(4) * 64)
                            dve.tensor_tensor(qkl[:, pair, :, b, :], ps_qk[b][:, :].rearrange("p (a t) -> p a t", a=2),
                                              qkh[:, pair, :, b, :], ALU.subtract).then_inc(s_lo, 1)
                    pipeline(dve, B, DEPTH, 4, step)

                @block.gpsimd
                def _(pool):
                    def step(at):
                        if i := at(0):
                            ln.rstd(pool, i, neghalf, eps)
                    pipeline(pool, B, DEPTH, 4, step)

                @block.tensor
                def _(pe):
                    def step(at):
                        if i := at(3):
                            b = i.slot(2)
                            pe.wait_ge(s_xT, i.at(1, 1))
                            after(pe, s_lo, i.at(1, -1))
                            for a in range(2):
                                mm = pe.matmul(ps_qk[b][:, a * T:(a + 1) * T], WeffT[:, a * D:(a + 1) * D],
                                               xT[:, i.slot(4), :], start=True, stop=True)
                            mm.then_inc(s_qk, 1)
                            after(pe, s_vc, i.at(1, -1))
                            for j in range(KT):
                                mm = pe.matmul(ps_v[b][:, j * D:(j + 1) * D], xT[:, i.slot(4), j * P:(j + 1) * P],
                                               WeffT[:, 2 * D:3 * D], start=True, stop=True)
                            mm.then_inc(s_v, 1)
                        if i := at(1):
                            b = i.slot(2)
                            pe.wait_ge(s_xn, i.at(KT, KT))
                            after(pe, s_xT, i.at(1, -1))
                            for j in range(KT):
                                mm = pe.transpose(ps_t[b][:, j * P:(j + 1) * P], xn[:, b, j, :], ident[:, :])
                            mm.then_inc(s_tp, 1)
                    pipeline(pe, B, DEPTH, 4, step)

                @block.scalar
                def _(act):
                    def step(at):
                        if i := at(3):
                            b = i.slot(2)
                            pair = i.slot(4) // 2
                            act.wait_ge(s_qk, i.at(1, 1))
                            after(act, s_st[pair], i.turn(4) * 64)
                            act.activation(qkh[:, pair, :, b, :], ps_qk[b][:, :].rearrange("p (a t) -> p a t", a=2),
                                           ACT.Copy).then_inc(s_hi, 1)
                            act.wait_ge(s_v, i.at(1, 1))
                            act.activation(vall[:, tiles(i, KT), :],
                                           ps_v[b][:, 0:T].rearrange("p (t d) -> p t d", t=KT), ACT.Copy)\
                                .then_inc(s_vc, 1)
                        if i := at(1):
                            b = i.slot(2)
                            act.wait_ge(s_tp, i.at(1, 1))
                            after(act, s_v, i.at(1, -3))
                            act.activation(xT[:, i.slot(4), :], ps_t[b][:, 0:T], ACT.Copy).then_inc(s_xT, 1)
                    pipeline(act, B, DEPTH, 4, step)

                @block.sync
                def _(sp):
                    def step(at):
                        if (i := at(4)) and i.slot(2) == 1:
                            pair = i.slot(4) // 2
                            sp.wait_ge(s_hi, i.at(1, 1))
                            for a, planes in ((0, slice(0, 3, 2)), (1, slice(1, 3))):
                                sp.dma_start(qk_dram[bass.ds(i.turn(2), 1), a, planes, :, :]
                                             .rearrange("o g p t -> p (o g) t"),
                                             qkh[:, pair, a, :, :].rearrange("p o t -> p (o t)").unsqueeze(1)
                                             .broadcast_to([P, 2, 2 * T]).bitcast(F32)).then_inc(s_st[pair], 16)
                            sp.wait_ge(s_lo, i.at(1, 1))
                            for a, plane in ((0, 1), (1, 0)):
                                sp.dma_start(qk_dram[bass.ds(i.turn(2), 1), a, plane, :, :]
                                             .rearrange("o p t -> p (o t)"),
                                             qkl[:, pair, a, :, :].rearrange("p o t -> p (o t)").bitcast(F32))\
                                    .then_inc(s_st[pair], 16)
                    pipeline(sp, B, DEPTH, 4, step)
                    sp.wait_ge(s_ones, NBUF * HC * 16)
                    for b in range(2):
                        sp.wait_ge(s_st[b], B // 4 * 64)

        c4.close()

        with ExitStack() as c2:
            sb2, pb2, sem2 = scope(nc, c2, "l0att")
            V0 = sb2("V0", [P, 2, KT, H, SL], F32)
            NPT = 3
            PT = sb2("PT", [P, NPT, HC, T], F32)
            OT = sb2("OT", [P, NC, T], F32)
            nmax = sb2("nmax", [P, KT, H], F32)
            mparts = sb2("mparts", [P, 2, KT, 2, H], F32R)
            mT = sb2("mT", [2 * H, 2, T], F32)
            rsum = sb2("rsum", [P, 2, H], F32)
            ps_a = [pb2(f"ps_a{i}") for i in range(2)]
            ps_s = [c2.enter_context(nc.psum_tensor(f"l0att_ps_s{i}", [P, HC, T], F32)) for i in range(2)]
            ps_o, ps_x = pb2("ps_o"), pb2("ps_x")
            s_ld = [sem2(f"s_loaded{i}") for i in range(NBUF)]
            s_mr = [sem2(f"s_maxrows{i}") for i in range(NBUF)]
            s_md = sem2("s_maxstored")
            s_a, s_mx, s_mp = sem2("s_passA"), sem2("s_max"), sem2("s_maxparts")
            s_mtp, s_mT = sem2("s_maxT_ps"), sem2("s_maxT")
            s_s, s_e, s_pv, s_oc = sem2("s_scores"), sem2("s_exp"), sem2("s_pv"), sem2("s_ocopied")
            s_v0 = sem2("s_v0")
            s_ot, s_rc, s_n = sem2("s_otT"), sem2("s_recip"), sem2("s_normed")
            STEPS = NC * KT
            LOADS = 2 * HC * 16
            DEPTH = 5
            with nc.Block() as block:
                @block.sync
                def _(sp):
                    def step(at):
                        if i := at(0):
                            b = i.slot(NBUF)
                            after(sp, s_s, i.at(STEPS, -(NBUF - 1) * STEPS))
                            for j in range(HC):
                                for a, dst in enumerate((QS[b][SL * j:SL * j + 3 * DH, j:H:HC, :],
                                                         KS[b][SL * j:SL * j + 3 * DH])):
                                    src = qk_dram[bass.ds(i.turn(2), 1), a, :, :, i.slot(2) * T:(i.slot(2) + 1) * T]\
                                        .rearrange("o g (r c j) t -> j (o g r) c t", r=DH, j=HC)[j]
                                    sp.dma_start(dst.bitcast(F32), src).then_inc(s_ld[b], 16)
                        if i := at(2):
                            b = i.slot(NBUF)
                            sp.wait_ge(s_mT, i.at(1, 1))
                            sp.dma_start(max_dram[b], mT[:, i.slot(2), :]).then_inc(s_md, 16)
                            sp.wait_ge(s_md, i.at(16, 16))
                            for j in range(HC):
                                row = SL * j + 3 * DH
                                sp.dma_start(QS[b][row:row + 2, j:H:HC, :].bitcast(F32),
                                             max_dram[b].rearrange("(l c j) t -> j l c t", l=2, j=HC)[j])\
                                    .then_inc(s_mr[b], 16)
                    pipeline(sp, B, DEPTH, NBUF, step)

                @block.gpsimd
                def _(pool):
                    pool.memset(V0[:, :, :, :, DH + 1:SL], 0.0)
                    pool.memset(V0[:, :, :, :, DH:DH + 1], 1.0)

                    def step(at):
                        if i := at(2):
                            b = i.slot(2)
                            after(pool, s_pv, i.at(STEPS, -STEPS))
                            pool.tensor_copy(V0[:, b, :, :, 0:DH],
                                             vall[:, tiles(i, KT), :].rearrange("p t (h d) -> p t h d", h=H))\
                                .then_inc(s_v0, 1)
                    pipeline(pool, B, DEPTH, NBUF, step)

                @block.tensor
                def _(pe):
                    def pass_a(i, k):
                        t, h = k // 8, 2 * (k % 8)
                        b = i.slot(NBUF)
                        after(pe, s_mx, i.at(16, k - 1))
                        for n in range(2):
                            mm = pe.matmul(ps_a[k % 2][:, n * T:(n + 1) * T], QS[b][:, h + n, t * P:(t + 1) * P],
                                           KS[b][:, (h + n) // HC, :], start=True, stop=True)
                        mm.then_inc(s_a, 1)

                    def scores(i, s):
                        c, kt = s // KT, s % KT
                        b = i.slot(NBUF)
                        after(pe, s_e, i.at(STEPS, s - 1))
                        for n in range(2):
                            mm = pe.matmul(ps_s[s % 2][:, 2 * n:2 * n + 2, :], KS[b][:, c, kt * P:(kt + 1) * P],
                                           QS[b][:, HC * c + 2 * n:HC * c + 2 * n + 2, :], start=True, stop=True)
                        mm.then_inc(s_s, 1)

                    def pv(i, s):
                        c, kt = s // KT, s % KT
                        pe.wait_ge(s_e, i.at(STEPS, s + 1))
                        if s == 0:
                            pe.wait_ge(s_v0, i.at(1, 1))
                        if s % 4 == 0:
                            after(pe, s_oc, i.at(2, s // 4))
                        for j in range(HC):
                            mm = pe.matmul(ps_o[SL * j:SL * (j + 1), (c % 2) * T:(c % 2 + 1) * T],
                                           V0[:, i.slot(2), kt, HC * c + j, :], PT[:, s % NPT, j, :],
                                           start=(kt == 0), stop=(kt == KT - 1))
                        mm.then_inc(s_pv, 1)

                    def max_transposed(i):
                        pe.wait_ge(s_mp, i.at(2, 2))
                        after(pe, s_n, i.at(KT, -2 * KT))
                        for t in range(KT):
                            mm = pe.transpose(ps_x[0:2 * H, t * P:(t + 1) * P],
                                              mparts[:, i.slot(2), t, :, :].bitcast(F32).rearrange("p l h -> p (l h)"),
                                              ident[:, :])
                        mm.then_inc(s_mtp, 1)

                    def out_transposed(i, t, other):
                        if t == 0:
                            pe.wait_ge(s_oc, i.at(2, 2))
                            if other:
                                pe.wait_ge(s_mT, other.at(1, 1))
                        after(pe, s_n, i.at(KT, t))
                        for c in range(NC):
                            mm = pe.transpose(ps_x[:, c * P:(c + 1) * P], OT[:, c, t * P:(t + 1) * P],
                                              ident[:, :])
                        mm.then_inc(s_ot, 1)

                    def step(at):
                        ia, im, ib, io = at(1), at(2), at(3), at(4)
                        if ia:
                            b = ia.slot(NBUF)
                            pe.wait_ge(s_ld[b], ia.turn(NBUF) * LOADS + LOADS)
                        if ib:
                            b = ib.slot(NBUF)
                            pe.wait_ge(s_mr[b], ib.turn(NBUF) * 64 + 64)
                        for s in range(STEPS):
                            if ia:
                                pass_a(ia, 2 * s)
                            if ib:
                                scores(ib, s)
                            if ia:
                                pass_a(ia, 2 * s + 1)
                            if im and s == 2:
                                max_transposed(im)
                            if ib and s >= 2:
                                pv(ib, s - 2)
                            elif io and s < 2:
                                pv(io, STEPS - 2 + s)
                            if io and s in (3, 5):
                                out_transposed(io, (s - 3) // 2, im if s == 3 else None)
                    pipeline(pe, B, DEPTH, NBUF, step)

                @block.scalar
                def _(act):
                    def o_copied(i, n):
                        act.wait_ge(s_pv, i.at(STEPS, 4 * n + 4))
                        if n == 0:
                            after(act, s_ot, i.at(KT))
                        act.activation(OT[:, 2 * n:2 * n + 2, :],
                                       ps_o[:, :].rearrange("p (c t) -> p c t", c=2), ACT.Copy)\
                            .then_inc(s_oc, 1)

                    def step(at):
                        im, ib, io = at(2), at(3), at(4)
                        for s in range(STEPS):
                            if ib:
                                act.wait_ge(s_s, ib.at(STEPS, s + 1))
                                after(act, s_pv, ib.at(STEPS, s - 1 if s < 2 else s - NPT + 1))
                                act.activation(PT[:, s % NPT, :, :], ps_s[s % 2][:, :, :], ACT.Exp, scale=SCALE)\
                                    .then_inc(s_e, 1)
                            if im and s == 2:
                                act.wait_ge(s_mtp, im.at(1, 1))
                                after(act, s_md, im.at(16, -16))
                                act.activation(mT[:, im.slot(2), :], ps_x[0:2 * H, 0:T], ACT.Copy).then_inc(s_mT, 1)
                            if ib and s == 5:
                                o_copied(ib, 0)
                            if io and s == 1:
                                o_copied(io, 1)
                    pipeline(act, B, DEPTH, NBUF, step)

                @block.vector
                def _(dve):
                    def normalise(i, t):
                        dve.wait_ge(s_ot, i.at(KT, t + 1))
                        o = ps_x[:, :].rearrange("p (h s) -> p h s", h=H)
                        dve.reciprocal(rsum[:, t, :], o[:, :, DH]).then_inc(s_rc, 1)
                        dve.wait_ge(s_rc, i.at(KT, t + 1))
                        dst = aall[:, bass.ds(i.at(KT, t), 1), :].rearrange("p o (h d) -> p (o h) d", h=H)
                        dve.tensor_tensor(dst, o[:, :, 0:DH],
                                          rsum[:, t, :].unsqueeze(2).broadcast_to([P, H, DH]),
                                          ALU.mult).then_inc(s_n, 1)

                    def step(at):
                        ia, io = at(1), at(4)
                        for k in range(2 * STEPS):
                            if ia:
                                t, h = k // 8, 2 * (k % 8)
                                dve.wait_ge(s_a, ia.at(16, k + 1))
                                if k == 0:
                                    after(dve, s_mp, ia.at(2))
                                dve.tensor_reduce(nmax[:, t, h:h + 2],
                                                  ps_a[k % 2][:, :].rearrange("p (n t) -> p n t", n=2), AX.X, ALU.max, negate=True).then_inc(s_mx, 1)
                            if io and k in (7, 11):
                                normalise(io, (k - 7) // 4)
                        if ia:
                            b = ia.slot(2)
                            dve.wait_ge(s_mx, ia.at(16, 16))
                            after(dve, s_mtp, ia.at(1, -1))
                            dve.tensor_copy(mparts[:, b, :, 0, :], nmax[:, :, :]).then_inc(s_mp, 1)
                            dve.wait_ge(s_mp, ia.at(2, 1))
                            dve.tensor_tensor(mparts[:, b, :, 1, :], nmax[:, :, :], mparts[:, b, :, 0, :],
                                              ALU.subtract).then_inc(s_mp, 1)
                    pipeline(dve, B, DEPTH, NBUF, step)

        c3.close()

        with ExitStack() as c2:
            sb2, pb2, sem2 = scope(nc, c2, "l0mix")
            G = 2 * KT
            N = G * P
            ln1, ln2, ln3 = (Norm((sb2, sem2), f"ln_c{k}", G, gates, shifted=k != 2) for k in (1, 2, 3))
            an = sb2("an", [P, 2, G, D], F32)
            aT = sb2("aT", [P, 2, N], F32)
            y = sb2("y", [P, 2, G, D], F32)
            z = sb2("z", [P, 2, G, D], F32)
            xn = sb2("xn", [P, 2, G, D], F32)
            xT = sb2("xT", [P, 2, 2, T + 1], F32)
            prev = sb2("prev", [P, 2, 2, N], F32)
            mix = sb2("mix", [P, 2, 2, N], F32)
            kr = sb2("kr", [P, 2, N], F32)
            k2 = sb2("k2", [P, 2, N], F32)
            sg = sb2("sg", [P, 2, G, D], F32)
            f = sb2("f", [P, 2, G, D], F32)
            ps_at = pb2("ps_at")
            ps_y = [pb2(f"ps_y{i}") for i in range(2)]
            ps_xt, ps_k, ps_r = pb2("ps_xt"), pb2("ps_k"), pb2("ps_r")
            ps_kv = [pb2(f"ps_kv{i}") for i in range(2)]
            names = "an at aT y yn x1 xn tp xT pv mix k r kr k2 sg kv f fn x2".split()
            s = {n: sem2(f"s_{n}") for n in names}
            DEPTH = 8

            def g3(ap):
                return ap.rearrange("p (g d) -> p g d", g=G)

            with nc.Block() as block:
                @block.sync
                def _(sp):
                    H1 = 16
                    Wq, Wk, Wv, Wo = next_weights
                    DH1 = Wq.shape[0] // H1
                    natural = layer1_natural(vall, H1, Wq.shape[0], D)
                    for w, nat in zip((Wq, Wk), natural):
                        sp.dma_start(nat, w.rearrange("(h r) d -> r h d", r=DH1)).then_inc(s_next, 16)
                    sp.dma_start(natural[2], Wv.rearrange("(c p) d -> p c d", p=P)).then_inc(s_next, 16)
                    sp.dma_start(natural[3], Wo).then_inc(s_next, 16)

                @block.tensor
                def _(pe):
                    def step(at):
                        if i := at(1):
                            b = i.slot(2)
                            pe.wait_ge(s["aT"], i.at(1, 1))
                            after(pe, s["yn"], i.at(G, -G))
                            for j in range(G):
                                mm = pe.matmul(ps_y[b][:, j * P:(j + 1) * P], aT[:, b, j * P:(j + 1) * P],
                                               WT[:, 0, :], start=True, stop=True)
                            mm.then_inc(s["y"], 1)
                        if i := at(4):
                            b = i.slot(2)
                            pe.wait_ge(s["mix"], i.at(2, 2))
                            after(pe, s["kr"], i.at(1))
                            pe.matmul(ps_k[:, :], WT[:, 2, :], mix[:, b, 1, :], start=True, stop=True)\
                                .then_inc(s["k"], 1)
                            after(pe, s["sg"], i.at(1))
                            for j in range(G):
                                mm = pe.matmul(ps_r[:, j * P:(j + 1) * P], mix[:, b, 0, j * P:(j + 1) * P],
                                               WT[:, 1, :], start=True, stop=True)
                            mm.then_inc(s["r"], 1)
                        if i := at(5):
                            b = i.slot(2)
                            pe.wait_ge(s["k2"], i.at(1, 1))
                            after(pe, s["f"], i.at(1, -1))
                            for j in range(G):
                                mm = pe.matmul(ps_kv[b][:, j * P:(j + 1) * P], k2[:, b, j * P:(j + 1) * P],
                                               WT[:, 3, :], start=True, stop=True)
                            mm.then_inc(s["kv"], 1)
                        if i := at(3):
                            b = i.slot(2)
                            pe.wait_ge(s["xn"], i.at(G, G))
                            after(pe, s["xT"], i.at(1))
                            for j in range(G):
                                mm = pe.transpose(ps_xt[:, j * P:(j + 1) * P], xn[:, b, j, :], ident[:, :])
                            mm.then_inc(s["tp"], 1)
                        if i := at(0):
                            pe.wait_ge(s["an"], i.at(1, 1))
                            after(pe, s["aT"], i.at(1))
                            for j in range(G):
                                mm = pe.transpose(ps_at[:, j * P:(j + 1) * P],
                                                  an[:, i.slot(2), j, :], ident[:, :])
                            mm.then_inc(s["at"], 1)
                    pipeline(pe, NT // G, DEPTH, 2, step)

                @block.scalar
                def _(act):
                    def step(at):
                        if i := at(0):
                            after(act, s["at"], i.at(1, -1))
                            act.activation(an[:, i.slot(2), :, :], aall[:, tiles(i, G), :], ACT.Copy)\
                                .then_inc(s["an"], 1)
                        if i := at(2):
                            b = i.slot(2)
                            after(act, s["x1"], i.at(1, -1))
                            ln1.apply_scaled(act, i, lambda j: y[:, b, j, :],
                                             lambda j: ps_y[b][:, j * P:(j + 1) * P], s["yn"])
                        if i := at(7):
                            b = i.slot(2)
                            after(act, s["x2"], i.at(1, -1))
                            ln3.apply_scaled(act, i, lambda j: z[:, b, j, :], lambda j: f[:, b, j, :], s["fn"])
                        if i := at(5):
                            b = i.slot(2)
                            act.wait_ge(s["kr"], i.at(1, 1))
                            after(act, s["kv"], i.at(1, -1))
                            act.activation(k2[:, b, :], kr[:, b, :], ACT.Square).then_inc(s["k2"], 1)
                        if i := at(4):
                            b = i.slot(2)
                            act.wait_ge(s["k"], i.at(1, 1))
                            after(act, s["k2"], i.at(1, -1))
                            act.activation(kr[:, b, :], ps_k[:, :], ACT.Relu).then_inc(s["kr"], 1)
                            act.wait_ge(s["r"], i.at(1, 1))
                            after(act, s["f"], i.at(1, -1))
                            act.activation(sg[:, b, :, :], g3(ps_r[:, :]), ACT.Sigmoid).then_inc(s["sg"], 1)
                        if i := at(3):
                            b = i.slot(2)
                            act.wait_ge(s["tp"], i.at(1, 1))
                            after(act, s["mix"], i.at(2, -2))
                            act.activation(xT[:, b, :, 1:T + 1], ps_xt[:, :].rearrange("p (c t) -> p c t", c=2),
                                           ACT.Copy).then_inc(s["xT"], 1)
                        if i := at(3):
                            b = i.slot(2)
                            act.wait_ge(s["xT"], i.at(1, 1))
                            for n in range(2):
                                act.activation(prev[:, b, n, :].rearrange("p (c t) -> p c t", c=2),
                                               xT[:, b, :, 0:T], ACT.Copy, scale=omu[:, n:n + 1])\
                                    .then_inc(s["pv"], 1)
                        if i := at(0):
                            b = i.slot(2)
                            act.wait_ge(s["at"], i.at(1, 1))
                            after(act, s["y"], i.at(1, -1))
                            act.activation(aT[:, b, :], ps_at[:, :], ACT.Copy).then_inc(s["aT"], 1)
                    pipeline(act, NT // G, DEPTH, 2, step)

                @block.gpsimd
                def _(pool):
                    def step(at):
                        if i := at(6):
                            ln3.rstd(pool, i, neghalf, eps)
                            ln3.shift(pool, i)
                        if i := at(2):
                            ln2.rstd(pool, i, neghalf, eps)
                        if i := at(1):
                            ln1.rstd(pool, i, neghalf, eps)
                            ln1.shift(pool, i)
                    pool.memset(xT[:, :, :, 0:1], 0.0)
                    pipeline(pool, NT // G, DEPTH, 2, step)

                @block.vector
                def _(dve):
                    def step(at):
                        if i := at(6):
                            b = i.slot(2)
                            dve.wait_ge(s["kv"], i.at(1, 1))
                            dve.wait_ge(s["sg"], i.at(1, 1))
                            dve.tensor_tensor(f[:, b, :, :], g3(ps_kv[b][:, :]), sg[:, b, :, :], ALU.mult)\
                                .then_inc(s["f"], 1)
                        if i := at(4):
                            b = i.slot(2)
                            dve.wait_ge(s["pv"], i.at(2, 2))
                            after(dve, s["r"], i.at(1, -1))
                            for n in range(2):
                                dve.scalar_tensor_tensor(mix[:, b, n, :].rearrange("p (c t) -> p c t", c=2),
                                                         xT[:, b, :, 1:T + 1], mu[:, n:n + 1],
                                                         prev[:, b, n, :].rearrange("p (c t) -> p c t", c=2),
                                                         ALU.mult, ALU.add).then_inc(s["mix"], 1)
                        if i := at(6):
                            gates.wait(dve, gates.dve, s["f"], i.at(1, 1))
                            ln3.stats(dve, i, lambda j: f[:, i.slot(2), j, :])
                        if i := at(3):
                            b = i.slot(2)
                            ln2.ready(dve, i)
                            after(dve, s["tp"], i.at(1, -1))
                            ln2.apply(dve, i, lambda j: xn[:, b, j, :], lambda j: xs[:, i.at(G, j), :], s["xn"])
                        if i := at(7):
                            b = i.slot(2)
                            dve.wait_ge(s["fn"], i.at(G, G))
                            dve.tensor_tensor(xs[:, tiles(i, G), :], xs[:, tiles(i, G), :], z[:, b, :, :],
                                              ALU.add).then_inc(s["x2"], 1)
                        if i := at(2):
                            b = i.slot(2)
                            dve.wait_ge(s["yn"], i.at(G, G))
                            dve.tensor_tensor(xs[:, tiles(i, G), :], xs[:, tiles(i, G), :], y[:, b, :, :],
                                              ALU.add).then_inc(s["x1"], 1)
                            gates.wait(dve, gates.dve, s["x1"], i.at(1, 1))
                            ln2.stats(dve, i, lambda j: xs[:, i.at(G, j), :])
                        if i := at(1):
                            b = i.slot(2)
                            gates.wait(dve, gates.dve, s["y"], i.at(1, 1))
                            ln1.stats(dve, i, lambda j: ps_y[b][:, j * P:(j + 1) * P])
                    pipeline(dve, NT // G, DEPTH, 2, step)


def split_matmul(pe, out, w, x, start=True, stop=True):
    pe.matmul(out, w[0], x[0], start=start, stop=False)
    pe.matmul(out, w[0], x[1], start=False, stop=False)
    return pe.matmul(out, w[1], x[0], start=False, stop=stop)


def layer1_attention(nc, gates, xs, ident, neghalf, spare, s_next, Wq, Wk, Wv, Wo, w_fc, w_proj, B, T, D, NT, KT, eps):
    H = 16
    F = Wq.shape[0]
    DH = F // H
    NP = H // 2
    CLAMP = 50.0
    SCALE = float(DH) ** -0.5
    W0, W = 2 * T, 2 * T + 2 * P
    with ExitStack() as ctx:
        sb, pb, sem = scope(nc, ctx, "l1")
        mh = sb("mh", [P, H, D], F32R)
        ml = sb("ml", [P, H, D], F32R)
        vh = sb("vh", [P, F], F32R)
        vl = sb("vl", [P, F], F32R)
        woT = sb("woT", [P, NP, D], F32)
        cols = sb("cols", [P, 4, 32], F32)
        sel = sb("sel", [P, NP, P], F32R)
        low = sb("low", [P, 1], F32)

        with ExitStack() as c2:
            sb2, pb2, sem2 = scope(nc, c2, "l1w")
            natq, natk, natv, wo = layer1_natural(spare, H, F, D)
            self32 = sb2("self32", [P, NP, P], F32)
            low_of = sb2("low_of", [P, H], F32)
            ps = [pb2(f"ps{i}") for i in range(4)]
            s_pe, s_hi, s_lo = sem2("s_pe"), sem2("s_hi"), sem2("s_lo")
            s_c, s_sel = sem2("s_c"), sem2("s_sel")
            GM = H // 4
            GV = NP // 4

            def parts(g):
                if g < GM:
                    return tuple(w[:, 4 * g:4 * g + 4, :].rearrange("p n d -> p (n d)") for w in (mh, ml))
                c = 512 * (g - GM)
                return vh[:, c:c + 512], vl[:, c:c + 512]

            with nc.Block() as block:
                @block.gpsimd
                def _(pool):
                    pool.memset(cols[:, :, 0:8], 0.0).then_inc(s_c, 1)
                    pool.memset(cols[:, :, 8:32], 1.0)
                    pool.memset(self32[:, :, :], 0.0).then_inc(s_c, 1)
                    pool.memset(low_of[:, :], 0.0).then_inc(s_c, 1)
                    pool.wait_ge(s_c, 3)
                    for c in range(4):
                        pool.memset(cols[:, c, c:c + 5:4], 1.0)
                    for part in range(2):
                        for h in range(H):
                            row = 32 * (h % 4) + h // 4 + 4 * part
                            o = self32[:, h // 2, (h % 2) * DH:(h % 2 + 1) * DH]
                            last = pool.affine_select(out=o, in_=o, compare_op=ALU.not_equal, fill=1.0, base=-row,
                                                      pattern=[[0, DH]], channel_multiplier=1)
                            if part:
                                o = low_of[:, h:h + 1]
                                last = pool.affine_select(out=o, in_=o, compare_op=ALU.not_equal, fill=-1.0,
                                                          base=-row, pattern=[[0, 1]], channel_multiplier=1)
                        last.then_inc(s_sel, 1)
                        pool.wait_ge(s_sel, part + 1)

                @block.tensor
                def _(pe):
                    pe.wait_ge(s_next, 64)
                    for g in range(GM + 2 * GV):
                        if g >= 4:
                            pe.wait_ge(s_lo, g - 3)
                        for n in range(4):
                            o = ps[g % 4][:, n * P:(n + 1) * P]
                            c = 4 * (g - GM) + n
                            if g < GM:
                                mm = pe.matmul(o, natq[:, 4 * g + n, :], natk[:, 4 * g + n, :], start=True, stop=True)
                            elif g < GM + GV:
                                mm = pe.transpose(o, natv[:, c, :], ident[:, :])
                            else:
                                mm = pe.transpose(o, wo[:, (c - NP) * P:(c - NP + 1) * P], ident[:, :])
                        mm.then_inc(s_pe, 1)

                @block.scalar
                def _(act):
                    for g in range(GM + GV):
                        act.wait_ge(s_pe, g + 1)
                        act.activation(parts(g)[0], ps[g % 4][:, :], ACT.Copy).then_inc(s_hi, 1)

                @block.vector
                def _(dve):
                    for g in range(GM + GV):
                        dve.wait_ge(s_hi, g + 1)
                        dve.tensor_tensor(parts(g)[1], ps[g % 4][:, :], parts(g)[0],
                                          ALU.subtract).then_inc(s_lo, 1)
                    for g in range(GV):
                        dve.wait_ge(s_pe, GM + GV + g + 1)
                        dve.tensor_copy(woT[:, 4 * g:4 * g + 4, :],
                                        ps[(GM + GV + g) % 4][:, :].rearrange("p (n d) -> p n d", n=4))
                    dve.wait_ge(s_sel, 2)
                    dve.tensor_copy(sel[:, :, :], self32[:, :, :])
                    dve.tensor_reduce(low[:, :], low_of[:, :], AX.X, ALU.add)

        with ExitStack() as c2:
            sb2, pb2, sem2 = scope(nc, c2, "l1att")
            ln = Norm((sb2, sem2), "l1_ln", KT, gates)
            ln2 = Norm((sb2, sem2), "l1_ln2", KT, gates)
            xn = sb2("xn", [P, 2, KT, D], F32)
            xh = sb2("xh", [P, 3, T], F32R)
            xl = sb2("xl", [P, 3, T], F32R)
            tH = sb2("tH", [P, NP, 2, T], F32R)
            tL = sb2("tL", [P, NP, 2, T], F32R)
            V = sb2("V", [P, 2, KT, F], F32)
            th = sb2("th", [P, 2, W], F32)
            pt = sb2("pt", [P, 4, W], F32)
            both = sb2("both", [P, 2, 2, P], F32)
            oraw = sb2("oraw", [P, 2, NP, T], F32)
            on = sb2("on", [P, 2, 2, T], F32)
            sums = sb2("sums", [P, T], F32)
            rec = sb2("rec", [P, 2, T], F32)
            rh = sb2("rh", [P, 2, T], F32R)
            rp = sb2("rp", [P, 2, T], F32R)
            y = sb2("y", [P, 2, KT, D], F32)
            z = sb2("z", [P, 2, KT, D], F32)
            ps_s = c2.enter_context(nc.psum_tensor("l1att_ps_s", [P, 1024], F32))
            ps_t, ps_j = pb2("ps_t"), pb2("ps_j")
            ps_o = [pb2(f"ps_o{i}") for i in range(2)]
            ps_sum, ps_y = pb2("ps_sum"), pb2("ps_y")
            names = "xn tp xh xl t tH tL v vc sc th ex mk ad pv oc sum rec rh rp r on y yc yn x".split()
            s = {n: sem2(f"s_{n}") for n in names}
            DEPTH = 7
            UNROLL = 6

            with nc.Block() as block:
                @block.sync
                def _(sp):
                    for e in range(w_fc.shape[0]):
                        fc, pr = expert_natural(spare, e, w_fc.shape[1] // P)
                        sp.dma_start(fc, w_fc[e].rearrange("(c p) d -> p c d", p=P)).then_inc(s_next, 16)
                        sp.dma_start(pr, w_proj[e].rearrange("d (c p) -> d c p", p=P)).then_inc(s_next, 16)

                @block.tensor
                def _(pe):
                    def scores(i, p):
                        b = i.slot(3)
                        after(pe, s["th"], i.at(NP, p))
                        if p == 0:
                            pe.wait_ge(s["tL"], i.at(NP, NP))
                        split_matmul(pe, ps_s[:, 0:W0], (xh[:, b, 0:P], xl[:, b, 0:P]),
                                     (tH[:, p, :, :], tL[:, p, :, :]))
                        split_matmul(pe, ps_s[:, W0:W], (xh[:, b, P:T], xl[:, b, P:T]),
                                     (tH[:, p, :, P:T], tL[:, p, :, P:T])).then_inc(s["sc"], 1)

                    def project(i, p):
                        b = i.slot(3)
                        if p == 0:
                            pe.wait_ge(s["xl"], i.at(1, 1))
                        after(pe, s["tL"], i.at(NP, p))
                        for hh in range(2):
                            mm = split_matmul(pe, ps_t[:, hh * T:(hh + 1) * T],
                                              (mh[:, 2 * p + hh, :], ml[:, 2 * p + hh, :]),
                                              (xh[:, b, :], xl[:, b, :]))
                        mm.then_inc(s["t"], 1)

                    def values(i, u, io):
                        b, kt, half = i.slot(3), u // 2, u % 2
                        if io:
                            pe.wait_ge(s["on"], io.at(4, u + 1))
                        elif u:
                            pe.wait_ge(s["vc"], i.at(4, u))
                        else:
                            pe.wait_ge(s["xl"], i.at(1, 2))
                        c = slice(kt * P, (kt + 1) * P)
                        f = slice(half * 512, (half + 1) * 512)
                        split_matmul(pe, ps_j[:, :], (xh[:, b, c], xl[:, b, c]), (vh[:, f], vl[:, f]))\
                            .then_inc(s["v"], 1)

                    def spread(i, u, ip, ix):
                        if u == 0:
                            pe.wait_ge(s["rp"], i.at(1, 1))
                            if ix:
                                pe.wait_ge(s["xl"], ix.at(1, 1))
                            else:
                                pe.wait_ge(s["vc"], min(i.at(4, 12), 4 * B))
                        if not ix or not ip:
                            after(pe, s["on"], i.at(4, u))
                        if ip and u:
                            pe.wait_ge(s["vc"], ip.at(4, u))
                        for n in range(2):
                            mm = pe.matmul(ps_j[:, n * T:(n + 1) * T], sel[:, 2 * u + n, :], rp[:, i.slot(2), :],
                                           start=True, stop=True)
                        mm.then_inc(s["r"], 1)

                    def project_out(i, u):
                        pe.wait_ge(s["on"], i.at(4, u + 1))
                        if u == 0:
                            after(pe, s["yc"], i.at(1))
                        for n in range(2):
                            for t in range(KT):
                                mm = pe.matmul(ps_y[:, t * P:(t + 1) * P], on[:, u % 2, n, t * P:(t + 1) * P],
                                               woT[:, 2 * u + n, :], start=(u == 0 and n == 0 and t == 0),
                                               stop=(u == 3 and n == 1), skip_group_check=True)
                        mm.then_inc(s["y"], 1)

                    def pv(i, p):
                        b = i.slot(2)
                        pe.wait_ge(s["mk"], i.at(NP, p + 1))
                        if p % 2 == 0:
                            after(pe, s["oc"], i.at(4, p // 2 - 1))
                        if p == 0:
                            pe.wait_ge(s["vc"], i.at(4, 4))
                        o, c = ps_o[p // 2 % 2], p % 2 * T

                        def probs(kt, hh):
                            at, n = (hh * T, T) if kt == 0 else (W0 + hh * P, P)
                            return pt[:, p % 4, at:at + n]

                        for kt in range(KT):
                            for hh in range(2):
                                h = 2 * p + hh
                                pe.matmul(o[hh * DH:(hh + 1) * DH, c + kt * P:c + T], V[:, b, kt, h * DH:(h + 1) * DH],
                                          probs(kt, hh), start=(kt == 0), stop=(kt == 1), skip_group_check=True)

                    def probability_sums(i, p):
                        pe.wait_ge(s["ad"], i.at(NP, p + 1))
                        if p == 0:
                            after(pe, s["sum"], i.at(1))
                        for hh in range(2):
                            h = 2 * p + hh
                            j = 32 * (h % 4)
                            for half, m in enumerate((pt[:, p % 4, hh * T:hh * T + P], both[:, p % 2, hh, :])):
                                mm = pe.matmul(ps_sum[j:j + 32, half * P:(half + 1) * P], cols[:, h // 4, :], m,
                                               start=(h < 4 and half == 0), stop=(h >= 12),
                                               skip_group_check=True)
                        mm.then_inc(s["pv"], 1)

                    def turned(i):
                        pe.wait_ge(s["xn"], i.at(KT, KT))
                        after(pe, s["vc"], i.at(4, -4))
                        for j in range(KT):
                            mm = pe.transpose(ps_j[:, j * P:(j + 1) * P], xn[:, i.slot(2), j, :], ident[:, :])
                        mm.then_inc(s["tp"], 1)

                    def step(at):
                        ix, ip, ic, il, io = at(1), at(2), at(3), at(4), at(5)
                        if ix:
                            turned(ix)
                        for p in range(NP):
                            if ic:
                                scores(ic, p)
                            if ic and p >= 2:
                                pv(ic, p - 2)
                            if il and p < 2:
                                pv(il, NP - 2 + p)
                            if ip:
                                project(ip, p)
                            if ic and p >= 2:
                                probability_sums(ic, p - 2)
                            if il and p < 2:
                                probability_sums(il, NP - 2 + p)
                            if p % 2 == 0:
                                if io:
                                    spread(io, p // 2, ip, ix)
                            else:
                                if ip:
                                    values(ip, p // 2, io)
                                if io:
                                    project_out(io, p // 2)
                    pipeline(pe, B, DEPTH, UNROLL, step)

                @block.scalar
                def _(act):
                    def probabilities(i, p):
                        if p < NP:
                            act.wait_ge(s["sc"], i.at(NP, p + 1))
                            after(act, s["ex"], i.at(NP, p - 1))
                            act.activation(th[:, p % 2, :], ps_s[:, 0:W], ACT.Tanh, scale=SCALE / CLAMP)\
                                .then_inc(s["th"], 1)
                        if p:
                            act.wait_ge(s["th"], i.at(NP, p))
                            after(act, s["pv"], i.at(NP, p - 4))
                            act.activation(pt[:, (p - 1) % 4, :], th[:, (p - 1) % 2, :], ACT.Exp, scale=CLAMP)\
                                .then_inc(s["ex"], 1)

                    def step(at):
                        ix, ip, ic, il, iy = at(1), at(2), at(3), at(4), at(6)
                        if iy:
                            act.wait_ge(s["y"], iy.at(4, 4))
                            after(act, s["yn"], iy.at(KT, -KT))
                            act.activation(y[:, iy.slot(2), :, :], ps_y[:, 0:T].rearrange("p (t d) -> p t d", t=KT),
                                           ACT.Copy).then_inc(s["yc"], 1)
                        if ix:
                            act.wait_ge(s["tp"], ix.at(1, 1))
                            after(act, s["sc"], ix.at(NP, -2 * NP))
                            act.activation(xh[:, ix.slot(3), :], ps_j[:, 0:T], ACT.Copy).then_inc(s["xh"], 1)
                        for p in range(NP + 1):
                            if ic:
                                probabilities(ic, p)
                            if ip and p < NP:
                                act.wait_ge(s["t"], ip.at(NP, p + 1))
                                after(act, s["sc"], ip.at(NP, p + 1 - NP))
                                act.activation(tH[:, p, :, :], ps_t[:, :].rearrange("p (n t) -> p n t", n=2),
                                               ACT.Copy).then_inc(s["tH"], 1)
                            if ip and p < NP and p % 2:
                                u = p // 2
                                b, kt, half = ip.slot(2), u // 2, u % 2
                                act.wait_ge(s["v"], ip.at(4, u + 1))
                                if u == 0:
                                    after(act, s["pv"], ip.at(NP, -NP))
                                act.activation(V[:, b, kt, half * 512:(half + 1) * 512], ps_j[:, :], ACT.Copy)\
                                    .then_inc(s["vc"], 1)
                            if il and p == 1:
                                act.wait_ge(s["pv"], il.at(NP, NP))
                                after(act, s["rec"], il.at(1))
                                act.activation(sums[:, :], ps_sum[:, 0:T], ACT.Copy).then_inc(s["sum"], 1)
                    pipeline(act, B, DEPTH, UNROLL, step)

                @block.gpsimd
                def _(pool):
                    def masked(i, p):
                        gates.wait(pool, gates.pool, s["ex"], i.at(NP, p + 1))
                        for d in (pt[:, p % 4, 0:W0].rearrange("p (h t) -> p h t", h=2)[:, :, 0:P],
                                  pt[:, p % 4, W0:W].rearrange("p (h t) -> p h t", h=2)):
                            last = pool.affine_select(out=d, in_=d, compare_op=ALU.is_ge, fill=0.0, base=0,
                                                      pattern=[[0, 2], [1, P]], channel_multiplier=-1)
                        last.then_inc(s["mk"], 1)

                    def step(at):
                        i0, ic, iy = at(0), at(3), at(6)
                        for p in range(NP):
                            if p == 6 and iy:
                                ln2.rstd(pool, iy, neghalf, eps)
                            if p == 4 and i0:
                                ln.rstd(pool, i0, neghalf, eps)
                            if ic:
                                masked(ic, p)
                    pipeline(pool, B, DEPTH, UNROLL, step)

                @block.vector
                def _(dve):
                    def copied(i, u):
                        dve.wait_ge(s["pv"], i.at(NP, 2 * u + 2))
                        dve.tensor_copy(oraw[:, i.slot(2), 2 * u:2 * u + 2, :],
                                        ps_o[u % 2][:, :].rearrange("p (n t) -> p n t", n=2)).then_inc(s["oc"], 1)

                    def added(i, p):
                        dve.wait_ge(s["mk"], i.at(NP, p + 1))
                        after(dve, s["pv"], i.at(NP, p - 1))
                        dve.tensor_tensor(both[:, p % 2, :, :],
                                          pt[:, p % 4, 0:W0].rearrange("p (h t) -> p h t", h=2)[:, :, P:T],
                                          pt[:, p % 4, W0:W].rearrange("p (h t) -> p h t", h=2), ALU.add)\
                            .then_inc(s["ad"], 1)

                    def step(at):
                        i0, ix, ip, ic, il, io, iy = (at(k) for k in range(7))
                        if ix:
                            b = ix.slot(3)
                            dve.wait_ge(s["xh"], ix.at(1, 1))
                            dve.tensor_tensor(xl[:, b, :], ps_j[:, 0:T], xh[:, b, :], ALU.subtract)\
                                .then_inc(s["xl"], 1)
                        for p in range(NP):
                            if ip:
                                dve.wait_ge(s["tH"], ip.at(NP, p + 1))
                                dve.tensor_tensor(tL[:, p, :, :], ps_t[:, :].rearrange("p (n t) -> p n t", n=2),
                                                  tH[:, p, :, :], ALU.subtract).then_inc(s["tL"], 1)
                            if io and p % 2 == 0:
                                u = p // 2
                                dve.wait_ge(s["r"], io.at(4, u + 1))
                                after(dve, s["y"], io.at(4, u - 1))
                                dve.tensor_tensor(on[:, u % 2, :, :], ps_j[:, :].rearrange("p (n t) -> p n t", n=2),
                                                  oraw[:, io.slot(2), 2 * u:2 * u + 2, :], ALU.mult)\
                                    .then_inc(s["on"], 1)
                            if ic and p:
                                added(ic, p - 1)
                            if il and p == 0:
                                added(il, NP - 1)
                            if il and p == 1:
                                dve.wait_ge(s["sum"], il.at(1, 1))
                                dve.reciprocal(rec[:, il.slot(2), :], sums[:, :]).then_inc(s["rec"], 1)
                            if il and p == 2:
                                copied(il, 3)
                                dve.wait_ge(s["rec"], il.at(1, 1))
                                after(dve, s["r"], il.at(4, -4))
                                dve.tensor_copy(rh[:, il.slot(2), :], rec[:, il.slot(2), :]).then_inc(s["rh"], 1)
                            if ic and p >= 3 and p % 2:
                                copied(ic, (p - 3) // 2)
                            if il and p == 3:
                                b = il.slot(2)
                                dve.wait_ge(s["rh"], il.at(1, 1))
                                dve.scalar_tensor_tensor(rp[:, b, :], rh[:, b, :], low[:, 0:1], rec[:, b, :],
                                                         ALU.mult, ALU.add).then_inc(s["rp"], 1)
                            if iy and p == 5:
                                gates.wait(dve, gates.dve, s["yc"], iy.at(1, 1))
                                ln2.stats(dve, iy, lambda j: y[:, iy.slot(2), j, :])
                            if iy and p == 7:
                                b = iy.slot(2)
                                ln2.ready(dve, iy)
                                ln2.apply(dve, iy, lambda j: z[:, b, j, :], lambda j: y[:, b, j, :], s["yn"])
                            if iy and p == 7:
                                dve.wait_ge(s["yn"], iy.at(KT, KT))
                                dve.tensor_tensor(xs[:, tiles(iy, KT), :], xs[:, tiles(iy, KT), :],
                                                  z[:, iy.slot(2), :, :], ALU.add).then_inc(s["x"], 1)
                            if i0 and p == 3:
                                ln.stats(dve, i0, lambda j: xs[:, i0.at(KT, j), :])
                            if i0 and p == 5:
                                ln.ready(dve, i0)
                                after(dve, s["tp"], i0.at(1, -1))
                                ln.apply(dve, i0, lambda j: xn[:, i0.slot(2), j, :],
                                         lambda j: xs[:, i0.at(KT, j), :], s["xn"])
                    pipeline(dve, B, DEPTH, UNROLL, step)


def layer1_experts(nc, gates, xs, ident, neghalf, spare, s_next, router_w, w_fc, w_proj, shared_fc, shared_proj,
                   out_dram, B, T, D, NT, E, eps):
    F = w_fc.shape[1]
    NF = F // P
    NE = E + 1
    G = 4
    N = G * P
    with ExitStack() as ctx:
        sb, pb, sem = scope(nc, ctx, "moe")
        fh = sb("fh", [P, NE, F], F32R)
        fl = sb("fl", [P, NE, F], F32R)
        pT = sb("pT", [P, NE, NF, D], F32)
        rT = sb("rT", [P, E], F32)
        iota = sb("iota", [P, G, E], F32)

        with ExitStack() as c2:
            sb2, pb2, sem2 = scope(nc, c2, "moew")
            shared = sb2("shared", [P, 2, NF, D], F32)

            def natural(e):
                return expert_natural(spare, e, NF) if e < E else (shared[:, 0, :, :], shared[:, 1, :, :])

            rw = sb2("rw", [E, D], F32)
            ii = sb2("ii", [P, G, E], mybir.dt.int32)
            ps_f = [pb2(f"ps_f{i}") for i in range(2)]
            ps_p = [pb2(f"ps_p{i}") for i in range(2)]
            ps_r = pb2("ps_r")
            s_w = sem2("s_w")
            s_r, s_rp, s_io = sem2("s_r"), sem2("s_rp"), sem2("s_io")
            s_f, s_p, s_hi, s_lo, s_pc = (sem2(n) for n in "s_f s_p s_hi s_lo s_pc".split())
            with nc.Block() as block:
                @block.sync
                def _(sp):
                    sp.dma_start(rw[:, :], router_w).then_inc(s_r, 16)
                    sp.dma_start(shared[:, 0, :, :], shared_fc.rearrange("(c p) d -> p c d", p=P)).then_inc(s_w, 16)
                    sp.dma_start(shared[:, 1, :, :], shared_proj.rearrange("d (c p) -> d c p", p=P)).then_inc(s_w, 16)

                @block.gpsimd
                def _(pool):
                    pool.iota(ii[:, :, :], [[0, G], [1, E]], base=0, channel_multiplier=0).then_inc(s_io, 1)

                @block.tensor
                def _(pe):
                    pe.wait_ge(s_next, 64 + 32 * E)
                    pe.wait_ge(s_r, 16)
                    pe.transpose(ps_r[:, 0:E], rw[:, :], ident[0:E, 0:E]).then_inc(s_rp, 1)
                    for e in range(NE):
                        if e == E:
                            pe.wait_ge(s_w, 32)
                        if e >= 2:
                            pe.wait_ge(s_lo, e - 1)
                            pe.wait_ge(s_pc, e - 1)
                        for ps, k, s in ((ps_f, 0, s_f), (ps_p, 1, s_p)):
                            for c in range(NF):
                                mm = pe.transpose(ps[e % 2][:, c * P:(c + 1) * P], natural(e)[k][:, c, :], ident[:, :])
                            mm.then_inc(s, 1)

                @block.scalar
                def _(act):
                    for e in range(NE):
                        act.wait_ge(s_f, e + 1)
                        act.activation(fh[:, e, :], ps_f[e % 2][:, :], ACT.Copy).then_inc(s_hi, 1)
                        act.wait_ge(s_p, e + 1)
                        act.activation(pT[:, e, :, :], ps_p[e % 2][:, :].rearrange("p (c d) -> p c d", c=NF),
                                       ACT.Copy).then_inc(s_pc, 1)

                @block.vector
                def _(dve):
                    dve.wait_ge(s_rp, 1)
                    dve.tensor_copy(rT[:, :], ps_r[:, 0:E])
                    dve.wait_ge(s_io, 1)
                    dve.tensor_copy(iota[:, :, :], ii[:, :, :])
                    for e in range(NE):
                        dve.wait_ge(s_hi, e + 1)
                        dve.tensor_tensor(fl[:, e, :], ps_f[e % 2][:, :], fh[:, e, :], ALU.subtract)\
                            .then_inc(s_lo, 1)

        with ExitStack() as c2:
            sb2, pb2, sem2 = scope(nc, c2, "exp")
            ln, ln2 = (Norm((sb2, sem2), f"moe_ln{k}", G, gates) for k in (1, 2))
            xn = sb2("xn", [P, 2, G, D], F32)
            x32 = sb2("x32", [P, 2, N], F32)
            xh = sb2("xh", [P, 2, N], F32R)
            xl = sb2("xl", [P, 2, N], F32R)
            r = sb2("r", [P, 2, N], F32)
            h = sb2("h", [P, 3, N], F32)
            acc = sb2("acc", [P, 2, G, D], F32)
            z = sb2("z", [P, 2, G, D], F32)
            lmax = sb2("lmax", [P, G], F32)
            lg = sb2("lg", [P, G, E], F32)
            ex = sb2("ex", [P, G, E], F32)
            esum = sb2("esum", [P, G], F32)
            erec = sb2("erec", [P, G], F32)
            pr = sb2("pr", [P, G, E], F32)
            top = sb2("top", [P, G, 8], F32)
            idx = sb2("idx", [P, G, 8], U32)
            idf = sb2("idf", [P, G, 8], F32)
            den = sb2("den", [P, G], F32)
            denm = sb2("denm", [P, G], F32)
            drec = sb2("drec", [P, G], F32)
            m0 = sb2("m0", [P, G, E], F32)
            m1 = sb2("m1", [P, G, E], F32)
            mk = sb2("mk", [P, G, E], F32)
            pw = sb2("pw", [P, G, E], F32)
            cw = sb2("cw", [P, 2, G, E], F32)
            ps_t, ps_r = pb2("ps_t"), pb2("ps_r")
            ps_h = [pb2(f"ps_h{i}") for i in range(3)]
            ps_y = [pb2(f"ps_y{i}") for i in range(2)]
            names = "xn tp x32 xh xl rt lsub lexp a r h b acc z x".split()
            s = {n: sem2(f"s_{n}") for n in names}
            s_r = sem2("s_router")
            s_out = [sem2(f"s_out{i}") for i in range(2)]
            DEPTH = 4
            CH = NE * NF
            LINKS = 13 + 2 * G

            def per_expert(ap):
                return ap.unsqueeze(2).broadcast_to([P, G, E])

            with nc.Block() as block:
                @block.tensor
                def _(pe):
                    def hidden(i, k):
                        b, e, f = i.slot(2), k // NF, k % NF
                        if k == 0:
                            pe.wait_ge(s["xl"], i.at(1, 1))
                        after(pe, s["r"], i.at(CH, k - 2))
                        c = slice(f * P, (f + 1) * P)
                        split_matmul(pe, ps_h[k % 3][:, :], (fh[:, e, c], fl[:, e, c]), (xh[:, b, :], xl[:, b, :]))\
                            .then_inc(s["a"], 1)

                    def projected(i, k):
                        e, f = k // NF, k % NF
                        pe.wait_ge(s["h"], i.at(CH, k + 1))
                        if f == 0:
                            after(pe, s["acc"], i.at(NE, e - 1))
                        bank = ps_y[(i.slot(2) * NE + e) % 2]
                        for t in range(G):
                            mm = pe.matmul(bank[:, t * P:(t + 1) * P], h[:, k % 3, t * P:(t + 1) * P], pT[:, e, f, :],
                                           start=(f == 0 and t == 0), stop=(f == NF - 1), skip_group_check=True)
                        mm.then_inc(s["b"], 1)

                    def step(at):
                        i, i1, i3 = at(2), at(1), at(3)
                        for k in range(CH):
                            if i:
                                hidden(i, k)
                            if i1 and k == 1:
                                pe.wait_ge(s["xn"], i1.at(G, G))
                                after(pe, s["xh"], i1.at(1))
                                for j in range(G):
                                    mm = pe.transpose(ps_t[:, j * P:(j + 1) * P], xn[:, i1.slot(2), j, :], ident[:, :])
                                mm.then_inc(s["tp"], 1)
                            if i1 and k == 6:
                                pe.wait_ge(s["x32"], i1.at(1, 1))
                                after(pe, s["lsub"], i1.at(1))
                                for j in range(G):
                                    mm = pe.matmul(ps_r[:, j * E:(j + 1) * E], x32[:, i1.slot(2), j * P:(j + 1) * P],
                                                   rT[:, :], start=True, stop=True)
                                mm.then_inc(s["rt"], 1)
                            if i and k >= 2:
                                projected(i, k - 2)
                            if i3 and k < 2:
                                projected(i3, CH - 2 + k)
                    pipeline(pe, NT // G, DEPTH, 2, step)

                @block.scalar
                def _(act):
                    def step(at):
                        i, i1 = at(2), at(1)
                        for k in range(CH):
                            if i:
                                act.wait_ge(s["a"], i.at(CH, k + 1))
                                after(act, s["h"], i.at(CH, k - 1))
                                act.activation(r[:, k % 2, :], ps_h[k % 3][:, :], ACT.Relu).then_inc(s["r"], 1)
                            if i1 and k == 2:
                                b = i1.slot(2)
                                act.wait_ge(s["tp"], i1.at(1, 1))
                                after(act, s["rt"], i1.at(1, -1))
                                after(act, s["xl"], i1.at(1, -1))
                                act.activation(x32[:, b, :], ps_t[:, :], ACT.Copy).then_inc(s["x32"], 1)
                                after(act, s["a"], i1.at(CH, -CH))
                                act.activation(xh[:, b, :], ps_t[:, :], ACT.Copy).then_inc(s["xh"], 1)
                            if i1 and k == 10:
                                act.wait_ge(s["lsub"], i1.at(1, 1))
                                act.activation(ex[:, :, :], lg[:, :, :], ACT.Exp).then_inc(s["lexp"], 1)
                    pipeline(act, NT // G, DEPTH, 2, step)

                @block.gpsimd
                def _(pool):
                    def step(at):
                        if i := at(3):
                            ln2.rstd(pool, i, neghalf, eps)
                        if i := at(0):
                            ln.rstd(pool, i, neghalf, eps)
                    pipeline(pool, NT // G, DEPTH, 2, step)

                @block.vector
                def _(dve):
                    def route(i, k):
                        def link(n):
                            gates.wait(dve, gates.dve, s_r, i.at(LINKS, n))

                        if k == 8:
                            dve.wait_ge(s["rt"], i.at(1, 1))
                            dve.tensor_reduce(lmax[:, :], logits, AX.X, ALU.max).then_inc(s_r, 1)
                        elif k == 9:
                            link(1)
                            dve.tensor_tensor(lg[:, :, :], logits, per_expert(lmax[:, :]), ALU.subtract)\
                                .then_inc(s["lsub"], 1)
                        elif k == 12:
                            dve.wait_ge(s["lexp"], i.at(1, 1))
                            dve.tensor_reduce(esum[:, :], ex[:, :, :], AX.X, ALU.add).then_inc(s_r, 1)
                        elif k == 13:
                            link(2)
                            dve.reciprocal(erec[:, :], esum[:, :]).then_inc(s_r, 1)
                        elif k == 14:
                            link(3)
                            dve.tensor_tensor(pr[:, :, :], ex[:, :, :], per_expert(erec[:, :]), ALU.mult)\
                                .then_inc(s_r, 1)
                        elif k == 15:
                            link(4)
                            for j in range(G):
                                dve.max(top[:, j, :], pr[:, j, :]).then_inc(s_r, 1)
                        elif k == 17:
                            link(4 + G)
                            for j in range(G):
                                dve.max_index(idx[:, j, :], top[:, j, :], pr[:, j, :]).then_inc(s_r, 1)
                        elif k == 19:
                            link(4 + 2 * G)
                            dve.tensor_copy(idf[:, :, :], idx[:, :, :]).then_inc(s_r, 1)
                            dve.tensor_tensor(den[:, :], top[:, :, 0], top[:, :, 1], ALU.add).then_inc(s_r, 1)
                        elif k == 20:
                            link(6 + 2 * G)
                            dve.tensor_scalar(denm[:, :], den[:, :], 1e-9, None, ALU.max).then_inc(s_r, 1)
                            dve.tensor_tensor(m0[:, :, :], iota[:, :, :], per_expert(idf[:, :, 0]), ALU.is_equal)\
                                .then_inc(s_r, 1)
                        elif k == 21:
                            link(8 + 2 * G)
                            dve.reciprocal(drec[:, :], denm[:, :]).then_inc(s_r, 1)
                            dve.tensor_tensor(m1[:, :, :], iota[:, :, :], per_expert(idf[:, :, 1]), ALU.is_equal)\
                                .then_inc(s_r, 1)
                        elif k == 22:
                            link(10 + 2 * G)
                            dve.tensor_tensor(mk[:, :, :], m0[:, :, :], m1[:, :, :], ALU.add).then_inc(s_r, 1)
                            dve.tensor_tensor(pw[:, :, :], pr[:, :, :], per_expert(drec[:, :]), ALU.mult)\
                                .then_inc(s_r, 1)
                        elif k == 23:
                            link(12 + 2 * G)
                            dve.tensor_tensor(cw[:, i.slot(2), :, :], pw[:, :, :], mk[:, :, :], ALU.mult)\
                                .then_inc(s_r, 1)

                    logits = ps_r[:, 0:G * E].rearrange("p (g e) -> p g e", g=G)

                    def weighed(i, e):
                        b = i.slot(2)
                        bank = ps_y[(i.slot(2) * NE + e) % 2]
                        dve.wait_ge(s["b"], i.at(CH, NF * (e + 1)))
                        if e:
                            dve.wait_ge(s["acc"], i.at(NE, e))
                        for t in range(G):
                            y = bank[:, t * P:(t + 1) * P]
                            a = acc[:, b, t, :]
                            if e == 0:
                                o = dve.tensor_scalar(a, y, cw[:, b, t, 0:1], None, ALU.mult)
                            elif e < E:
                                o = dve.scalar_tensor_tensor(a, y, cw[:, b, t, e:e + 1], a, ALU.mult, ALU.add)
                            else:
                                o = dve.tensor_tensor(a, y, a, ALU.add)
                        o.then_inc(s["acc"], 1)

                    def step(at):
                        i0, i1, i, i3 = (at(n) for n in range(4))
                        for k in range(CH):
                            if i:
                                dve.wait_ge(s["r"], i.at(CH, k + 1))
                                after(dve, s["b"], i.at(CH, k - 2))
                                dve.tensor_tensor(h[:, k % 3, :], r[:, k % 2, :], r[:, k % 2, :], ALU.mult)\
                                    .then_inc(s["h"], 1)
                            if i3 and k == 2:
                                weighed(i3, NE - 1)
                            if i and k >= NF + 2 and (k - 2) % NF == 0:
                                weighed(i, (k - 2) // NF - 1)
                            if i3 and k == 4:
                                gates.wait(dve, gates.dve, s["acc"], i3.at(NE, NE))
                                ln2.stats(dve, i3, lambda j: acc[:, i3.slot(2), j, :])
                            if i1 and k == 5:
                                b = i1.slot(2)
                                dve.wait_ge(s["xh"], i1.at(1, 1))
                                after(dve, s["a"], i1.at(CH, -CH))
                                dve.tensor_tensor(xl[:, b, :], x32[:, b, :], xh[:, b, :], ALU.subtract)\
                                    .then_inc(s["xl"], 1)
                            if i3 and k == 7:
                                b = i3.slot(2)
                                ln2.ready(dve, i3)
                                ln2.apply(dve, i3, lambda j: z[:, b, j, :], lambda j: acc[:, b, j, :], s["z"])
                            if i3 and k == 11:
                                dve.wait_ge(s["z"], i3.at(G, G))
                                dve.tensor_tensor(xs[:, tiles(i3, G), :], xs[:, tiles(i3, G), :],
                                                  z[:, i3.slot(2), :, :], ALU.add).then_inc(s["x"], 1)
                            if i1:
                                route(i1, k)
                            if i0 and k == 24:
                                ln.stats(dve, i0, lambda j: xs[:, i0.at(G, j), :])
                            if i0 and k == 28:
                                ln.ready(dve, i0)
                                after(dve, s["tp"], i0.at(1, -1))
                                ln.apply(dve, i0, lambda j: xn[:, i0.slot(2), j, :],
                                         lambda j: xs[:, i0.at(G, j), :], s["xn"])
                    pipeline(dve, NT // G, DEPTH, 2, step)

                @block.sync
                def _(sp):
                    def step(at):
                        if i := at(3):
                            sp.wait_ge(s["x"], i.at(1, 1))
                            sp.dma_start(out_dram[:, tiles(i, G), :], xs[:, tiles(i, G), :])\
                                .then_inc(s_out[i.slot(2)], 16)
                    pipeline(sp, NT // G, DEPTH, 2, step)
                    for b in range(2):
                        sp.wait_ge(s_out[b], NT // G // 2 * 16)


INPUTS = ("L0_attn_x", "L0_attn_W_in", "L0_attn_A_in", "L0_attn_B_in", "L0_attn_W_out", "L0_ffn_W_r",
          "L0_ffn_W_k", "L0_ffn_W_v", "L0_ffn_mu_r", "L0_ffn_mu_k", "L1_attn_Wq", "L1_attn_Wk",
          "L1_attn_Wv", "L1_attn_Wo", "L1_ffn_router_w", "L1_ffn_w_fc", "L1_ffn_w_proj",
          "L1_ffn_shared_fc", "L1_ffn_shared_proj")


def kernel(**inputs):
    import numpy as np
    from concourse import bacc
    from concourse.bass_utils import run_bass_kernel_spmd

    nc = bacc.Bacc("TRN2", target_bir_lowering=False, num_devices=1)
    arrays, args = {}, []
    for name in INPUTS:
        a = np.ascontiguousarray(inputs[name])
        arrays[f"in_{name}"] = a
        args.append(nc.dram_tensor(f"in_{name}", a.shape, mybir.dt.from_np(a.dtype), kind="ExternalInput").ap())
    out = nc.dram_tensor("out_x", inputs["L0_attn_x"].shape, F32, kind="ExternalOutput").ap()
    program(nc, *args, out)
    r = run_bass_kernel_spmd(nc, [arrays], core_ids=[0])
    return r.results[0]["out_x"]
```
